# Optimizing a Trainium2 kernel written in Bass

```python
import numpy as np
import jax
import jax.numpy as jnp

def _softmax(x, axis=-1):
    return jax.nn.softmax(x, axis=axis)

def _gelu(x):
    return jax.nn.gelu(x, approximate=True)

def _silu(x):
    return jax.nn.silu(x)

def _sigmoid(x):
    return jax.nn.sigmoid(x)

def _layernorm(x, axis=-1, eps=1e-05):
    m = jnp.mean(x, axis=axis, keepdims=True)
    v = jnp.var(x, axis=axis, keepdims=True)
    return (x - m) / jnp.sqrt(v + eps)

def _scatter_add(tgt, idx, src, axis=0):
    return tgt.at[idx].add(src)

def _segment_sum(src, seg, n):
    return jax.ops.segment_sum(src, seg, n)
kernel_name = 'mk_vit_tower_d4_tok_img1024_r4_118aca'

def setup_inputs(seed: int=0):
    np.random.seed(seed)
    _w = jnp.asarray

    def _rec_inputs():
        import jax
        import jax.numpy as jnp
        _rk = jax.random.key(seed)
        x = 7.22013e-05 + 1.00017 * jax.random.normal(jax.random.fold_in(_rk, 1), (8, 64, 256, 4), jnp.float32)
        return x
    x = _rec_inputs()

    def _L0_tok_setup():
        import jax, jax.numpy as jnp
        import numpy as np
        B, F, L, H, D = (8, 64, 256, 4, 64)
        MODEL = H * F
        WIN = 128

        def _local_mask():
            m = np.ones((L, L), dtype=bool)
            m = np.tril(m, WIN - 1)
            m = np.triu(m, -(WIN - 1))
            return jnp.asarray(m)

        def _flatten(y):
            n = y.shape[0]
            return y.transpose(0, 2, 3, 1).reshape(n, L, -1)
        key = jax.random.key(seed)
        ks = jax.random.split(key, 12)
        s = lambda n: 1.0 / np.sqrt(n)
        xav = np.sqrt(6.0 / (L + L))
        return {'x': jax.random.normal(ks[0], (B, F, L, H), jnp.float32), 'Wq_w': jax.random.normal(ks[1], (D, F), jnp.float32) * s(F), 'Wq_b': jnp.zeros((D,), jnp.float32), 'Wk_w': jax.random.normal(ks[2], (D, F), jnp.float32) * s(F), 'Wk_b': jnp.zeros((D,), jnp.float32), 'Wv_w': jax.random.normal(ks[3], (D, F), jnp.float32) * s(F), 'Wv_b': jnp.zeros((D,), jnp.float32), 'w_bias': jax.random.uniform(ks[4], (L, L), jnp.float32, -xav, xav), 'out_w': jax.random.normal(ks[5], (H * D, MODEL), jnp.float32) * s(H * D), 'out_b': jnp.zeros((MODEL,), jnp.float32), 'ln_g': jnp.ones((MODEL,), jnp.float32), 'ln_b': jnp.zeros((MODEL,), jnp.float32), 'local_mask': _local_mask()}
    _L0_tok_all = _L0_tok_setup()
    _L0_tok_in = {k: v for k, v in _L0_tok_all.items() if k in ('Wq_w', 'Wq_b', 'Wk_w', 'Wk_b', 'Wv_w', 'Wv_b', 'w_bias', 'out_w', 'out_b', 'ln_g', 'ln_b', 'local_mask')}
    del _L0_tok_all

    def _L0_attn_setup():
        import jax, jax.numpy as jnp
        import numpy as np
        HEADS = 16

        def fenwick_mask(T):
            m = np.zeros((T, T), dtype=bool)
            for i in range(T):
                j = i + 1
                while j <= T:
                    m[i, j - 1] = True
                    j += j & -j
                step = 1
                while i - step >= 0:
                    m[i, i - step] = True
                    step *= 2
            m &= np.tril(np.ones((T, T), dtype=bool))
            return jnp.asarray(m)
        key = jax.random.key(seed)
        ks = jax.random.split(key, 4)
        B, T, C = (2, 512, 256)
        x = jax.random.normal(ks[0], (B, T, C), dtype=jnp.float32)
        W_qkv = jax.random.normal(ks[1], (C, 3 * C), dtype=jnp.float32) * C ** (-0.5)
        b_qkv = jnp.zeros((3 * C,), dtype=jnp.float32)
        W_proj = jax.random.normal(ks[2], (C, C), dtype=jnp.float32) * C ** (-0.5)
        b_proj = jnp.zeros((C,), dtype=jnp.float32)
        return {'x': x, 'W_qkv': W_qkv, 'b_qkv': b_qkv, 'W_proj': W_proj, 'b_proj': b_proj}
    _L0_attn_all = _L0_attn_setup()
    _L0_attn_in = {k: v for k, v in _L0_attn_all.items() if k in ('W_qkv', 'b_qkv', 'W_proj', 'b_proj')}
    del _L0_attn_all

    def _L0_ffn_setup():
        import jax, jax.numpy as jnp
        import numpy as np
        EPS = 1e-06
        LN_EPS = 1e-05

        def _absmean_core(W):
            gamma = jnp.mean(jnp.abs(W)) + EPS
            Ws = W / gamma
            Wq = jnp.sign(Ws) * jnp.minimum(jnp.round(jnp.abs(Ws)), 1.0)
            return (Wq, gamma)

        @jax.custom_vjp
        def absmean(W):
            return _absmean_core(W)[0]

        def _absmean_fwd(W):
            Wq, gamma = _absmean_core(W)
            return (Wq, gamma)

        def _absmean_bwd(gamma, g):
            return (g / gamma,)
        absmean.defvjp(_absmean_fwd, _absmean_bwd)

        def layernorm(x, w, b, eps=LN_EPS):
            mu = jnp.mean(x, axis=-1, keepdims=True)
            var = jnp.mean((x - mu) ** 2, axis=-1, keepdims=True)
            return (x - mu) * jax.lax.rsqrt(var + eps) * w + b
        key = jax.random.key(seed)
        k1, k2, k3 = jax.random.split(key, 3)
        d, h = (256, 1024)
        B, T = (8, 512)
        return {'x': jax.random.normal(k1, (B, T, d), jnp.float32), 'W_fc': jax.random.normal(k2, (h, d), jnp.float32), 'ln_w': jnp.ones((h,), jnp.float32), 'ln_b': jnp.zeros((h,), jnp.float32), 'W_proj': jax.random.normal(k3, (d, h), jnp.float32)}
    _L0_ffn_all = _L0_ffn_setup()
    _L0_ffn_in = {k: v for k, v in _L0_ffn_all.items() if k in ('W_fc', 'ln_w', 'ln_b', 'W_proj')}
    del _L0_ffn_all

    def _L1_attn_setup():
        import jax, jax.numpy as jnp
        import numpy as np
        import math
        D_MODEL = 256
        NUM_HEADS = 16
        D_K = D_MODEL // NUM_HEADS
        B, S = (2, 512)

        def _linear_weight(key, out_f, in_f):
            return jax.random.normal(key, (out_f, in_f), jnp.float32) * math.sqrt(2.0 / in_f)
        key = jax.random.key(seed)
        ks = jax.random.split(key, 5)
        x = jax.random.normal(ks[0], (B, S, D_MODEL), jnp.float32)
        return {'x': x, 'Wq': _linear_weight(ks[1], D_MODEL, D_MODEL), 'bq': jnp.zeros((D_MODEL,), jnp.float32), 'Wk': _linear_weight(ks[2], D_MODEL, D_MODEL), 'bk': jnp.zeros((D_MODEL,), jnp.float32), 'Wv': _linear_weight(ks[3], D_MODEL, D_MODEL), 'bv': jnp.zeros((D_MODEL,), jnp.float32), 'Wo': _linear_weight(ks[4], D_MODEL, D_MODEL), 'bo': jnp.zeros((D_MODEL,), jnp.float32)}
    _L1_attn_all = _L1_attn_setup()
    _L1_attn_in = {k: v for k, v in _L1_attn_all.items() if k in ('Wq', 'bq', 'Wk', 'bk', 'Wv', 'bv', 'Wo', 'bo')}
    del _L1_attn_all

    def _L1_ffn_setup():
        import jax, jax.numpy as jnp
        import numpy as np
        DIM = 256

        def _reference_tuple_inner(x, W_r, W_k, W_v, mu_r, mu_k):
            B, T, C = x.shape
            x_prev = jnp.concatenate([jnp.zeros((B, 1, C), x.dtype), x[:, :-1, :]], axis=1)
            xr = mu_r * x + (1.0 - mu_r) * x_prev
            xk = mu_k * x + (1.0 - mu_k) * x_prev
            r = jax.nn.sigmoid(jnp.einsum('btc,dc->btd', xr, W_r))
            k = jnp.einsum('btc,dc->btd', xk, W_k)
            k_act = jnp.square(jax.nn.relu(k))
            out = r * jnp.einsum('btc,dc->btd', k_act, W_v)
            new_state = x[:, -1, :]
            return (out, new_state)
        key = jax.random.key(seed)
        ks = jax.random.split(key, 6)
        B, T, C = (8, 512, DIM)
        x = jax.random.normal(ks[0], (B, T, C), dtype=jnp.float32)
        s = 1.0 / np.sqrt(C)
        W_r = jax.random.uniform(ks[1], (C, C), jnp.float32, -s, s)
        W_k = jax.random.uniform(ks[2], (C, C), jnp.float32, -s, s)
        W_v = jax.random.uniform(ks[3], (C, C), jnp.float32, -s, s)
        mu_r = jax.random.uniform(ks[4], (C,), jnp.float32)
        mu_k = jax.random.uniform(ks[5], (C,), jnp.float32)
        return {'x': x, 'W_r': W_r, 'W_k': W_k, 'W_v': W_v, 'mu_r': mu_r, 'mu_k': mu_k}
    _L1_ffn_all = _L1_ffn_setup()
    _L1_ffn_in = {k: v for k, v in _L1_ffn_all.items() if k in ('W_r', 'W_k', 'W_v', 'mu_r', 'mu_k')}
    del _L1_ffn_all

    def _L2_attn_setup():
        import jax, jax.numpy as jnp
        import numpy as np
        B, S, E, H, P = (2, 512, 256, 16, 512)
        HD = E // H
        key = jax.random.key(seed)
        ks = jax.random.split(key, 10)
        std = E ** (-0.5)
        x = jax.random.normal(ks[0], (B, S, E), jnp.float32)
        Wq = jax.random.normal(ks[1], (E, E), jnp.float32) * std
        Wk = jax.random.normal(ks[2], (E, E), jnp.float32) * std
        Wv = jax.random.normal(ks[3], (E, E), jnp.float32) * std
        Wo = jax.random.normal(ks[4], (E, E), jnp.float32) * std
        rel_key = jax.random.normal(ks[5], (P, HD), jnp.float32) * 0.02
        z = jnp.zeros((E,), jnp.float32)
        return {'x': x, 'Wq': Wq, 'bq': z, 'Wk': Wk, 'bk': z, 'Wv': Wv, 'bv': z, 'Wo': Wo, 'bo': z, 'rel_key': rel_key}
    _L2_attn_all = _L2_attn_setup()
    _L2_attn_in = {k: v for k, v in _L2_attn_all.items() if k in ('Wq', 'bq', 'Wk', 'bk', 'Wv', 'bv', 'Wo', 'bo', 'rel_key')}
    del _L2_attn_all

    def _L2_ffn_setup():
        import jax, jax.numpy as jnp
        import numpy as np
        B, S, D = (4, 1024, 256)
        E, F_EXP = (16, 512)
        F_C = 2.0
        F_SH = 512
        key = jax.random.key(seed)
        ks = jax.random.split(key, 8)
        s = 0.02
        return {'hidden_states': jax.random.normal(ks[0], (B, S, D), jnp.float32), 'gate_w': jax.random.normal(ks[1], (E, D), jnp.float32) * s, 'Wg': jax.random.normal(ks[2], (E, F_EXP, D), jnp.float32) * s, 'Wu': jax.random.normal(ks[3], (E, F_EXP, D), jnp.float32) * s, 'Wd': jax.random.normal(ks[4], (E, D, F_EXP), jnp.float32) * s, 'Ws_g': jax.random.normal(ks[5], (F_SH, D), jnp.float32) * s, 'Ws_u': jax.random.normal(ks[6], (F_SH, D), jnp.float32) * s, 'Ws_d': jax.random.normal(ks[7], (D, F_SH), jnp.float32) * s}
    _L2_ffn_all = _L2_ffn_setup()
    _L2_ffn_in = {k: v for k, v in _L2_ffn_all.items() if k in ('gate_w', 'Wg', 'Wu', 'Wd', 'Ws_g', 'Ws_u', 'Ws_d')}
    del _L2_ffn_all

    def _L3_attn_setup():
        import jax, jax.numpy as jnp
        import numpy as np
        import math
        B, S, D = (4, 512, 256)
        H = 16
        HD = D // H
        DL = 64
        LAMBDA_DECAY = 0.01
        key = jax.random.key(seed)
        ks = jax.random.split(key, 8)
        sc = lambda fan_in: 1.0 / math.sqrt(fan_in)
        return {'x': jax.random.normal(ks[0], (B, S, D), dtype=jnp.float32), 'W_q': jax.random.normal(ks[1], (D, D), dtype=jnp.float32) * sc(D), 'W_k': jax.random.normal(ks[2], (D, D), dtype=jnp.float32) * sc(D), 'W_v': jax.random.normal(ks[3], (D, D), dtype=jnp.float32) * sc(D), 'W_o': jax.random.normal(ks[4], (D, D), dtype=jnp.float32) * sc(D), 'W_down_kv': jax.random.normal(ks[5], (D, DL), dtype=jnp.float32) * sc(D), 'W_up_k': jax.random.normal(ks[6], (DL, D), dtype=jnp.float32) * sc(DL), 'W_up_v': jax.random.normal(ks[7], (DL, D), dtype=jnp.float32) * sc(DL)}
    _L3_attn_all = _L3_attn_setup()
    _L3_attn_in = {k: v for k, v in _L3_attn_all.items() if k in ('W_q', 'W_k', 'W_v', 'W_o', 'W_down_kv', 'W_up_k', 'W_up_v')}
    del _L3_attn_all

    def _L3_ffn_setup():
        import jax, jax.numpy as jnp
        import numpy as np
        import math
        HID, HD, E, MIN_E = (256, 128, 16, 2)
        B, T = (4, 512)
        IS_CAUSAL = True

        def _l2norm(x, axis):
            return x / jnp.sqrt(jnp.sum(x * x, axis=axis, keepdims=True) + 1e-12)

        def _gating(hidden_states, sim_matrix, gates):
            b, t, c = hidden_states.shape
            flat = hidden_states.reshape(b * t, c)
            logits = _l2norm(flat, -1) @ _l2norm(sim_matrix, 0) - jax.nn.sigmoid(gates)
            gated = jax.nn.relu(logits)
            mask = (gated > 0).astype(gated.dtype)
            inactive = jnp.sum(mask, axis=1) == 0
            _, top_idx = jax.lax.top_k(logits, MIN_E)
            fb = jnp.sum(jax.nn.one_hot(top_idx, E, dtype=mask.dtype), axis=1)
            mask = mask + inactive[:, None].astype(mask.dtype) * fb
            masked = jnp.where(mask > 0, gated, -jnp.inf)
            probs = jax.nn.softmax(masked, axis=-1)
            return probs
        key = jax.random.key(seed)
        ks = jax.random.split(key, 6)
        a_qkv = math.sqrt(6.0 / (HID + HD))
        a_o = math.sqrt(6.0 / (HD + HID))
        return {'hidden_states': jax.random.normal(ks[0], (B, T, HID), jnp.float32), 'sim_matrix': jax.random.normal(ks[1], (HID, E), jnp.float32), 'gates': jnp.zeros((E,), jnp.float32), 'q_proj': jax.random.uniform(ks[2], (E, HID, HD), jnp.float32, -a_qkv, a_qkv), 'k_proj': jax.random.uniform(ks[3], (E, HID, HD), jnp.float32, -a_qkv, a_qkv), 'v_proj': jax.random.uniform(ks[4], (E, HID, HD), jnp.float32, -a_qkv, a_qkv), 'o_proj': jax.random.uniform(ks[5], (E, HD, HID), jnp.float32, -a_o, a_o)}
    _L3_ffn_all = _L3_ffn_setup()
    _L3_ffn_in = {k: v for k, v in _L3_ffn_all.items() if k in ('sim_matrix', 'gates', 'q_proj', 'k_proj', 'v_proj', 'o_proj')}
    del _L3_ffn_all
    return {'x': x, 'L0_tok_Wq_w': _L0_tok_in['Wq_w'], 'L0_tok_Wq_b': _L0_tok_in['Wq_b'], 'L0_tok_Wk_w': _L0_tok_in['Wk_w'], 'L0_tok_Wk_b': _L0_tok_in['Wk_b'], 'L0_tok_Wv_w': _L0_tok_in['Wv_w'], 'L0_tok_Wv_b': _L0_tok_in['Wv_b'], 'L0_tok_w_bias': _L0_tok_in['w_bias'], 'L0_tok_out_w': _L0_tok_in['out_w'], 'L0_tok_out_b': _L0_tok_in['out_b'], 'L0_tok_ln_g': _L0_tok_in['ln_g'], 'L0_tok_ln_b': _L0_tok_in['ln_b'], 'L0_tok_local_mask': _L0_tok_in['local_mask'], 'L0_attn_W_qkv': _L0_attn_in['W_qkv'], 'L0_attn_b_qkv': _L0_attn_in['b_qkv'], 'L0_attn_W_proj': _L0_attn_in['W_proj'], 'L0_attn_b_proj': _L0_attn_in['b_proj'], 'L0_ffn_W_fc': _L0_ffn_in['W_fc'], 'L0_ffn_ln_w': _L0_ffn_in['ln_w'], 'L0_ffn_ln_b': _L0_ffn_in['ln_b'], 'L0_ffn_W_proj': _L0_ffn_in['W_proj'], 'L1_attn_Wq': _L1_attn_in['Wq'], 'L1_attn_bq': _L1_attn_in['bq'], 'L1_attn_Wk': _L1_attn_in['Wk'], 'L1_attn_bk': _L1_attn_in['bk'], 'L1_attn_Wv': _L1_attn_in['Wv'], 'L1_attn_bv': _L1_attn_in['bv'], 'L1_attn_Wo': _L1_attn_in['Wo'], 'L1_attn_bo': _L1_attn_in['bo'], 'L1_ffn_W_r': _L1_ffn_in['W_r'], 'L1_ffn_W_k': _L1_ffn_in['W_k'], 'L1_ffn_W_v': _L1_ffn_in['W_v'], 'L1_ffn_mu_r': _L1_ffn_in['mu_r'], 'L1_ffn_mu_k': _L1_ffn_in['mu_k'], 'L2_attn_Wq': _L2_attn_in['Wq'], 'L2_attn_bq': _L2_attn_in['bq'], 'L2_attn_Wk': _L2_attn_in['Wk'], 'L2_attn_bk': _L2_attn_in['bk'], 'L2_attn_Wv': _L2_attn_in['Wv'], 'L2_attn_bv': _L2_attn_in['bv'], 'L2_attn_Wo': _L2_attn_in['Wo'], 'L2_attn_bo': _L2_attn_in['bo'], 'L2_attn_rel_key': _L2_attn_in['rel_key'], 'L2_ffn_gate_w': _L2_ffn_in['gate_w'], 'L2_ffn_Wg': _L2_ffn_in['Wg'], 'L2_ffn_Wu': _L2_ffn_in['Wu'], 'L2_ffn_Wd': _L2_ffn_in['Wd'], 'L2_ffn_Ws_g': _L2_ffn_in['Ws_g'], 'L2_ffn_Ws_u': _L2_ffn_in['Ws_u'], 'L2_ffn_Ws_d': _L2_ffn_in['Ws_d'], 'L3_attn_W_q': _L3_attn_in['W_q'], 'L3_attn_W_k': _L3_attn_in['W_k'], 'L3_attn_W_v': _L3_attn_in['W_v'], 'L3_attn_W_o': _L3_attn_in['W_o'], 'L3_attn_W_down_kv': _L3_attn_in['W_down_kv'], 'L3_attn_W_up_k': _L3_attn_in['W_up_k'], 'L3_attn_W_up_v': _L3_attn_in['W_up_v'], 'L3_ffn_sim_matrix': _L3_ffn_in['sim_matrix'], 'L3_ffn_gates': _L3_ffn_in['gates'], 'L3_ffn_q_proj': _L3_ffn_in['q_proj'], 'L3_ffn_k_proj': _L3_ffn_in['k_proj'], 'L3_ffn_v_proj': _L3_ffn_in['v_proj'], 'L3_ffn_o_proj': _L3_ffn_in['o_proj']}

def reference(x, L0_tok_Wq_w, L0_tok_Wq_b, L0_tok_Wk_w, L0_tok_Wk_b, L0_tok_Wv_w, L0_tok_Wv_b, L0_tok_w_bias, L0_tok_out_w, L0_tok_out_b, L0_tok_ln_g, L0_tok_ln_b, L0_tok_local_mask, L0_attn_W_qkv, L0_attn_b_qkv, L0_attn_W_proj, L0_attn_b_proj, L0_ffn_W_fc, L0_ffn_ln_w, L0_ffn_ln_b, L0_ffn_W_proj, L1_attn_Wq, L1_attn_bq, L1_attn_Wk, L1_attn_bk, L1_attn_Wv, L1_attn_bv, L1_attn_Wo, L1_attn_bo, L1_ffn_W_r, L1_ffn_W_k, L1_ffn_W_v, L1_ffn_mu_r, L1_ffn_mu_k, L2_attn_Wq, L2_attn_bq, L2_attn_Wk, L2_attn_bk, L2_attn_Wv, L2_attn_bv, L2_attn_Wo, L2_attn_bo, L2_attn_rel_key, L2_ffn_gate_w, L2_ffn_Wg, L2_ffn_Wu, L2_ffn_Wd, L2_ffn_Ws_g, L2_ffn_Ws_u, L2_ffn_Ws_d, L3_attn_W_q, L3_attn_W_k, L3_attn_W_v, L3_attn_W_o, L3_attn_W_down_kv, L3_attn_W_up_k, L3_attn_W_up_v, L3_ffn_sim_matrix, L3_ffn_gates, L3_ffn_q_proj, L3_ffn_k_proj, L3_ffn_v_proj, L3_ffn_o_proj):
    import jax
    import jax.numpy as jnp

    def _L0_tok_ref(x, Wq_w, Wq_b, Wk_w, Wk_b, Wv_w, Wv_b, w_bias, out_w, out_b, ln_g, ln_b, local_mask):
        import jax, jax.numpy as jnp
        import numpy as np
        B, F, L, H, D = (8, 64, 256, 4, 64)
        MODEL = H * F
        WIN = 128

        def _local_mask():
            m = np.ones((L, L), dtype=bool)
            m = np.tril(m, WIN - 1)
            m = np.triu(m, -(WIN - 1))
            return jnp.asarray(m)

        def _flatten(y):
            n = y.shape[0]
            return y.transpose(0, 2, 3, 1).reshape(n, L, -1)

        def proj(w, b):
            y = jnp.einsum('nclh,dc->ndlh', x, w) + b[None, :, None, None]
            return _flatten(y)
        q = proj(Wq_w, Wq_b)
        k = proj(Wk_w, Wk_b)
        v = proj(Wv_w, Wv_b)
        wb = w_bias * local_mask.astype(w_bias.dtype)
        ew = jnp.exp(wb)
        ek = jnp.exp(k)
        num = jnp.einsum('ts,nsd->ntd', ew, ek * v)
        den = jnp.einsum('ts,nsd->ntd', ew, ek)
        y = jax.nn.sigmoid(q) * num / den
        h = y @ out_w + out_b + _flatten(x)
        mu = jnp.mean(h, axis=-1, keepdims=True)
        var = jnp.mean(jnp.square(h - mu), axis=-1, keepdims=True)
        return (h - mu) * jax.lax.rsqrt(var + 1e-05) * ln_g + ln_b

    def _L0_attn_ref(x, W_qkv, b_qkv, W_proj, b_proj):
        import jax, jax.numpy as jnp
        import numpy as np
        HEADS = 16

        def fenwick_mask(T):
            m = np.zeros((T, T), dtype=bool)
            for i in range(T):
                j = i + 1
                while j <= T:
                    m[i, j - 1] = True
                    j += j & -j
                step = 1
                while i - step >= 0:
                    m[i, i - step] = True
                    step *= 2
            m &= np.tril(np.ones((T, T), dtype=bool))
            return jnp.asarray(m)
        B, T, C = x.shape
        H = HEADS
        Dh = C // H
        scale = Dh ** (-0.5)
        qkv = (x @ W_qkv + b_qkv).reshape(B, T, 3, H, Dh)
        qkv = jnp.transpose(qkv, (2, 0, 3, 1, 4))
        q, k, v = (qkv[0], qkv[1], qkv[2])
        attn = jnp.einsum('bhtd,bhsd->bhts', q, k) * scale
        mask = fenwick_mask(T)
        attn = jnp.where(mask[None, None], attn, -jnp.inf)
        attn = jax.nn.softmax(attn, axis=-1)
        out = jnp.einsum('bhts,bhsd->bhtd', attn, v)
        out = jnp.transpose(out, (0, 2, 1, 3)).reshape(B, T, C)
        return out @ W_proj + b_proj

    def _L0_ffn_ref(x, W_fc, ln_w, ln_b, W_proj):
        import jax, jax.numpy as jnp
        import numpy as np
        EPS = 1e-06
        LN_EPS = 1e-05

        def _absmean_core(W):
            gamma = jnp.mean(jnp.abs(W)) + EPS
            Ws = W / gamma
            Wq = jnp.sign(Ws) * jnp.minimum(jnp.round(jnp.abs(Ws)), 1.0)
            return (Wq, gamma)

        @jax.custom_vjp
        def absmean(W):
            return _absmean_core(W)[0]

        def _absmean_fwd(W):
            Wq, gamma = _absmean_core(W)
            return (Wq, gamma)

        def _absmean_bwd(gamma, g):
            return (g / gamma,)
        absmean.defvjp(_absmean_fwd, _absmean_bwd)

        def layernorm(x, w, b, eps=LN_EPS):
            mu = jnp.mean(x, axis=-1, keepdims=True)
            var = jnp.mean((x - mu) ** 2, axis=-1, keepdims=True)
            return (x - mu) * jax.lax.rsqrt(var + eps) * w + b
        h = jnp.einsum('btd,hd->bth', x, absmean(W_fc))
        h = jax.nn.gelu(h, approximate=False)
        h = layernorm(h, ln_w, ln_b)
        return jnp.einsum('bth,dh->btd', h, absmean(W_proj))

    def _L1_attn_ref(x, Wq, bq, Wk, bk, Wv, bv, Wo, bo):
        import jax, jax.numpy as jnp
        import numpy as np
        import math
        D_MODEL = 256
        NUM_HEADS = 16
        D_K = D_MODEL // NUM_HEADS
        B, S = (2, 512)

        def _linear_weight(key, out_f, in_f):
            return jax.random.normal(key, (out_f, in_f), jnp.float32) * math.sqrt(2.0 / in_f)
        b, s, _ = x.shape
        q = jnp.einsum('bsd,ed->bse', x, Wq) + bq
        k = jnp.einsum('bsd,ed->bse', x, Wk) + bk
        v = jnp.einsum('bsd,ed->bse', x, Wv) + bv
        q = q.reshape(b, s, NUM_HEADS, D_K).transpose(0, 2, 1, 3)
        k = k.reshape(b, s, NUM_HEADS, D_K).transpose(0, 2, 1, 3)
        v = v.reshape(b, s, NUM_HEADS, D_K).transpose(0, 2, 1, 3)
        scores = jnp.einsum('bhqd,bhkd->bhqk', q, k) / math.sqrt(D_K)
        attn = jax.nn.softmax(scores, axis=-1)
        out = jnp.einsum('bhqk,bhkd->bhqd', attn, v)
        out = out.transpose(0, 2, 1, 3).reshape(b, s, D_MODEL)
        return jnp.einsum('bsd,ed->bse', out, Wo) + bo

    def _L1_ffn_ref(x, W_r, W_k, W_v, mu_r, mu_k):
        import jax, jax.numpy as jnp
        import numpy as np
        DIM = 256

        def _reference_tuple_inner(x, W_r, W_k, W_v, mu_r, mu_k):
            B, T, C = x.shape
            x_prev = jnp.concatenate([jnp.zeros((B, 1, C), x.dtype), x[:, :-1, :]], axis=1)
            xr = mu_r * x + (1.0 - mu_r) * x_prev
            xk = mu_k * x + (1.0 - mu_k) * x_prev
            r = jax.nn.sigmoid(jnp.einsum('btc,dc->btd', xr, W_r))
            k = jnp.einsum('btc,dc->btd', xk, W_k)
            k_act = jnp.square(jax.nn.relu(k))
            out = r * jnp.einsum('btc,dc->btd', k_act, W_v)
            new_state = x[:, -1, :]
            return (out, new_state)
        return _reference_tuple_inner(x, W_r, W_k, W_v, mu_r, mu_k)[0]

    def _L2_attn_ref(x, Wq, bq, Wk, bk, Wv, bv, Wo, bo, rel_key):
        import jax, jax.numpy as jnp
        import numpy as np
        B, S, E, H, P = (2, 512, 256, 16, 512)
        HD = E // H
        b, s, e = x.shape
        p, hd = rel_key.shape
        h = e // hd
        scale = hd ** (-0.5)

        def split_heads(t):
            return t.reshape(b, s, h, hd).transpose(0, 2, 1, 3)
        q = split_heads(x @ Wq + bq)
        k = split_heads(x @ Wk + bk)
        v = split_heads(x @ Wv + bv)
        scores = jnp.einsum('bhid,bhjd->bhij', q, k)
        rel = jnp.einsum('bhid,pd->bhip', q, rel_key)
        i = jnp.arange(s)[:, None]
        j = jnp.arange(s)[None, :]
        rel_idx = jnp.clip(j - i + p - 1, 0, p - 1)
        bias = jnp.take_along_axis(rel, jnp.broadcast_to(rel_idx[None, None], (b, h, s, s)), axis=3)
        causal = j <= i
        logits = jnp.where(causal[None, None], (scores + bias) * scale, -jnp.inf)
        attn = jax.nn.softmax(logits, axis=-1)
        out = jnp.einsum('bhij,bhjd->bhid', attn, v)
        out = out.transpose(0, 2, 1, 3).reshape(b, s, e)
        return out @ Wo + bo

    def _L2_ffn_ref(hidden_states, gate_w, Wg, Wu, Wd, Ws_g, Ws_u, Ws_d):
        import jax, jax.numpy as jnp
        import numpy as np
        B, S, D = (4, 1024, 256)
        E, F_EXP = (16, 512)
        F_C = 2.0
        F_SH = 512
        b, s, d = hidden_states.shape
        e = gate_w.shape[0]
        cap = int(s * F_C / e)
        logits = jnp.einsum('bsd,ed->bse', hidden_states, gate_w)
        scores = jax.nn.softmax(logits, axis=-1).transpose(0, 2, 1)
        topk_w, topk_idx = jax.lax.top_k(scores, cap)
        x_tok = jnp.take_along_axis(hidden_states[:, None, :, :], topk_idx[..., None], axis=2)
        g = jnp.einsum('becd,efd->becf', x_tok, Wg)
        u = jnp.einsum('becd,efd->becf', x_tok, Wu)
        h = jax.nn.gelu(g, approximate=False) * u
        eo = jnp.einsum('becf,edf->becd', h, Wd) * topk_w[..., None]
        offs = (jnp.arange(b) * s)[:, None, None]
        flat_idx = (topk_idx + offs).reshape(-1)
        flat = jnp.zeros((b * s, d), hidden_states.dtype)
        flat = flat.at[flat_idx].add(eo.reshape(-1, d))
        out = flat.reshape(b, s, d)
        gs = jnp.einsum('bsd,fd->bsf', hidden_states, Ws_g)
        us = jnp.einsum('bsd,fd->bsf', hidden_states, Ws_u)
        shared = jnp.einsum('bsf,df->bsd', jax.nn.gelu(gs, approximate=False) * us, Ws_d)
        return out + shared

    def _L3_attn_ref(x, W_q, W_k, W_v, W_o, W_down_kv, W_up_k, W_up_v):
        import jax, jax.numpy as jnp
        import numpy as np
        import math
        B, S, D = (4, 512, 256)
        H = 16
        HD = D // H
        DL = 64
        LAMBDA_DECAY = 0.01
        b, s, d = x.shape
        q = x @ W_q
        k = x @ W_k
        v = x @ W_v
        latent_kv = (k + v) @ W_down_kv
        k_rec = (latent_kv @ W_up_k).reshape(b, s, H, HD).transpose(0, 2, 1, 3)
        v_rec = (latent_kv @ W_up_v).reshape(b, s, H, HD).transpose(0, 2, 1, 3)
        qh = q.reshape(b, s, H, HD).transpose(0, 2, 1, 3)
        scores = jnp.einsum('bhqd,bhkd->bhqk', qh, k_rec) / math.sqrt(d)
        t = jnp.arange(s, dtype=jnp.float32)
        decay = jnp.exp(-LAMBDA_DECAY * jnp.abs(t[:, None] - t[None, :]))
        scores = scores * decay[None, None, :, :]
        attn = jax.nn.softmax(scores, axis=-1)
        out = jnp.einsum('bhqk,bhkd->bhqd', attn, v_rec)
        out = out.transpose(0, 2, 1, 3).reshape(b, s, d)
        return out @ W_o

    def _L3_ffn_ref(hidden_states, sim_matrix, gates, q_proj, k_proj, v_proj, o_proj):
        import jax, jax.numpy as jnp
        import numpy as np
        import math
        HID, HD, E, MIN_E = (256, 128, 16, 2)
        B, T = (4, 512)
        IS_CAUSAL = True

        def _l2norm(x, axis):
            return x / jnp.sqrt(jnp.sum(x * x, axis=axis, keepdims=True) + 1e-12)

        def _gating(hidden_states, sim_matrix, gates):
            b, t, c = hidden_states.shape
            flat = hidden_states.reshape(b * t, c)
            logits = _l2norm(flat, -1) @ _l2norm(sim_matrix, 0) - jax.nn.sigmoid(gates)
            gated = jax.nn.relu(logits)
            mask = (gated > 0).astype(gated.dtype)
            inactive = jnp.sum(mask, axis=1) == 0
            _, top_idx = jax.lax.top_k(logits, MIN_E)
            fb = jnp.sum(jax.nn.one_hot(top_idx, E, dtype=mask.dtype), axis=1)
            mask = mask + inactive[:, None].astype(mask.dtype) * fb
            masked = jnp.where(mask > 0, gated, -jnp.inf)
            probs = jax.nn.softmax(masked, axis=-1)
            return probs
        b, t, c = hidden_states.shape
        rw = _gating(hidden_states, sim_matrix, gates).reshape(b, t, E)
        q = jnp.einsum('btc,ech,bte->bth', hidden_states, q_proj, rw)
        k = jnp.einsum('btc,ech,bte->bth', hidden_states, k_proj, rw)
        v = jnp.einsum('btc,ech,bte->bth', hidden_states, v_proj, rw)
        scale = 1.0 / math.sqrt(HD)
        scores = jnp.einsum('bqh,bkh->bqk', q, k) * scale
        if IS_CAUSAL:
            causal = jnp.tril(jnp.ones((t, t), dtype=bool))
            scores = jnp.where(causal[None], scores, -jnp.inf)
        attn = jax.nn.softmax(scores, axis=-1)
        ao = jnp.einsum('bqk,bkh->bqh', attn, v)
        out = jnp.einsum('bth,ehc,bte->btc', ao, o_proj, rw)
        return out
    h = _L0_tok_ref(x, L0_tok_Wq_w, L0_tok_Wq_b, L0_tok_Wk_w, L0_tok_Wk_b, L0_tok_Wv_w, L0_tok_Wv_b, L0_tok_w_bias, L0_tok_out_w, L0_tok_out_b, L0_tok_ln_g, L0_tok_ln_b, L0_tok_local_mask)
    h = h + _L0_attn_ref(_layernorm(h, axis=-1), L0_attn_W_qkv, L0_attn_b_qkv, L0_attn_W_proj, L0_attn_b_proj)
    h = h + _L0_ffn_ref(_layernorm(h, axis=-1), L0_ffn_W_fc, L0_ffn_ln_w, L0_ffn_ln_b, L0_ffn_W_proj)
    h = h + _L1_attn_ref(_layernorm(h, axis=-1), L1_attn_Wq, L1_attn_bq, L1_attn_Wk, L1_attn_bk, L1_attn_Wv, L1_attn_bv, L1_attn_Wo, L1_attn_bo)
    h = h + _L1_ffn_ref(_layernorm(h, axis=-1), L1_ffn_W_r, L1_ffn_W_k, L1_ffn_W_v, L1_ffn_mu_r, L1_ffn_mu_k)
    h = h + _L2_attn_ref(_layernorm(h, axis=-1), L2_attn_Wq, L2_attn_bq, L2_attn_Wk, L2_attn_bk, L2_attn_Wv, L2_attn_bv, L2_attn_Wo, L2_attn_bo, L2_attn_rel_key)
    h = h + _L2_ffn_ref(_layernorm(h, axis=-1), L2_ffn_gate_w, L2_ffn_Wg, L2_ffn_Wu, L2_ffn_Wd, L2_ffn_Ws_g, L2_ffn_Ws_u, L2_ffn_Ws_d)
    h = h + _L3_attn_ref(_layernorm(h, axis=-1), L3_attn_W_q, L3_attn_W_k, L3_attn_W_v, L3_attn_W_o, L3_attn_W_down_kv, L3_attn_W_up_k, L3_attn_W_up_v)
    h = h + _L3_ffn_ref(_layernorm(h, axis=-1), L3_ffn_sim_matrix, L3_ffn_gates, L3_ffn_q_proj, L3_ffn_k_proj, L3_ffn_v_proj, L3_ffn_o_proj)
    return h

_drawn_inputs = setup_inputs


def setup_inputs(seed=0):
    import zlib

    import numpy as np

    out = dict(_drawn_inputs(seed))
    spreads = {'L0_tok_Wq_b': (0.0, 0.8),
     'L0_tok_Wk_b': (0.0, 2.0),
     'L0_tok_Wv_b': (0.0, 0.1),
     'L0_tok_out_b': (0.0, 0.1),
     'L0_tok_ln_g': (1.0, 0.2),
     'L0_tok_ln_b': (0.0, 0.1),
     'L0_attn_b_qkv': (0.0, 0.1),
     'L0_attn_b_proj': (0.0, 0.1),
     'L0_ffn_ln_w': (1.0, 0.2),
     'L0_ffn_ln_b': (0.0, 0.1),
     'L1_attn_bq': (0.0, 0.8),
     'L1_attn_bk': (0.0, 2.0),
     'L1_attn_bv': (0.0, 0.8),
     'L1_attn_bo': (0.0, 0.8),
     'L2_attn_bq': (0.0, 0.8),
     'L2_attn_bk': (0.0, 2.0),
     'L2_attn_bv': (0.0, 2.0),
     'L2_attn_bo': (0.0, 2.0),
     'L3_ffn_gates': (0.0, 2.0)}
    factors = {'L0_tok_w_bias': 8.0,
     'L1_attn_Wq': 2.849,
     'L1_attn_Wk': 2.802,
     'L1_ffn_W_r': 8.0,
     'L1_ffn_W_k': 8.0,
     'L1_ffn_W_v': 8.0,
     'L1_ffn_mu_r': 8.0,
     'L1_ffn_mu_k': 8.0,
     'L2_attn_Wq': 8.0,
     'L2_attn_Wk': 8.0,
     'L2_attn_Wv': 4.96,
     'L2_attn_Wo': 4.7,
     'L2_attn_rel_key': 23.26,
     'L2_ffn_gate_w': 8.0,
     'L2_ffn_Wg': 8.0,
     'L2_ffn_Wu': 8.0,
     'L2_ffn_Wd': 8.0,
     'L2_ffn_Ws_g': 8.0,
     'L2_ffn_Ws_u': 8.0,
     'L2_ffn_Ws_d': 8.0,
     'L3_attn_W_q': 8.0,
     'L3_attn_W_k': 7.742,
     'L3_attn_W_v': 7.886,
     'L3_attn_W_o': 5.323,
     'L3_attn_W_down_kv': 5.274,
     'L3_attn_W_up_k': 8.0,
     'L3_attn_W_up_v': 5.298,
     'L3_ffn_sim_matrix': 64.0,
     'L3_ffn_q_proj': 57.943,
     'L3_ffn_k_proj': 58.304,
     'L3_ffn_v_proj': 55.415,
     'L3_ffn_o_proj': 55.42}
    for name, (base, spread) in spreads.items():
        noise = np.random.default_rng([zlib.crc32(name.encode()), seed]).standard_normal(out[name].shape)
        drawn = base * np.exp(spread * noise) if base else spread * noise
        out[name] = jnp.asarray(drawn.astype(out[name].dtype))
    for name, factor in factors.items():
        out[name] = (out[name] * factor).astype(out[name].dtype)
    return out
```

```python
from contextlib import ExitStack

import numpy as np

import concourse.bass as bass
from concourse import mybir

ALU = mybir.AluOpType
ACT = mybir.ActivationFunctionType
AX = mybir.AxisListType.X
F32 = mybir.dt.float32
BF16 = mybir.dt.bfloat16

P = 128
B = 8
S = 256
D = 256
TS = S // P
TILES = B * TS
KD = D // P
HEADS = 16
HD = D // HEADS
HG = 4
NG = HEADS // HG
SUMCOL = HD
PAD = 2 * TS
EPS = 1e-5
BIG = 3.0e38
NEG = -1.0e30
ds = bass.ds


class Chain:

    def __init__(self, eng, sem, before=0, turn=0, per=0):
        self.eng, self.sem, self.n, self.per = eng, sem, before, per
        self.base = turn * per if per else 0

    def link(self, ins):
        self.n += 1
        ins.then_inc(self.sem, 1)
        self.eng.wait_ge(self.sem, self.base + self.n if self.per else self.n)

    def done(self, before):
        assert self.n - before == self.per, (self.n, before, self.per)


class Stage:

    def __init__(self, nc, name):
        self.nc, self.name, self.ctx, self.sems, self.work = nc, name, ExitStack(), [], None

    def __enter__(self):
        self.ctx.__enter__()
        return self

    def __exit__(self, *a):
        if a[0] is not None:
            return self.ctx.__exit__(*a)
        self.work.__exit__(*a)
        with self.nc.Block() as clearing:
            @clearing.sync
            def _(sp):
                for s in self.sems:
                    sp.sem_clear(s)
        return self.ctx.__exit__(*a)

    def sem(self, name):
        self.sems.append(self.ctx.enter_context(self.nc.semaphore(f"{self.name}_{name}")))
        return self.sems[-1]

    def sb(self, name, shape, dt=F32):
        return self.ctx.enter_context(self.nc.sbuf_tensor(f"{self.name}_{name}", shape, dt))

    def ps(self, name, shape=(P, 512)):
        return self.ctx.enter_context(self.nc.psum_tensor(f"{self.name}_{name}_ps", list(shape), F32))

    def block(self):
        self.work = self.nc.Block()
        return self.work.__enter__()


class Norm:

    def __init__(self, nc, st, h):
        self.nc, self.h = nc, h
        self.stats = st.sb("ln_stats", [P, TILES, 6])
        self.mr = st.sb("ln_mean_rstd", [P, TILES + PAD, 2])
        self.std = st.sb("ln_std", [P, TILES])
        self.cur = st.sb("ln_cur", [P, TS, 2])
        self.var_ready = st.sem("ln_var_ready")
        self.std_ready = st.sem("ln_std_ready")

    def stats_dve(self, dve, ch):
        nc = self.nc
        for t in range(TILES):
            last = nc.vector.bn_stats(self.stats[:, t, :], self.h[:, t, :])
        ch.link(last)
        for t in range(TILES):
            last = nc.vector.bn_aggr(self.mr[:, t, :], self.stats[:, t, :])
        nc.vector.memset(self.mr[:, TILES:TILES + PAD, :], 0.0)
        ch.link(nc.vector.memset(self.h[:, TILES:TILES + PAD, :], 0.0))
        nc.vector.tensor_scalar(self.std[:, :], self.mr[:, 0:TILES, 1], EPS, None, ALU.add).then_inc(self.var_ready, 1)
        dve.wait_ge(self.std_ready, 1)
        ch.link(nc.vector.reciprocal(self.mr[:, 0:TILES, 1], self.std[:, :]))

    def sqrt_act(self, act):
        act.wait_ge(self.var_ready, 1)
        self.nc.scalar.activation(self.std[:, :], self.std[:, :], ACT.Sqrt).then_inc(self.std_ready, 1)

    def apply_dve(self, ch, b, dst):
        nc = self.nc
        ch.link(nc.vector.tensor_copy(self.cur[:, :, :], self.mr[:, ds(TS * b, TS), :]))
        for s in range(TS):
            last = nc.vector.tensor_scalar(dst(s), self.h[:, ds(TS * b + s, 1), :], self.cur[:, s, 0:1],
                                           self.cur[:, s, 1:2], ALU.subtract, ALU.mult)
        return last

    STATS_LINKS = 3
    APPLY_LINKS = 1


def tok_mixer(nc, dram, h, ident):
    F, H = 64, 4
    QKV = 3 * F
    with Stage(nc, "tok") as st:
        xa = st.sb("xa", [F + 1, 2, H, S])
        xflat = st.sb("xflat", [P, 2, TS, D])
        wqkv = st.sb("wqkv", [F + 1, QKV])
        ewT = st.sb("ewT", [P, TS, S])
        mask_int = st.sb("mask_int", [P, TS, S], mybir.dt.int32)
        maskf = st.sb("maskf", [P, TS, S])
        outw = st.sb("outw", [P, KD, D])
        vecs = st.sb("vecs", [P, 3, D])
        enq = st.sb("enq", [P, TS, D])
        rhs = st.sb("rhs", [P, TS, 2, D])
        dn = st.sb("dn", [P, TS, D])
        y = st.sb("y", [P, TS, D])
        yT = st.sb("yT", [P, KD, S])
        hp = st.sb("hp", [P, TS, D])
        norm = Norm(nc, st, h)
        proj_ps = [st.ps(f"proj{n}") for n in range(4)]
        mix_ps = [st.ps(f"mix{n}") for n in range(2)]
        t_ps = st.ps("t")
        out_ps = st.ps("out")

        w_in = st.sem("w_in")
        x_in = [st.sem(f"x{o}_in") for o in range(2)]
        xf_in = [st.sem(f"xflat{o}_in") for o in range(2)]
        pre = st.sem("pre")
        ew_ready = st.sem("ew_ready")
        proj_done = st.sem("proj_done")
        proj_read = st.sem("proj_read")
        exps = st.sem("exps")
        rhs_ready = st.sem("rhs_ready")
        mix_done = st.sem("mix_done")
        chain = st.sem("chain")
        y_ready = st.sem("y_ready")
        yt_done = st.sem("yt_done")
        yt_ready = st.sem("yt_ready")
        out_done = st.sem("out_done")
        out_read = st.sem("out_read")
        block = st.block()
        NW = 6

        @block.sync
        def _(sp):
            sp.dma_start(wqkv[:, :], dram["tok_wqkv"]).then_inc(w_in, 16)
            sp.dma_start(ewT[:, :, :], dram["tok_wbT"].rearrange("(k p) t -> p k t", p=P)).then_inc(w_in, 16)
            sp.dma_start(mask_int[:, :, :], dram["tok_maskT"].rearrange("(k p) t -> p k t", p=P)).then_inc(w_in, 16)
            sp.dma_start(outw[:, :, :], dram["tok_outw"].rearrange("(k p) t -> p k t", p=P)).then_inc(w_in, 16)
            sp.dma_start(vecs[:, :, :], dram["tok_vecs"].partition_broadcast(P)).then_inc(w_in, 16)
            sp.dma_start(ident[:, :], dram["ident"]).then_inc(w_in, 16)
            with sp.Fori(0, B // 2) as i:
                for o in range(2):
                    sp.wait_ge(proj_done, 4 * i)
                    sp.dma_start(xa[:, o, :, :], dram["tok_x"][ds(2 * i + o, 1)].rearrange("a c h l -> (a c) h l")).then_inc(x_in[o], 16)
                    sp.wait_ge(out_read, 2 * i)
                    sp.dma_start(xflat[:, o, :, :], dram["tok_xflat"][ds(2 * i + o, 1)].rearrange(
                        "a (s p) d -> p (a s) d", p=P)).then_inc(xf_in[o], 16)

        @block.tensor
        def _(pe):
            pe.wait_ge(w_in, 16 * NW)
            pe.wait_ge(ew_ready, 1)
            with pe.Fori(0, B // 2) as i:
                for o in range(2):
                    b = 2 * i + o
                    pe.wait_ge(x_in[o], 16 * i + 16)
                    pe.wait_ge(proj_read, 2 * b)
                    pe.wait_ge(rhs_ready, 2 * b)
                    for s in range(TS):
                        for hh in range(H):
                            last = nc.tensor.matmul(
                                proj_ps[2 * s + hh // 2][:, (hh % 2) * QKV:(hh % 2 + 1) * QKV],
                                xa[:, o, hh, s * P:(s + 1) * P], wqkv[:, :], start=True, stop=True)
                        last.then_inc(proj_done, 1)
                    pe.wait_ge(rhs_ready, 2 * b + 2)
                    pe.wait_ge(y_ready, b)
                    for t in range(TS):
                        for s in range(TS):
                            last = nc.tensor.matmul(mix_ps[t][:, :], ewT[:, s, t * P:(t + 1) * P],
                                                    rhs[:, s, :, :], start=(s == 0), stop=(s == TS - 1))
                        last.then_inc(mix_done, 1)
                    pe.wait_ge(y_ready, b + 1)
                    pe.wait_ge(yt_ready, b)
                    for k in range(KD):
                        for s in range(TS):
                            last = nc.tensor.transpose(t_ps[:, k * S + s * P:k * S + (s + 1) * P],
                                                       y[:, s, k * P:(k + 1) * P], ident[:, :])
                    last.then_inc(yt_done, 1)
                    pe.wait_ge(yt_ready, b + 1)
                    pe.wait_ge(out_read, b)
                    for s in range(TS):
                        for k in range(KD):
                            last = nc.tensor.matmul(out_ps[:, s * D:(s + 1) * D], yT[:, k, s * P:(s + 1) * P],
                                                    outw[:, k, :], start=(k == 0), stop=(k == KD - 1))
                    last.then_inc(out_done, 1)

        @block.scalar
        def _(act):
            act.wait_ge(w_in, 16 * NW)
            act.wait_ge(pre, 2)
            nc.scalar.activation(ewT[:, :, :], ewT[:, :, :], ACT.Exp).then_inc(ew_ready, 1)
            with act.Fori(0, B // 2) as i:
                for o in range(2):
                    b = 2 * i + o
                    act.wait_ge(mix_done, 2 * b)
                    act.wait_ge(y_ready, b)
                    for s in range(TS):
                        act.wait_ge(proj_done, 2 * b + s + 1)
                        for n in range(2):
                            v = proj_ps[2 * s + n][:, 0:2 * QKV].rearrange("p (a r) -> p a r", a=2)
                            nc.scalar.activation(rhs[:, s, 1, n * 128:(n + 1) * 128].rearrange("p (a r) -> p a r", a=2),
                                                 v[:, :, F:2 * F], ACT.Exp)
                            last = nc.scalar.activation(enq[:, s, n * 128:(n + 1) * 128].rearrange("p (a r) -> p a r", a=2),
                                                        v[:, :, 0:F], ACT.Exp, scale=-1.0)
                        last.then_inc(proj_read, 1)
                    act.wait_ge(yt_done, b + 1)
                    act.wait_ge(out_done, b)
                    nc.scalar.activation(yT[:, :, :], t_ps[:, :].rearrange("p (k t) -> p k t", k=KD),
                                         ACT.Copy).then_inc(yt_ready, 1)
            norm.sqrt_act(act)

        @block.vector
        def _(dve):
            dve.wait_ge(w_in, 16 * NW)
            nc.vector.tensor_copy(maskf[:, :, :], mask_int[:, :, :]).then_inc(pre, 1)
            dve.wait_ge(pre, 1)
            nc.vector.tensor_tensor(ewT[:, :, :], ewT[:, :, :], maskf[:, :, :], ALU.mult).then_inc(pre, 1)
            per = 2 * (2 + 1)
            with dve.Fori(0, B // 2) as i:
                ch = Chain(dve, chain, 0, i, per)
                for o in range(2):
                    b = 2 * i + o
                    dve.wait_ge(mix_done, 2 * b)
                    for s in range(TS):
                        dve.wait_ge(proj_read, 2 * b + s + 1)
                        for n in range(2):
                            v = proj_ps[2 * s + n][:, 0:2 * QKV].rearrange("p (a r) -> p a r", a=2)
                            last = nc.vector.tensor_tensor(
                                rhs[:, s, 0, n * 128:(n + 1) * 128].rearrange("p (a r) -> p a r", a=2),
                                rhs[:, s, 1, n * 128:(n + 1) * 128].rearrange("p (a r) -> p a r", a=2),
                                v[:, :, 2 * F:3 * F], ALU.mult)
                        last.then_inc(rhs_ready, 1)
                    for t in range(TS):
                        dve.wait_ge(mix_done, 2 * b + t + 1)
                        last = nc.vector.scalar_tensor_tensor(dn[:, t, :], enq[:, t, :], 1.0, mix_ps[t][:, D:2 * D],
                                                              ALU.add, ALU.mult)
                    ch.link(last)
                    ch.link(nc.vector.reciprocal(dn[:, :, :], dn[:, :, :]))
                    dve.wait_ge(yt_done, b)
                    for t in range(TS):
                        last = nc.vector.tensor_tensor(y[:, t, :], mix_ps[t][:, 0:D], dn[:, t, :], ALU.mult)
                    last.then_inc(y_ready, 1)
                    dve.wait_ge(xf_in[o], 16 * i + 16)
                    for s in range(TS):
                        last = nc.vector.tensor_tensor(hp[:, s, :], xflat[:, o, s, :], vecs[:, 0, :], ALU.add)
                    ch.link(last)
                    dve.wait_ge(out_done, b + 1)
                    for s in range(TS):
                        last = nc.vector.tensor_tensor(
                            h[:, ds(TS * b + s, 1), :], out_ps[:, s * D:(s + 1) * D].rearrange("p (a d) -> p a d", a=1),
                            hp[:, s:s + 1, :], ALU.add)
                    last.then_inc(out_read, 1)
                ch.done(0)
            ch = Chain(dve, chain, per * (B // 2))
            dve.wait_ge(out_read, B)
            norm.stats_dve(dve, ch)
            for t in range(TILES):
                last = nc.vector.tensor_scalar(h[:, t, :], h[:, t, :], norm.mr[:, t, 0:1], norm.mr[:, t, 1:2],
                                               ALU.subtract, ALU.mult)
            ch.link(last)
            for n, op in ((1, ALU.mult), (2, ALU.add)):
                ch.link(nc.vector.tensor_tensor(h[:, 0:TILES, :], h[:, 0:TILES, :],
                                                vecs[:, n:n + 1, :].broadcast_to([P, TILES, D]), op))


def opened(eng, *sems):
    for s in sems:
        eng.sem_inc(s, 1)


def at(n):
    return n + 1


def attention(nc, dram, h, ident, name, scale, causal=False, kind="plain", latent=False, relative=False):
    HU = 2
    NU = HEADS // HU
    width = [P, S] if causal else [S, S]
    off = [0, width[0]]
    W = width[0] + width[1]
    with Stage(nc, name) as st:
        wq = st.sb("wq", [P, KD, NG * P])
        wk = st.sb("wk", [P, KD, NG * P])
        wv = st.sb("wv", [P, KD, NG * P])
        wo = st.sb("wo", [P, NG, D])
        bqk = st.sb("bqk", [P, 2, NG])
        bv = st.sb("bv", [P, NG * P])
        bo = st.sb("bo", [P, D])
        sumsel = st.sb("sumsel", [P, P])
        if kind != "plain":
            matrix = st.sb("matrix", [P, TS, S])
        xn = st.sb("xn", [P, TS, D])
        xT = st.sb("xT", [P, KD, S])
        qT = st.sb("qT", [P, NG, S])
        kT = st.sb("kT", [P, NG, S])
        v = st.sb("v", [P, TS, NG * P])
        if kind != "plain":
            z = st.sb("z", [P, 2, HU, W])
        pr = st.sb("pr", [P, 2, HU, W])
        nmax = st.sb("nmax", [P, 2, HU, TS])
        gate = st.sb("gate", [P, NU])
        prT = st.sb("prT", [P, 2, HU, TS, S])
        oT = st.sb("oT", [P, 2, S])
        rs = st.sb("rs", [P, 2, S])
        on = st.sb("on", [P, NG, S])
        sc_ps = st.ps("scores", (P, HG, 512))
        t_ps = st.ps("t", (P, 2, 512))
        o_ps = st.ps("o")
        m_ps = st.ps("m")
        norm = Norm(nc, st, h)

        w_in = st.sem("w_in")
        chain = st.sem("chain")
        xn_ready, xt_done, xt_ready = st.sem("xn_ready"), st.sem("xt_done"), st.sem("xt_ready")
        qk_done, v_done, qk_ready, v_ready = (st.sem(n) for n in ("qk_done", "v_done", "qk_ready", "v_ready"))
        sc_done, max_ready, exp_done = st.sem("sc_done"), st.sem("max_ready"), st.sem("exp_done")
        t_done, t_read_act, t_read_dve = st.sem("t_done"), st.sem("t_read_act"), st.sem("t_read_dve")
        av_done, o_ready, sum_done, on_ready = (st.sem(n) for n in ("av_done", "o_ready", "sum_done", "on_ready"))
        y_done, h_ready, hb_ready = st.sem("y_done"), st.sem("h_ready"), st.sem("hb_ready")
        if latent:
            wdown = st.sb("wdown", [P, KD, 64])
            wupk = st.sb("wupk", [64, NG * P])
            wupv = st.sb("wupv", [64, NG * P])
            kvT = st.sb("kvT", [P, KD, S])
            latT = st.sb("latT", [64, S])
            kv_done, kv_ready, lat_done, lat_ready = (st.sem(n) for n in ("kv_done", "kv_ready", "lat_done", "lat_ready"))
        if relative:
            relT = st.sb("relT", [P, S])
            rel_out = st.sb("rel_out", [P, NU, HU, W])
            bias = st.sb("bias", [P, NU, HU, W])
            rel_dram = nc.dram_tensor(f"{name}_rel", (NU, HU, TS, P, S), F32).ap()
            rel_done, bias_ready = st.sem("rel_done"), st.sem("bias_ready")
            rel_ready = [st.sem(f"rel_ready_{e}") for e in ("dve", "act")]
            rel_sent = [st.sem(f"rel_sent{u}") for u in range(NU)]
            bias_in = [st.sem(f"bias_in{u}") for u in range(NU)]
        norm_per = 1 + NG + (NU if kind == "mult" else 0)
        block = st.block()
        loads = [(wq, "wq"), (wo, "wo")] + [(wk, "wk"), (wv, "wv")]
        if latent:
            loads += [(wdown, "wdown")]
        nw = 0

        sc_free = exp_done if kind == "plain" else max_ready

        cols = [slice(0, S), slice(S + P, 2 * S)] if causal else [slice(0, 2 * S)]

        def group_width(g):
            return slice(g * P, (g + 1) * P)

        def rows(u, t, w, ap, first):
            flat = rel_dram[u, 0, t]
            return bass.AP(flat.tensor, flat.offset + first, ap)

        @block.sync
        def _(sp):
            nonlocal nw
            for t, n in loads:
                sp.dma_start(t[:, :, 0:dram[f"{name}_{n}"].shape[1]], dram[f"{name}_{n}"].rearrange("(k p) n -> p k n", p=P)).then_inc(w_in, 16)
                nw += 1
            flat = [(bqk, "bqk"), (sumsel, "sumsel")] + ([(wupk, "wupk"), (wupv, "wupv")] if latent else [])
            flat += [(relT, "relT")] if relative else []
            flat += [(matrix, "matrix")] if kind != "plain" else []
            for t, n in flat:
                a = dram[f"{name}_{n}"] if n != "sumsel" else dram["sumsel"]
                idx = (slice(None),) * len(a.shape)
                sp.dma_start(t[idx], a).then_inc(w_in, 16)
                nw += 1
            sp.dma_start(bv[:, :], dram[f"{name}_bv"].partition_broadcast(P)).then_inc(w_in, 16)
            sp.dma_start(bo[:, :], dram[f"{name}_bo"].partition_broadcast(P)).then_inc(w_in, 16)
            nw += 2
            if relative:
                with sp.Fori(0, B) as i:
                    for u in range(NU):
                        sp.wait_ge(rel_ready[u % 2], at(NU // 2 * i + u // 2 + 1))
                        for t, w in enumerate(width):
                            sp.dma_start(rows(u, t, w, [[w, P], [TS * P * S, HU], [1, w]], 0),
                                         rel_out[:, u, :, off[t]:off[t] + w]).then_inc(rel_sent[u], 16)
                    for u in range(NU):
                        sp.wait_ge(rel_sent[u], 16 * TS * (i + 1))
                        if u == 0:
                            sp.wait_ge(max_ready, at(NU * i))
                        for t, w in enumerate(width):
                            sp.dma_start(bias[:, u, :, off[t]:off[t] + w],
                                         rows(u, t, w, [[w - 1, P], [TS * P * S, HU], [1, w]], P - 1)).then_inc(bias_in[u], 16)

        @block.tensor
        def _(pe):
            opened(pe, xt_done, qk_done, v_done, sc_done, t_done, av_done, sum_done, y_done)
            if latent:
                opened(pe, kv_done, lat_done)
            if relative:
                opened(pe, rel_done)
            pe.wait_ge(w_in, 16 * nw)

            def transpose_x(n):
                pe.wait_ge(xn_ready, at(n + 1))
                for k in range(KD):
                    for s in range(TS):
                        last = nc.tensor.transpose(t_ps[:, 0, k * S + s * P:k * S + (s + 1) * P],
                                                   xn[:, s, k * P:(k + 1) * P], ident[:, :])
                last.then_inc(xt_done, 1)

            def scores(i, u):
                g = u // 2
                if u < 2:
                    pe.wait_ge(qk_ready, at(2 * i + 2))
                else:
                    pe.wait_ge(sc_free, at(NU * i + u - 1))
                for j in range(HU):
                    r = slice(32 * (HU * (u % 2) + j), 32 * (HU * (u % 2) + j) + 32)
                    for s in range(TS):
                        last = nc.tensor.matmul(sc_ps[:, HU * (u % 2) + j, off[s]:off[s] + width[s]],
                                                qT[r, g, s * P:(s + 1) * P], kT[r, g, 0:width[s]],
                                                start=True, stop=True)
                last.then_inc(sc_done, 1)

            def transpose_weights(i, u):
                pe.wait_ge(exp_done, at(NU * i + u + 1))
                pe.wait_ge(t_read_act, at((NU + 1) * i + 1 + u))
                if u == 0:
                    pe.wait_ge(v_ready, at(TS * (i + 1)))
                else:
                    pe.wait_ge(t_read_dve, at(NU * i + u))
                for j in range(HU):
                    for s in range(TS):
                        for k in range(width[s] // P):
                            last = nc.tensor.transpose(t_ps[:, j, k * S + s * P:k * S + (s + 1) * P],
                                                       pr[:, u % 2, j, off[s] + k * P:off[s] + (k + 1) * P], ident[:, :])
                last.then_inc(t_done, 1)

            def values(i, u):
                g = u // 2
                pe.wait_ge(t_read_act, at((NU + 1) * i + 2 + u))
                pe.wait_ge(t_read_dve, at(NU * i + u + 1))
                if u % 2 == 0:
                    pe.wait_ge(o_ready, at(NG * i + g))
                for j in range(HU):
                    jj = HU * (u % 2) + j
                    for k in range(TS):
                        q0 = P * k if causal else 0
                        last = nc.tensor.matmul(o_ps[32 * jj:32 * jj + 32, q0:S], v[:, k, g * P + 32 * jj:g * P + 32 * jj + 32],
                                                prT[:, u % 2, j, k, q0:S], start=(k == 0), stop=(k == TS - 1),
                                                skip_group_check=True)
                last.then_inc(av_done, 1)

            def sums(i, g):
                pe.wait_ge(o_ready, at(NG * i + g + 1))
                pe.wait_ge(on_ready, at(NG * i + g))
                nc.tensor.matmul(m_ps[:, 0:S], sumsel[:, :], oT[:, g % 2, :],
                                 start=True, stop=True).then_inc(sum_done, 1)

            transpose_x(0)
            with pe.Fori(0, B) as i:
                pe.wait_ge(t_read_act, at((NU + 1) * i + 1))
                pe.wait_ge(exp_done, at(NU * i))
                if kind != "plain":
                    pe.wait_ge(max_ready, at(NU * i))
                pe.wait_ge(h_ready, at(i))
                if not latent:
                    projections = [(wq, 0, xT, KD, 0), (wk, 1, xT, KD, 0)]
                else:
                    for m in range(KD):
                        for n, w in enumerate((wk, wv)):
                            for k in range(KD):
                                last = nc.tensor.matmul(m_ps[:, m * S:(m + 1) * S], w[:, k, m * P:(m + 1) * P], xT[:, k, :],
                                                        start=(n + k == 0), stop=(n == 1 and k == KD - 1))
                    last.then_inc(kv_done, 1)
                    pe.wait_ge(kv_ready, at(i + 1))
                    for k in range(KD):
                        last = nc.tensor.matmul(o_ps[0:64, 0:S], wdown[:, k, :], kvT[:, k, :],
                                                start=(k == 0), stop=(k == KD - 1))
                    last.then_inc(lat_done, 1)
                    projections = [(wq, 0, xT, KD, 0), (wupk, 1, latT, 1, 1)]
                for w, n, x, chunks, lat in projections:
                    if lat:
                        pe.wait_ge(lat_ready, at(i + 1))
                    for g in range(NG):
                        for k in range(chunks):
                            lhs = w[:, group_width(g)] if lat else w[:, k, group_width(g)]
                            rhs = x[:, :] if lat else x[:, k, :]
                            last = nc.tensor.matmul(sc_ps[:, 2 * n + g // 2, (g % 2) * S:(g % 2 + 1) * S], lhs, rhs,
                                                    start=(k == 0), stop=(k == chunks - 1))
                    last.then_inc(qk_done, 1)
                pe.wait_ge(t_read_dve, at(NU * i))
                for s in range(TS):
                    if latent:
                        last = nc.tensor.matmul(t_ps[:, s, :], latT[:, s * P:(s + 1) * P], wupv[:, :], start=True, stop=True)
                    else:
                        for k in range(KD):
                            last = nc.tensor.matmul(t_ps[:, s, :], xT[:, k, s * P:(s + 1) * P], wv[:, k, :],
                                                    start=(k == 0), stop=(k == KD - 1))
                    last.then_inc(v_done, 1)
                if relative:
                    for u in range(NU):
                        g = u // 2
                        if u == 0:
                            pe.wait_ge(qk_ready, at(2 * i + 2))
                        if u >= 2:
                            pe.wait_ge(rel_ready[u % 2], at(NU // 2 * i + u // 2))
                        for j in range(HU):
                            r = slice(32 * (HU * (u % 2) + j), 32 * (HU * (u % 2) + j) + 32)
                            for s in range(TS):
                                last = nc.tensor.matmul(sc_ps[:, HU * (u % 2) + j, off[s]:off[s] + width[s]],
                                                        qT[r, g, s * P:(s + 1) * P], relT[r, S - width[s]:S],
                                                        start=True, stop=True)
                        last.then_inc(rel_done, 1)
                    for n in range(2):
                        pe.wait_ge(rel_ready[n], at(NU // 2 * (i + 1)))
                scores(i, 0)
                scores(i, 1)
                for u in range(NU):
                    transpose_weights(i, u)
                    if u + 2 < NU:
                        scores(i, u + 2)
                    if u >= 1:
                        values(i, u - 1)
                    if u % 2 == 1 and u >= 3:
                        sums(i, u // 2 - 1)
                values(i, NU - 1)
                pe.wait_ge(t_read_act, at((NU + 1) * i + 1 + NU))
                transpose_x(i + 1)
                sums(i, NG - 1)
                pe.wait_ge(on_ready, at(NG * (i + 1)))
                for s in range(TS):
                    for g in range(NG):
                        last = nc.tensor.matmul(m_ps[:, s * D:(s + 1) * D], on[:, g, s * P:(s + 1) * P], wo[:, g, :],
                                                start=(g == 0), stop=(g == NG - 1))
                last.then_inc(y_done, 1)

        @block.scalar
        def _(act):
            opened(act, exp_done, t_read_act, o_ready, qk_ready)
            if relative:
                opened(act, rel_ready[1])
            if latent:
                opened(act, kv_ready, lat_ready)
            act.wait_ge(w_in, 16 * nw)
            norm.sqrt_act(act)

            def copy_x(n):
                act.wait_ge(xt_done, at(n + 1))
                nc.scalar.activation(xT[:, :, :], t_ps[:, 0, :].rearrange("p (k t) -> p k t", k=KD), ACT.Copy)\
                    .then_inc(t_read_act, 1)

            def copy_weights(i, u):
                act.wait_ge(t_done, at(NU * i + u + 1))
                act.wait_ge(av_done, at(NU * i + max(0, u - 1)))
                for c in cols:
                    last = nc.scalar.activation(prT[:, u % 2, 0, :, :].rearrange("p k q -> p (k q)")[:, c], t_ps[:, 0, c], ACT.Copy)
                last.then_inc(t_read_act, 1)

            def copy_o(i, g):
                act.wait_ge(av_done, at(NU * i + 2 * g + 2))
                act.wait_ge(on_ready, at(NG * i + max(0, g - 1)))
                nc.scalar.activation(oT[:, g % 2, :], o_ps[:, 0:S], ACT.Copy).then_inc(o_ready, 1)

            def copy_rel(i, u):
                act.wait_ge(rel_done, at(NU * i + u + 1))
                nc.scalar.activation(rel_out[:, u, :, :], sc_ps[:, 2:4, 0:W], ACT.Copy)\
                    .then_inc(rel_ready[u % 2], 1)

            copy_x(0)
            with act.Fori(0, B) as i:
                if latent:
                    act.wait_ge(kv_done, at(i + 1))
                    nc.scalar.activation(kvT[:, :, :], m_ps[:, :].rearrange("p (k t) -> p k t", k=KD), ACT.Copy)\
                        .then_inc(kv_ready, 1)
                    act.wait_ge(lat_done, at(i + 1))
                    nc.scalar.activation(latT[:, :], o_ps[0:64, 0:S], ACT.Copy).then_inc(lat_ready, 1)
                for n, dst in ((0, qT), (1, kT)):
                    act.wait_ge(qk_done, at(2 * i + n + 1))
                    for g in range(NG):
                        last = nc.scalar.activation(dst[:, g, :], sc_ps[:, 2 * n + g // 2, (g % 2) * S:(g % 2 + 1) * S],
                                                    ACT.Identity, bias=bqk[:, n, g:g + 1], scale=scale if n == 0 else 1.0)
                    last.then_inc(qk_ready, 1)
                if relative:
                    for u in range(1, NU, 2):
                        copy_rel(i, u)
                for u in range(NU):
                    act.wait_ge(max_ready, at(NU * i + u + 1))
                    if u >= 2:
                        act.wait_ge(t_done, at(NU * i + u - 1))
                    for j in range(HU):
                        for s, w in enumerate(width):
                            c = slice(off[s], off[s] + w)
                            if kind == "plain":
                                src, sgn = sc_ps[:, HU * (u % 2) + j, c], 1.0
                            else:
                                src, sgn = z[:, u % 2, j, c], -1.0 if kind == "add" else 1.0
                            last = nc.scalar.activation(pr[:, u % 2, j, c], src, ACT.Exp,
                                                        bias=nmax[:, u % 2, j, s:s + 1], scale=sgn)
                    last.then_inc(exp_done, 1)
                    if u >= 1:
                        copy_weights(i, u - 1)
                    if u % 2 == 1 and u >= 3:
                        copy_o(i, u // 2 - 1)
                copy_weights(i, NU - 1)
                copy_o(i, NG - 1)
                copy_x(i + 1)


        @block.vector
        def _(dve):
            opened(dve, xn_ready, v_ready, max_ready, t_read_dve, on_ready, h_ready)
            if relative:
                opened(dve, rel_ready[0])
            ch = Chain(dve, chain)
            dve.wait_ge(w_in, 16 * nw)
            ch.link(nc.vector.tensor_scalar(bqk[:, 0, :], bqk[:, 0, :], scale, None, ALU.mult))
            norm.stats_dve(dve, ch)
            norm.apply_dve(ch, 0, lambda s: xn[:, s:s + 1, :]).then_inc(xn_ready, 1)
            before = ch.n

            def copy_weights(i, u):
                dve.wait_ge(t_done, at(NU * i + u + 1))
                dve.wait_ge(av_done, at(NU * i + max(0, u - 1)))
                for c in cols:
                    last = nc.vector.tensor_copy(prT[:, u % 2, 1, :, :].rearrange("p k q -> p (k q)")[:, c], t_ps[:, 1, c])
                last.then_inc(t_read_dve, 1)

            def normalize(i, g):
                dve.wait_ge(sum_done, at(NG * i + g + 1))
                ch.link(nc.vector.reciprocal(rs[:, g % 2, :], m_ps[:, 0:S]))
                if g == 0:
                    dve.wait_ge(y_done, at(i))
                nc.vector.tensor_tensor(on[:, g, :], oT[:, g % 2, :], rs[:, g % 2, :], ALU.mult).then_inc(on_ready, 1)

            with dve.Fori(0, B) as i:
                ch = Chain(dve, chain, before, i, norm_per)
                for s in range(TS):
                    dve.wait_ge(v_done, at(TS * i + s + 1))
                    dve.wait_ge(av_done, at(NU * i))
                    nc.vector.tensor_tensor(v[:, s, :], t_ps[:, s, :], bv[:, :], ALU.add).then_inc(v_ready, 1)
                if relative:
                    for u in range(0, NU, 2):
                        dve.wait_ge(rel_done, at(NU * i + u + 1))
                        nc.vector.tensor_copy(rel_out[:, u, :, :], sc_ps[:, 0:2, 0:W])\
                            .then_inc(rel_ready[0], 1)
                for u in range(NU):
                    banks = slice(HU * (u % 2), HU * (u % 2) + HU)
                    dve.wait_ge(sc_done, at(NU * i + u + 1))
                    if u >= 2:
                        dve.wait_ge(exp_done, at(NU * i + u - 1))
                    if relative:
                        dve.wait_ge(bias_ready, at(NU * i + u + 1))
                    if kind == "plain":
                        nc.vector.tensor_reduce(nmax[:, u % 2, :, :], sc_ps[:, banks, :].rearrange("p j (s k) -> p j s k", s=TS),
                                                AX, ALU.max, negate=True)\
                            .then_inc(max_ready, 1)
                    else:
                        nc.vector.memset(gate[:, u:u + 1], 0.0)
                        if kind == "add":
                            op0, op1, sgn, start = ALU.add, ALU.min, -1.0, BIG
                        else:
                            op0, op1, sgn, start = ALU.mult, ALU.max, 1.0, -BIG
                        for j in range(HU):
                            for s, w in enumerate(width):
                                c = slice(off[s], off[s] + w)
                                m = bias[:, u, j, c] if relative else matrix[:, s, 0:w]
                                last = nc.vector.tensor_tensor_reduce(z[:, u % 2, j, c], sc_ps[:, HU * (u % 2) + j, c], m,
                                                                      sgn, start, op0, op1, nmax[:, u % 2, j, s:s + 1])
                        if kind == "mult":
                            ch.link(last)
                            last = nc.vector.tensor_scalar(nmax[:, u % 2, :, :], nmax[:, u % 2, :, :], -1.0, None, ALU.mult)
                        last.then_inc(max_ready, 1)
                    if u >= 1:
                        copy_weights(i, u - 1)
                    if u == 3:
                        dve.wait_ge(xt_done, at(i + 1))
                        norm.apply_dve(ch, i + 1, lambda s: xn[:, s:s + 1, :]).then_inc(xn_ready, 1)
                    if u % 2 == 0 and u >= 4:
                        normalize(i, u // 2 - 2)
                copy_weights(i, NU - 1)
                normalize(i, NG - 2)
                normalize(i, NG - 1)
                dve.wait_ge(y_done, at(i + 1))
                dve.wait_ge(hb_ready, at(i + 1))
                for s in range(TS):
                    hs = h[:, ds(TS * i + s, 1), :]
                    last = nc.vector.tensor_tensor(hs, m_ps[:, s * D:(s + 1) * D].rearrange("p (a d) -> p a d", a=1),
                                                   hs, ALU.add)
                last.then_inc(h_ready, 1)
                ch.done(before)

        @block.gpsimd
        def _(pool):
            opened(pool, hb_ready)
            if relative:
                opened(pool, bias_ready)
            pool.wait_ge(w_in, 16 * nw)
            with pool.Fori(0, B) as i:
                pool.wait_ge(xn_ready, at(i + 1))
                for s in range(TS):
                    hs = h[:, ds(TS * i + s, 1), :]
                    last = nc.gpsimd.tensor_tensor(hs, hs, bo[:, :].rearrange("p (a d) -> p a d", a=1), ALU.add)
                last.then_inc(hb_ready, 1)
                if relative:
                    for u in range(NU):
                        pool.wait_ge(bias_in[u], 16 * TS * (i + 1))
                        for s, w in enumerate(width):
                            c = slice(off[s], off[s] + w)
                            last = nc.gpsimd.tensor_tensor(bias[:, u, :, c], bias[:, u, :, c],
                                                           matrix[:, s:s + 1, 0:w].broadcast_to([P, HU, w]), ALU.add)
                        last.then_inc(bias_ready, 1)


def ternary_mlp(nc, dram, h, ident):
    FF = 4 * D
    KF = FF // P
    with Stage(nc, "f0") as st:
        wfc = st.sb("wfc", [P, KD, FF])
        wproj = st.sb("wproj", [P, KF, D])
        low = st.sb("low", [P, 2048])
        lnwb = st.sb("lnwb", [P, 2, KF])
        ones = st.sb("ones", [P, P])
        sizes = st.sb("sizes", [P, 2])
        limit = st.sb("limit", [P, 2, 2])
        xn = st.sb("xn", [P, TS, D])
        xT = st.sb("xT", [P, KD, S])
        g = st.sb("g", [P, TILES + PAD, FF])
        gstats = st.sb("gstats", [P, 2, TS, 2, 6])
        gmv = st.sb("gmv", [P, 2, TS, 2])
        gmr = st.sb("gmr", [P, TILES + PAD, 2])
        gstd = st.sb("gstd", [P, TILES])
        gcur = st.sb("gcur", [P, TS, 2])
        gate = st.sb("gate", [P, 1])
        gn = st.sb("gn", [P, TS, FF])
        gT = st.sb("gT", [P, 2, KF, S])
        b_ps = [st.ps(f"b{n}") for n in range(4)]
        t_ps = st.ps("t")
        y_ps = st.ps("y")
        norm = Norm(nc, st, h)

        w_in, chain, sizes_ready, total_done, w_ready = (st.sem(n) for n in ("w_in", "chain", "sizes_ready", "total_done", "w_ready"))
        xn_ready, xt_done, xt_ready, fc_done, g_ready = (st.sem(n) for n in ("xn_ready", "xt_done", "xt_ready", "fc_done", "g_ready"))
        gvar_ready, gstd_ready, stats_read = st.sem("gvar_ready"), st.sem("gstd_ready"), st.sem("stats_read")
        gn_ready, gt_done, gt_act, gt_dve, y_done, h_ready = (
            st.sem(n) for n in ("gn_ready", "gt_done", "gt_act", "gt_dve", "y_done", "h_ready"))
        block = st.block()
        NW = 3

        @block.sync
        def _(sp):
            sp.dma_start(wfc[:, :, :], dram["f0_wfcT"].rearrange("(k p) n -> p k n", p=P)).then_inc(w_in, 16)
            sp.dma_start(wproj[:, :, :], dram["f0_wprojT"].rearrange("(k p) n -> p k n", p=P)).then_inc(w_in, 16)
            sp.dma_start(lnwb[:, :, :], dram["f0_lnwb"]).then_inc(w_in, 16)

        @block.tensor
        def _(pe):
            opened(pe, xt_done, fc_done, gt_done, y_done)
            pe.wait_ge(sizes_ready, 1)
            nc.tensor.matmul(y_ps[:, 0:2], ones[:, :], sizes[:, :], start=True, stop=True).then_inc(total_done, 1)

            def transpose_x(n):
                pe.wait_ge(xn_ready, at(n + 1))
                pe.wait_ge(xt_ready, at(n))
                for k in range(KD):
                    for s in range(TS):
                        last = nc.tensor.transpose(t_ps[:, k * S + s * P:k * S + (s + 1) * P],
                                                   xn[:, s, k * P:(k + 1) * P], ident[:, :])
                last.then_inc(xt_done, 1)

            transpose_x(0)
            pe.wait_ge(w_ready, 1)
            with pe.Fori(0, B) as i:
                pe.wait_ge(xt_ready, at(i + 1))
                for s in range(TS):
                    pe.wait_ge(g_ready, at(TS * i))
                    for n in range(2):
                        for k in range(KD):
                            last = nc.tensor.matmul(b_ps[2 * s + n][:, :], xT[:, k, s * P:(s + 1) * P],
                                                    wfc[:, k, n * 512:(n + 1) * 512], start=(k == 0), stop=(k == KD - 1))
                    last.then_inc(fc_done, 1)
                transpose_x(i + 1)
            pe.wait_ge(g_ready, at(TILES))

            def transpose_g(n, o):
                pe.wait_ge(gn_ready, at(n + 1))
                pe.wait_ge(gt_act, at(n))
                pe.wait_ge(gt_dve, at(n))
                for k in range(KF):
                    for s in range(TS):
                        last = nc.tensor.transpose(b_ps[k // 2][:, (k % 2) * S + s * P:(k % 2) * S + (s + 1) * P],
                                                   gn[:, s, k * P:(k + 1) * P], ident[:, :])
                last.then_inc(gt_done, 1)

            transpose_g(0, 0)
            with pe.Fori(0, B // 2) as i:
                for o in range(2):
                    b = 2 * i + o
                    transpose_g(b + 1, 1 - o)
                    pe.wait_ge(h_ready, at(b))
                    for s in range(TS):
                        for k in range(KF):
                            last = nc.tensor.matmul(y_ps[:, s * D:(s + 1) * D], gT[:, o, k, s * P:(s + 1) * P],
                                                    wproj[:, k, :], start=(k == 0), stop=(k == KF - 1))
                    last.then_inc(y_done, 1)

        @block.scalar
        def _(act):
            opened(act, xt_ready, g_ready, gt_act)
            norm.sqrt_act(act)

            def copy_x(n):
                act.wait_ge(xt_done, at(n + 1))
                act.wait_ge(fc_done, at(TS * n))
                nc.scalar.activation(xT[:, :, :], t_ps[:, :].rearrange("p (k t) -> p k t", k=KD), ACT.Copy)\
                    .then_inc(xt_ready, 1)

            copy_x(0)
            with act.Fori(0, B) as i:
                for s in range(TS):
                    act.wait_ge(fc_done, at(TS * i + s + 1))
                    for n in range(2):
                        last = nc.scalar.activation(g[:, ds(TS * i + s, 1), n * 512:(n + 1) * 512],
                                                    b_ps[2 * s + n][:, :].rearrange("p (a n) -> p a n", a=1), ACT.Gelu)
                    last.then_inc(g_ready, 1)
                copy_x(i + 1)
            act.wait_ge(gvar_ready, 1)
            nc.scalar.activation(gstd[:, :], gstd[:, :], ACT.Sqrt).then_inc(gstd_ready, 1)

            def copy_g(n, o):
                act.wait_ge(gt_done, at(n + 1))
                if not isinstance(n, int):
                    act.wait_ge(y_done, at(n - 1))
                for k in range(KF // 2):
                    last = nc.scalar.activation(gT[:, o, k, :], b_ps[k // 2][:, (k % 2) * S:(k % 2 + 1) * S], ACT.Identity,
                                                bias=lnwb[:, 1, k:k + 1], scale=lnwb[:, 0, k:k + 1])
                last.then_inc(gt_act, 1)

            copy_g(0, 0)
            with act.Fori(0, B // 2) as i:
                for o in range(2):
                    copy_g(2 * i + o + 1, 1 - o)

        @block.vector
        def _(dve):
            opened(dve, xn_ready, gn_ready, gt_dve, h_ready)
            ch = Chain(dve, chain)
            nc.vector.memset(ones[:, :], 1.0)
            nc.vector.memset(g[:, TILES:TILES + PAD, :], 0.0)
            nc.vector.memset(gmr[:, TILES:TILES + PAD, :], 0.0)
            dve.wait_ge(w_in, 16 * NW)
            for n, w in enumerate((wfc, wproj)):
                last = nc.vector.tensor_reduce(sizes[:, n:n + 1], w[:, :, :].rearrange("p k n -> p (k n)"), AX, ALU.add,
                                               apply_absolute_value=True)
            last.then_inc(sizes_ready, 1)
            norm.stats_dve(dve, ch)
            norm.apply_dve(ch, 0, lambda s: xn[:, s:s + 1, :]).then_inc(xn_ready, 1)
            dve.wait_ge(total_done, 1)
            ch.link(nc.vector.tensor_scalar(limit[:, 0, :], y_ps[:, 0:2], 1.0 / (D * FF), 1e-6, ALU.mult, ALU.add))
            ch.link(nc.vector.tensor_scalar(limit[:, 0, :], limit[:, 0, :], 0.5, None, ALU.mult))
            ch.link(nc.vector.tensor_scalar(limit[:, 1, :], limit[:, 0, :], -1.0, None, ALU.mult))
            for n, w in enumerate((wfc, wproj)):
                flat = w[:, :, :].rearrange("p k n -> p (k n)")
                ch.link(nc.vector.tensor_scalar(low[:, :], flat, limit[:, 1, n:n + 1], None, ALU.is_lt))
                last = nc.vector.scalar_tensor_tensor(flat, flat, limit[:, 0, n:n + 1], low[:, :], ALU.is_gt, ALU.subtract)
                if n == 0:
                    ch.link(last)
            last.then_inc(w_ready, 1)
            before = ch.n
            per = 1 + 3
            with dve.Fori(0, B) as i:
                ch = Chain(dve, chain, before, i, per)
                dve.wait_ge(xt_done, at(i + 1))
                norm.apply_dve(ch, i + 1, lambda s: xn[:, s:s + 1, :]).then_inc(xn_ready, 1)
                for s in range(TS):
                    dve.wait_ge(g_ready, at(TS * i + s + 1))
                    for n in range(2):
                        last = nc.vector.bn_stats(gstats[:, 0, s, n, :], g[:, ds(TS * i + s, 1), n * 512:(n + 1) * 512])
                ch.link(last)
                nc.vector.memset(gate[:, :], 0.0)
                for s in range(TS):
                    last = nc.vector.bn_aggr(gmv[:, 0, s, :], gstats[:, 0, s, :, :])
                ch.link(last)
                ch.link(nc.vector.tensor_copy(gmr[:, ds(TS * i, TS), :], gmv[:, 0, :, :]))
                ch.done(before)
            before2 = before + per * B
            ch = Chain(dve, chain, before2)
            nc.vector.tensor_scalar(gstd[:, :], gmr[:, 0:TILES, 1], EPS, None, ALU.add).then_inc(gvar_ready, 1)
            dve.wait_ge(gstd_ready, 1)
            ch.link(nc.vector.reciprocal(gmr[:, 0:TILES, 1], gstd[:, :]))

            def normalize_g(n):
                ch.link(nc.vector.tensor_copy(gcur[:, :, :], gmr[:, ds(TS * n, TS), :]))
                dve.wait_ge(gt_done, at(n))
                for s in range(TS):
                    last = nc.vector.tensor_scalar(gn[:, s:s + 1, :], g[:, ds(TS * n + s, 1), :], gcur[:, s, 0:1],
                                                   gcur[:, s, 1:2], ALU.subtract, ALU.mult)
                last.then_inc(gn_ready, 1)

            def copy_g(n, o):
                dve.wait_ge(gt_done, at(n + 1))
                if not isinstance(n, int):
                    dve.wait_ge(y_done, at(n - 1))
                for k in range(KF // 2, KF):
                    last = nc.vector.tensor_scalar(gT[:, o, k, :], b_ps[k // 2][:, (k % 2) * S:(k % 2 + 1) * S],
                                                   lnwb[:, 0, k:k + 1], lnwb[:, 1, k:k + 1], ALU.mult, ALU.add)
                last.then_inc(gt_dve, 1)

            normalize_g(0)
            copy_g(0, 0)
            normalize_g(1)
            before3 = ch.n
            per = 2
            with dve.Fori(0, B // 2) as i:
                ch = Chain(dve, chain, before3, i, per)
                for o in range(2):
                    b = 2 * i + o
                    copy_g(b + 1, 1 - o)
                    normalize_g(b + 2)
                    dve.wait_ge(y_done, at(b + 1))
                    for s in range(TS):
                        hs = h[:, ds(TS * b + s, 1), :]
                        last = nc.vector.tensor_tensor(hs, y_ps[:, s * D:(s + 1) * D].rearrange("p (a d) -> p a d", a=1),
                                                       hs, ALU.add)
                    last.then_inc(h_ready, 1)
                ch.done(before3)


def channel_mixer(nc, dram, h, ident):
    with Stage(nc, "f1") as st:
        w = st.sb("w", [P, 3, KD, D])
        mu = st.sb("mu", [P, 2, 2, KD])
        xn = st.sb("xn", [P, TS, D])
        xT = st.sb("xT", [P, KD, S + 1])
        part = st.sb("part", [P, 2, KD, S])
        mixed = st.sb("mixed", [P, 2, KD, S])
        r = st.sb("r", [P, TS, D])
        kr = st.sb("kr", [P, KD, S])
        k2 = st.sb("k2", [P, KD, S])
        o = st.sb("o", [P, TS, D])
        t_ps, r_ps, k_ps, v_ps = (st.ps(n) for n in ("t", "r", "k", "v"))
        norm = Norm(nc, st, h)
        w_in, chain, xn_ready, xt_done, xt_ready, mixed_ready = (
            st.sem(n) for n in ("w_in", "chain", "xn_ready", "xt_done", "xt_ready", "mixed_ready"))
        r_done, k_done, r_ready, kr_ready, k2_ready, v_done, o_ready, h_ready = (
            st.sem(n) for n in ("r_done", "k_done", "r_ready", "kr_ready", "k2_ready", "v_done", "o_ready", "h_ready"))
        block = st.block()
        NW = 4

        @block.sync
        def _(sp):
            for n, name in enumerate(("wr", "wk", "wv")):
                sp.dma_start(w[:, n, :, :], dram[f"f1_{name}T"].rearrange("(k p) n -> p k n", p=P)).then_inc(w_in, 16)
            sp.dma_start(mu[:, 0, :, :], dram["f1_mu"]).then_inc(w_in, 16)

        @block.tensor
        def _(pe):
            opened(pe, xt_done, r_done, k_done, v_done)
            pe.wait_ge(w_in, 16 * NW)

            def transpose_x(n):
                pe.wait_ge(xn_ready, at(n + 1))
                pe.wait_ge(xt_ready, at(n))
                for k in range(KD):
                    for s in range(TS):
                        last = nc.tensor.transpose(t_ps[:, k * S + s * P:k * S + (s + 1) * P],
                                                   xn[:, s, k * P:(k + 1) * P], ident[:, :])
                last.then_inc(xt_done, 1)

            transpose_x(0)
            with pe.Fori(0, B) as i:
                transpose_x(i + 1)
                pe.wait_ge(mixed_ready, at(i + 1))
                pe.wait_ge(kr_ready, at(i))
                for m in range(KD):
                    for k in range(KD):
                        last = nc.tensor.matmul(k_ps[:, m * S:(m + 1) * S], w[:, 1, k, m * P:(m + 1) * P],
                                                mixed[:, 1, k, :], start=(k == 0), stop=(k == KD - 1))
                last.then_inc(k_done, 1)
                pe.wait_ge(r_ready, at(i))
                for s in range(TS):
                    for k in range(KD):
                        last = nc.tensor.matmul(r_ps[:, s * D:(s + 1) * D], mixed[:, 0, k, s * P:(s + 1) * P],
                                                w[:, 0, k, :], start=(k == 0), stop=(k == KD - 1))
                last.then_inc(r_done, 1)
                pe.wait_ge(k2_ready, at(i + 1))
                pe.wait_ge(o_ready, at(i))
                for s in range(TS):
                    for k in range(KD):
                        last = nc.tensor.matmul(v_ps[:, s * D:(s + 1) * D], k2[:, k, s * P:(s + 1) * P],
                                                w[:, 2, k, :], start=(k == 0), stop=(k == KD - 1))
                last.then_inc(v_done, 1)

        @block.scalar
        def _(act):
            opened(act, xt_ready, kr_ready, r_ready)
            norm.sqrt_act(act)

            def copy_x(n):
                act.wait_ge(xt_done, at(n + 1))
                act.wait_ge(mixed_ready, at(n))
                nc.scalar.activation(xT[:, :, 1:S + 1], t_ps[:, :].rearrange("p (k t) -> p k t", k=KD), ACT.Copy)\
                    .then_inc(xt_ready, 1)

            copy_x(0)
            with act.Fori(0, B) as i:
                copy_x(i + 1)
                act.wait_ge(k_done, at(i + 1))
                act.wait_ge(k2_ready, at(i))
                nc.scalar.activation(kr[:, :, :], k_ps[:, :].rearrange("p (k t) -> p k t", k=KD), ACT.Relu)\
                    .then_inc(kr_ready, 1)
                act.wait_ge(r_done, at(i + 1))
                act.wait_ge(o_ready, at(i))
                nc.scalar.activation(r[:, :, :], r_ps[:, :].rearrange("p (s d) -> p s d", s=TS), ACT.Sigmoid)\
                    .then_inc(r_ready, 1)

        @block.vector
        def _(dve):
            opened(dve, xn_ready, mixed_ready, o_ready)
            ch = Chain(dve, chain)
            nc.vector.memset(xT[:, :, 0:1], 0.0)
            dve.wait_ge(w_in, 16 * NW)
            ch.link(nc.vector.tensor_scalar(mu[:, 1, :, :], mu[:, 0, :, :], -1.0, 1.0, ALU.mult, ALU.add))
            norm.stats_dve(dve, ch)
            norm.apply_dve(ch, 0, lambda s: xn[:, s:s + 1, :]).then_inc(xn_ready, 1)

            def mix(n):
                dve.wait_ge(xt_ready, at(n + 1))
                for m in range(2):
                    for k in range(KD):
                        last = nc.vector.tensor_scalar(part[:, m, k, :], xT[:, k, 0:S], mu[:, 1, m, k:k + 1], None, ALU.mult)
                ch.link(last)
                dve.wait_ge(r_done, at(n))
                for m in range(2):
                    for k in range(KD):
                        last = nc.vector.scalar_tensor_tensor(mixed[:, m, k, :], xT[:, k, 1:S + 1], mu[:, 0, m, k:k + 1],
                                                              part[:, m, k, :], ALU.mult, ALU.add)
                last.then_inc(mixed_ready, 1)

            def next_x(n):
                dve.wait_ge(xt_done, at(n))
                norm.apply_dve(ch, n, lambda s: xn[:, s:s + 1, :]).then_inc(xn_ready, 1)

            dve.wait_ge(xt_done, at(1))
            norm.apply_dve(ch, 1, lambda s: xn[:, s:s + 1, :]).then_inc(xn_ready, 1)
            mix(0)
            before = ch.n
            per = 2
            with dve.Fori(0, B) as i:
                ch = Chain(dve, chain, before, i, per)
                next_x(i + 2)
                mix(i + 1)
                dve.wait_ge(v_done, at(i + 1))
                dve.wait_ge(r_ready, at(i + 1))
                dve.wait_ge(h_ready, at(i))
                nc.vector.tensor_tensor(o[:, :, :], v_ps[:, :].rearrange("p (s d) -> p s d", s=TS), r[:, :, :], ALU.mult)\
                    .then_inc(o_ready, 1)
                ch.done(before)

        @block.gpsimd
        def _(pool):
            opened(pool, k2_ready, h_ready)
            with pool.Fori(0, B) as i:
                pool.wait_ge(kr_ready, at(i + 1))
                pool.wait_ge(v_done, at(i))
                nc.gpsimd.tensor_tensor(k2[:, :, :], kr[:, :, :], kr[:, :, :], ALU.mult).then_inc(k2_ready, 1)
                pool.wait_ge(o_ready, at(i + 1))
                hs = h[:, ds(TS * i, TS), :]
                nc.gpsimd.tensor_tensor(hs, hs, o[:, :, :], ALU.add).then_inc(h_ready, 1)


def expert_choice(nc, dram, h, ident):
    E = 16
    CAP = int(S * 2.0 / E)
    FF = 512
    KF = FF // P
    EG = P // CAP
    NEG_E = E // EG
    BG = P // CAP
    SLOTS = B * CAP
    with Stage(nc, "moe") as st:
        gate = st.sb("gate", [P, KD, E])
        iota = st.sb("iota", [P, 1, CAP])
        xn = st.sb("xn", [P, TS, D])
        xTb = st.sb("xTb", [P, KD, S])
        xT = st.sb("xT", [P, KD, B * S])
        sc = st.sb("sc", [P, TS, B, E])
        smax = st.sb("smax", [P, TS * B])
        ssum = st.sb("ssum", [P, TS * B])
        work = st.sb("work", [P, S])
        top8 = st.sb("top8", [P, 8])
        taken = st.sb("taken", [P, S])
        zeros = st.sb("zeros", [P, S])
        slot = st.sb("slot", [P, S])
        slotT = st.sb("slotT", [P, TS, B, E])
        pick = st.sb("pick", [P, TS, E, CAP])
        pickw = st.sb("pickw", [P, TS, E, CAP])
        xg = st.sb("xg", [P, KD, E, B, CAP])
        back = st.sb("back", [P, B, NEG_E, S])
        backb = st.sb("backb", [P, NEG_E, S])
        wx = [st.sb(f"wx{n}", [P, 2 * KD * FF + KF * D]) for n in range(2)]
        act_g = st.sb("act_g", [P, KF, S])
        hT = st.sb("hT", [P, KF, S])
        eo = st.sb("eo", [P, 2, B // BG, D])
        eo2 = st.sb("eo2", [P, NEG_E, B, D])
        g_ps = [st.ps(f"g{n}") for n in range(2)]
        u_ps = [st.ps(f"u{n}") for n in range(2)]
        e_ps = st.ps("e")
        t_ps = st.ps("t")
        l_ps = st.ps("l")
        norm = Norm(nc, st, h)

        w_in, chain, xn_ready, xt_done, xt_ready, xall_ready, lg_done, lg_ready = (
            st.sem(n) for n in ("w_in", "chain", "xn_ready", "xt_done", "xt_ready", "xall_ready", "lg_done", "lg_ready"))
        less_max, exp_ready, sc_ready, scT_done, slot_ready, slotT_done = (
            st.sem(n) for n in ("less_max", "exp_ready", "sc_ready", "scT_done", "slot_ready", "slotT_done"))
        xg_xn_ready, pick_ready, pickw_ready, gather_done, gather_act, gather_dve, back_done, back_act, back_dve = (
            st.sem(n) for n in ("xg_xn_ready", "pick_ready", "pickw_ready", "gather_done", "gather_act", "gather_dve",
                                "back_done", "back_act", "back_dve"))
        gu_done, gelu_ready, hT_ready, eo_done, eo_ready = (
            st.sem(n) for n in ("gu_done", "gelu_ready", "hT_ready", "eo_done", "eo_ready"))
        wx_in = [st.sem(f"wx{n}_in") for n in range(2)]
        eo_sent = [st.sem(f"eo_sent{n}") for n in range(2)]
        backb_ready, y_done, h_ready = st.sem("backb_ready"), st.sem("y_done"), st.sem("h_ready")
        block = st.block()
        NW = 2

        def weights(n):
            a = KD * FF
            return (wx[n][:, 0:a].rearrange("p (k f) -> p k f", k=KD), wx[n][:, a:2 * a].rearrange("p (k f) -> p k f", k=KD),
                    wx[n][:, 2 * a:].rearrange("p (k d) -> p k d", k=KF))

        @block.sync
        def _(sp):
            sp.dma_start(gate[:, :, :], dram["moe_gateT"].rearrange("(k p) n -> p k n", p=P)).then_inc(w_in, 16)
            sp.dma_start(iota[:, 0, :], dram["moe_iota"].partition_broadcast(P)).then_inc(w_in, 16)
            for e in range(2):
                sp.dma_start(wx[e][:, :], dram["moe_experts"][e]).then_inc(wx_in[e], 16)
            for s in eo_sent:
                sp.sem_inc(s, 16)
            with sp.Fori(0, NEG_E) as q:
                for e in range(EG):
                    sp.wait_ge(eo_ready, at(EG * q + e + 1))
                    for b in range(BG):
                        sp.dma_start(eo2[CAP * e:CAP * (e + 1), ds(q, 1), b:B:BG, :],
                                     eo[CAP * b:CAP * (b + 1), e % 2, :, :].rearrange("p (a b) d -> p a b d", a=1))\
                            .then_inc(eo_sent[e % 2], 16)
                    sp.dma_start(wx[e % 2][:, :], dram["moe_experts"][ds(EG * q + e + 2, 1)].rearrange("a p n -> (a p) n"))\
                        .then_inc(wx_in[e % 2], 16)

        @block.tensor
        def _(pe):
            opened(pe, xt_done, lg_done, gather_done, back_done, gu_done, eo_done, y_done)
            pe.wait_ge(w_in, 16 * NW)
            with pe.Fori(0, B) as i:
                pe.wait_ge(xn_ready, at(i + 1))
                for k in range(KD):
                    for s in range(TS):
                        last = nc.tensor.transpose(t_ps[:, k * S + s * P:k * S + (s + 1) * P],
                                                   xn[:, s, k * P:(k + 1) * P], ident[:, :])
                last.then_inc(xt_done, 1)
                pe.wait_ge(xt_ready, at(i + 1))
                pe.wait_ge(lg_ready, at(i))
                for s in range(TS):
                    for k in range(KD):
                        last = nc.tensor.matmul(l_ps[:, s * E:(s + 1) * E], xTb[:, k, s * P:(s + 1) * P], gate[:, k, :],
                                                start=(k == 0), stop=(k == KD - 1))
                last.then_inc(lg_done, 1)
            pe.wait_ge(sc_ready, 1)
            for s in range(TS):
                last = nc.tensor.transpose(l_ps[:, s * P:(s + 1) * P], sc[:, s, :, :].rearrange("p b e -> p (b e)"), ident[:, :])
            last.then_inc(scT_done, 1)
            pe.wait_ge(slot_ready, 1)
            for s in range(TS):
                last = nc.tensor.transpose(l_ps[:, s * P:(s + 1) * P], slot[:, s * P:(s + 1) * P], ident[:, :])
            last.then_inc(slotT_done, 1)
            with pe.Fori(0, B) as i:
                pe.wait_ge(xg_xn_ready, at(i + 1))
                pe.wait_ge(pick_ready, at(i + 1))
                pe.wait_ge(gather_act, at(i))
                pe.wait_ge(gather_dve, at(i))
                for k in range(KD):
                    for s in range(TS):
                        last = nc.tensor.matmul(g_ps[k][:, :], xn[:, s, k * P:(k + 1) * P],
                                                pick[:, s, :, :].rearrange("p e c -> p (e c)"),
                                                start=(s == 0), stop=(s == TS - 1))
                last.then_inc(gather_done, 1)
                pe.wait_ge(pickw_ready, at(i + 1))
                pe.wait_ge(back_act, at(i))
                pe.wait_ge(back_dve, at(i))
                for q in range(NEG_E):
                    for s in range(TS):
                        last = nc.tensor.transpose(
                            u_ps[q // 2][:, (q % 2) * S + s * P:(q % 2) * S + (s + 1) * P],
                            pickw[:, s, EG * q:EG * (q + 1), :].rearrange("p e c -> p (e c)"), ident[:, :])
                last.then_inc(back_done, 1)

            def gate_up(w, x, n):
                for m in range(2):
                    pe.wait_ge(gelu_ready, at(2 * n))
                    pe.wait_ge(hT_ready, at(2 * n))
                    for ps, wn in ((g_ps[m], w[0]), (u_ps[m], w[1])):
                        for f in range(2):
                            for k in range(KD):
                                c = (2 * m + f) * P
                                last = nc.tensor.matmul(ps[:, f * S:(f + 1) * S], wn[:, k, c:c + P], x(k),
                                                        start=(k == 0), stop=(k == KD - 1))
                    last.then_inc(gu_done, 1)

            pe.wait_ge(gather_act, at(B))
            pe.wait_ge(gather_dve, at(B))
            pe.wait_ge(back_act, at(B))
            pe.wait_ge(back_dve, at(B))
            with pe.Fori(0, NEG_E) as q:
                for e in range(EG):
                    n = EG * q + e
                    w = weights(e % 2)
                    pe.wait_ge(wx_in[e % 2], 32 * q + 16 * (e // 2) + 16)
                    gate_up(w, lambda k: xg[:, k, ds(n, 1), :, :].rearrange("p a b c -> p (a b c)"), n)
                    pe.wait_ge(hT_ready, at(2 * n + 2))
                    pe.wait_ge(eo_ready, at(n))
                    for g in range(B // BG):
                        for k in range(KF):
                            last = nc.tensor.matmul(e_ps[:, g * D:(g + 1) * D], hT[:, k, g * P:(g + 1) * P], w[2][:, k, :],
                                                    start=(k == 0), stop=(k == KF - 1))
                    last.then_inc(eo_done, 1)
            w = weights(0)
            pe.wait_ge(wx_in[0], 16 * (E // 2 + 1))
            pe.wait_ge(wx_in[1], 16 * (E // 2 + 1))
            pe.wait_ge(eo_ready, at(E))
            for o in range(2):
                pe.wait_ge(eo_sent[o], 16 * BG * E // 2 + 16)
            with pe.Fori(0, B) as i:
                gate_up(w, lambda k: xT[:, k, ds(S * i, S)], i + E)
                pe.wait_ge(hT_ready, at(2 * (i + E) + 2))
                pe.wait_ge(backb_ready, at(i + 1))
                pe.wait_ge(h_ready, at(i))
                for s in range(TS):
                    for k in range(KF):
                        nc.tensor.matmul(e_ps[:, s * D:(s + 1) * D], hT[:, k, s * P:(s + 1) * P], w[2][:, k, :],
                                         start=(k == 0), stop=False)
                    for q in range(NEG_E):
                        last = nc.tensor.matmul(e_ps[:, s * D:(s + 1) * D], backb[:, q, s * P:(s + 1) * P],
                                                eo2[:, q, ds(i, 1), :].rearrange("p a d -> p (a d)"),
                                                start=False, stop=(q == NEG_E - 1))
                last.then_inc(y_done, 1)

        @block.scalar
        def _(act):
            opened(act, xt_ready, gather_act, back_act, gelu_ready, eo_ready)
            norm.sqrt_act(act)
            with act.Fori(0, B) as i:
                act.wait_ge(xt_done, at(i + 1))
                act.wait_ge(xall_ready, at(i))
                act.wait_ge(lg_done, at(i))
                nc.scalar.activation(xTb[:, :, :], t_ps[:, :].rearrange("p (k t) -> p k t", k=KD), ACT.Copy)\
                    .then_inc(xt_ready, 1)
            act.wait_ge(less_max, 1)
            nc.scalar.activation(sc[:, :, :, :], sc[:, :, :, :], ACT.Exp).then_inc(exp_ready, 1)
            with act.Fori(0, B) as i:
                act.wait_ge(gather_done, at(i + 1))
                nc.scalar.activation(xg[:, 0, :, ds(i, 1), :], g_ps[0][:, :].rearrange("p (e a c) -> p e a c", e=E, a=1),
                                     ACT.Copy).then_inc(gather_act, 1)
                act.wait_ge(back_done, at(i + 1))
                nc.scalar.activation(back[:, ds(i, 1), 0:2, :], u_ps[0][:, :].rearrange("p (a q t) -> p a q t", a=1, q=2),
                                     ACT.Copy).then_inc(back_act, 1)

            def gelus(n):
                for m in range(2):
                    act.wait_ge(gu_done, at(2 * n + m + 1))
                    act.wait_ge(hT_ready, at(2 * n))
                    nc.scalar.activation(act_g[:, 2 * m:2 * m + 2, :], g_ps[m][:, :].rearrange("p (f t) -> p f t", f=2),
                                         ACT.Gelu).then_inc(gelu_ready, 1)

            with act.Fori(0, NEG_E) as q:
                for e in range(EG):
                    n = EG * q + e
                    gelus(n)
                    act.wait_ge(eo_done, at(n + 1))
                    act.wait_ge(eo_sent[e % 2], 16 * BG * (2 * q + e // 2) + 16)
                    nc.scalar.activation(eo[:, e % 2, :, :], e_ps[:, :].rearrange("p (g d) -> p g d", g=B // BG), ACT.Copy)\
                        .then_inc(eo_ready, 1)
            with act.Fori(0, B) as i:
                gelus(i + E)

        @block.vector
        def _(dve):
            opened(dve, xn_ready, lg_ready, xg_xn_ready, pick_ready, gather_dve, back_dve, hT_ready, h_ready)
            ch = Chain(dve, chain)
            nc.vector.memset(zeros[:, :], 0.0)
            norm.stats_dve(dve, ch)
            before, per = ch.n, 1
            with dve.Fori(0, B) as i:
                ch = Chain(dve, chain, before, i, per)
                dve.wait_ge(xt_done, at(i))
                norm.apply_dve(ch, i, lambda s: xn[:, s:s + 1, :]).then_inc(xn_ready, 1)
                dve.wait_ge(lg_done, at(i + 1))
                nc.vector.tensor_copy(sc[:, :, ds(i, 1), :], l_ps[:, 0:TS * E].rearrange("p (s a e) -> p s a e", s=TS, a=1))\
                    .then_inc(lg_ready, 1)
                ch.done(before)
            ch = Chain(dve, chain, before + per * B)
            dve.wait_ge(lg_ready, at(B))
            rows = sc[:, :, :, :].rearrange("p s b e -> p (s b) e")
            wide = lambda t: t[:, :].rearrange("p (n a) -> p n a", a=1).broadcast_to([P, TS * B, E])
            ch.link(nc.vector.tensor_reduce(smax[:, :], rows, AX, ALU.max))
            nc.vector.tensor_tensor(rows, rows, wide(smax), ALU.subtract).then_inc(less_max, 1)
            dve.wait_ge(exp_ready, 1)
            ch.link(nc.vector.tensor_reduce(ssum[:, :], rows, AX, ALU.add))
            ch.link(nc.vector.reciprocal(ssum[:, :], ssum[:, :]))
            nc.vector.tensor_tensor(rows, rows, wide(ssum), ALU.mult).then_inc(sc_ready, 1)
            dve.wait_ge(scT_done, 1)
            ch.link(nc.vector.tensor_copy(work[:, :], l_ps[:, 0:S]))
            for _ in range(CAP // 8):
                ch.link(nc.vector.max(out=top8[:, :], in_=work[:, :]))
                ch.link(nc.vector.match_replace(out=work[:, :], in_to_replace=top8[:, :], in_values=work[:, :], imm_value=-1.0))
            ch.link(nc.vector.tensor_scalar(taken[:, :], work[:, :], 0.0, None, ALU.is_lt))
            ch.link(nc.vector.tensor_tensor_scan(slot[:, :], taken[:, :], zeros[:, :], 0.0, ALU.add, ALU.add))
            nc.vector.tensor_tensor(slot[:, :], slot[:, :], taken[:, :], ALU.mult).then_inc(slot_ready, 1)
            dve.wait_ge(slotT_done, 1)
            ch.link(nc.vector.tensor_copy(slotT[:, :, :, :].rearrange("p s b e -> p s (b e)"),
                                          l_ps[:, 0:S].rearrange("p (s n) -> p s n", s=TS)))
            before = ch.n
            with dve.Fori(0, B) as i:
                ch = Chain(dve, chain, before, i, per)
                dve.wait_ge(gather_done, at(i))
                norm.apply_dve(ch, i, lambda s: xn[:, s:s + 1, :]).then_inc(xg_xn_ready, 1)
                dve.wait_ge(pickw_ready, at(i))
                for s in range(TS):
                    last = nc.vector.tensor_tensor(
                        pick[:, s, :, :], iota[:, :, :].broadcast_to([P, E, CAP]),
                        slotT[:, s, ds(i, 1), :].rearrange("p a e -> p e a").broadcast_to([P, E, CAP]), ALU.is_equal)
                last.then_inc(pick_ready, 1)
                dve.wait_ge(gather_done, at(i + 1))
                nc.vector.tensor_copy(xg[:, 1, :, ds(i, 1), :], g_ps[1][:, :].rearrange("p (e a c) -> p e a c", e=E, a=1))\
                    .then_inc(gather_dve, 1)
                dve.wait_ge(back_done, at(i + 1))
                nc.vector.tensor_copy(back[:, ds(i, 1), 2:4, :], u_ps[1][:, :].rearrange("p (a q t) -> p a q t", a=1, q=2))\
                    .then_inc(back_dve, 1)
                ch.done(before)

            def times_half(n, m):
                dve.wait_ge(gelu_ready, at(2 * n + m + 1))
                nc.vector.tensor_tensor(hT[:, 2 * m:2 * m + 2, :], act_g[:, 2 * m:2 * m + 2, :],
                                        u_ps[m][:, :].rearrange("p (f t) -> p f t", f=2), ALU.mult).then_inc(hT_ready, 1)

            with dve.Fori(0, NEG_E) as q:
                for e in range(EG):
                    n = EG * q + e
                    dve.wait_ge(eo_done, at(n))
                    for m in range(2):
                        times_half(n, m)
            with dve.Fori(0, B) as i:
                dve.wait_ge(eo_done, at(E))
                dve.wait_ge(y_done, at(i))
                for m in range(2):
                    times_half(i + E, m)
                dve.wait_ge(y_done, at(i + 1))
                hs = h[:, ds(TS * i, TS), :]
                nc.vector.tensor_tensor(hs, e_ps[:, :].rearrange("p (s d) -> p s d", s=TS), hs, ALU.add).then_inc(h_ready, 1)

        @block.gpsimd
        def _(pool):
            opened(pool, xall_ready, pickw_ready, backb_ready)
            with pool.Fori(0, B) as i:
                pool.wait_ge(xt_ready, at(i + 1))
                nc.gpsimd.tensor_copy(xT[:, :, ds(S * i, S)], xTb[:, :, :]).then_inc(xall_ready, 1)
            with pool.Fori(0, B) as i:
                pool.wait_ge(pick_ready, at(i + 1))
                pool.wait_ge(back_done, at(i))
                for s in range(TS):
                    last = nc.gpsimd.tensor_tensor(
                        pickw[:, s, :, :], pick[:, s, :, :],
                        sc[:, s, ds(i, 1), :].rearrange("p a e -> p e a").broadcast_to([P, E, CAP]), ALU.mult)
                last.then_inc(pickw_ready, 1)
            with pool.Fori(0, B) as i:
                pool.wait_ge(back_act, at(B))
                pool.wait_ge(back_dve, at(B))
                pool.wait_ge(y_done, at(i))
                nc.gpsimd.tensor_copy(backb[:, :, :], back[:, ds(i, 1), :, :].rearrange("p a q t -> p (a q) t"))\
                    .then_inc(backb_ready, 1)


def attention_experts(nc, dram, h, ident):
    E = 16
    HW = 128
    QKV = 3 * HW
    SCALE = 1.0 / float(np.sqrt(HW))
    NQ = E * TS
    NO = E // 2 * TS
    NY = NQ + NO
    RING = 4
    CUT = [0, 12, 22, NQ]
    WG = 4
    width = [P, S]
    off = [0, P]
    W = P + S
    with Stage(nc, "f3") as st:
        sim = st.sb("sim", [P, KD, E])
        sim2 = st.sb("sim2", [P, KD, E])
        gates = st.sb("gates", [P, 1, E])
        index = st.sb("index", [P, 1, E])
        ones = st.sb("ones", [P, P])
        mask = st.sb("mask", [P, TS, S])
        wqkv = st.sb("wqkv", [P, E, KD, QKV])
        wo = st.sb("wo", [P, E, D])
        xn = st.sb("xn", [P, TS, D])
        xT = st.sb("xT", [P, KD, S])
        square = st.sb("square", [P, D])
        ssq = st.sb("ssq", [P, TS])
        ssq_all = st.sb("ssq_all", [P, TILES])
        norms = st.sb("norms", [P, E])
        rows = [st.sb(f"rows{n}", [P, TILES]) for n in range(4)]
        lg = st.sb("lg", [P, TILES, E])
        e1 = st.sb("e1", [P, TILES, E])
        e2 = st.sb("e2", [P, TILES, E])
        best = st.sb("best", [P, TILES, E])
        rw = st.sb("rw", [P, TILES + PAD, E])
        rw_q = st.sb("rw_q", [P, TS, E])
        rw_o = st.sb("rw_o", [P, TS, E])
        acc = st.sb("acc", [P, TS, QKV])
        v = st.sb("v", [P, TS, HW])
        qkT = st.sb("qkT", [P, 2, S])
        gatew = st.sb("gatew", [P, TS])
        z = st.sb("z", [P, W])
        nmax = st.sb("nmax", [P, TS])
        bias = st.sb("bias", [P, TS])
        pr = st.sb("pr", [P, W])
        psum_of = st.sb("psum_of", [P, TS])
        rsum = st.sb("rsum", [P, TS])
        prT = st.sb("prT", [P, TS, S])
        aoT = st.sb("aoT", [P, S])
        acco = st.sb("acco", [P, TS, D])
        acco2 = st.sb("acco2", [P, TS, D])
        y_ps = [st.ps(f"y{n}") for n in range(RING)]
        t_ps, s_ps, p_ps, a_ps = (st.ps(n) for n in ("t", "s", "p", "a"))
        norm = Norm(nc, st, h)

        w_in, chain = st.sem("w_in"), st.sem("chain")
        wq_in = [st.sem(f"wq{n}_in") for n in range(E // WG)]
        wo_in = st.sem("wo_in")
        gates_ready, sim2_ready, norms_done, norms_var, norms_std, sim_ready = (
            st.sem(n) for n in ("gates_ready", "sim2_ready", "norms_done", "norms_var", "norms_std", "sim_ready"))
        xg_ready, xgt_done, xgt_ready, lg_done, lg_ready = (
            st.sem(n) for n in ("xg_ready", "xgt_done", "xgt_ready", "lg_done", "lg_ready"))
        ssq_ready, len_ready, less_max, exps_ready = (
            st.sem(n) for n in ("ssq_ready", "len_ready", "less_max", "exps_ready"))
        xn_ready, xt_done, xt_ready = st.sem("xn_ready"), st.sem("xt_done"), st.sem("xt_ready")
        y_done, y_used, acc_ready, v_ready, qkt_done, qkt_ready = (
            st.sem(n) for n in ("y_done", "y_used", "acc_ready", "v_ready", "qkt_done", "qkt_ready"))
        sc_done, z_ready, exp_done, pt_done, pt_ready, ao_done, ao_ready = (
            st.sem(n) for n in ("sc_done", "z_ready", "exp_done", "pt_done", "pt_ready", "ao_done", "ao_ready"))
        h_ready = st.sem("h_ready")
        block = st.block()
        NW = 4

        @block.sync
        def _(sp):
            sp.dma_start(sim[:, :, :], dram["f3_sim"].rearrange("(k p) n -> p k n", p=P)).then_inc(w_in, 16)
            sp.dma_start(gates[:, 0, :], dram["f3_gates"].partition_broadcast(P)).then_inc(w_in, 16)
            sp.dma_start(index[:, 0, :], dram["f3_index"].partition_broadcast(P)).then_inc(w_in, 16)
            sp.dma_start(mask[:, :, :], dram["f3_mask"]).then_inc(w_in, 16)
            for n in range(E // WG):
                sp.dma_start(wqkv[:, WG * n:WG * (n + 1), :, :], dram["f3_wqkv"][:, WG * n:WG * (n + 1)]).then_inc(wq_in[n], 16)
            sp.dma_start(wo[:, :, :], dram["f3_wo"]).then_inc(wo_in, 16)

        def unit_qkv(n):
            return n // TS, n % TS

        def unit_out(n):
            return n // (E // 2), n % (E // 2)

        @block.tensor
        def _(pe):
            opened(pe, xgt_done, lg_done, xt_done, y_done, qkt_done, sc_done, pt_done, ao_done)
            pe.wait_ge(sim2_ready, 1)
            for k in range(KD):
                last = nc.tensor.matmul(a_ps[:, 0:E], ones[:, :], sim2[:, k, :], start=(k == 0), stop=(k == KD - 1))
            last.then_inc(norms_done, 1)
            pe.wait_ge(sim_ready, 1)

            def transposes(done):
                for k in range(KD):
                    for s in range(TS):
                        last = nc.tensor.transpose(t_ps[:, k * S + s * P:k * S + (s + 1) * P],
                                                   xn[:, s, k * P:(k + 1) * P], ident[:, :])
                last.then_inc(done, 1)

            with pe.Fori(0, B) as i:
                pe.wait_ge(xg_ready, at(i + 1))
                transposes(xgt_done)
                pe.wait_ge(xgt_ready, at(i + 1))
                pe.wait_ge(lg_ready, at(i))
                for s in range(TS):
                    for k in range(KD):
                        last = nc.tensor.matmul(a_ps[:, s * E:(s + 1) * E], xT[:, k, s * P:(s + 1) * P], sim[:, k, :],
                                                start=(k == 0), stop=(k == KD - 1))
                last.then_inc(lg_done, 1)

            def transpose_x(n):
                pe.wait_ge(xn_ready, at(n + 1))
                transposes(xt_done)

            def products_qkv(b, n0, n1, before):
                for n in range(n0, n1):
                    e, s = unit_qkv(n)
                    if before is None:
                        if n % (TS * WG) == 0:
                            pe.wait_ge(wq_in[e // WG], 16)
                        if n >= RING:
                            pe.wait_ge(y_used, at(n - RING + 1))
                    else:
                        pe.wait_ge(y_used, at(before + n - RING + 1))
                    for k in range(KD):
                        last = nc.tensor.matmul(y_ps[n % RING][:, 0:QKV], xT[:, k, s * P:(s + 1) * P], wqkv[:, e, k, :],
                                                start=(k == 0), stop=(k == KD - 1))
                    last.then_inc(y_done, 1)

            transpose_x(0)
            pe.wait_ge(xt_ready, at(1))
            products_qkv(0, 0, NQ, None)
            transpose_x(1)
            pe.wait_ge(wo_in, 16)
            with pe.Fori(0, B) as i:
                before = NQ + NY * i
                pe.wait_ge(acc_ready, at(i + 1))
                pe.wait_ge(xt_ready, at(i + 2))
                for a in range(2):
                    for s in range(TS):
                        last = nc.tensor.transpose(t_ps[:, a * S + s * P:a * S + (s + 1) * P],
                                                   acc[:, s, a * HW:(a + 1) * HW], ident[:, :])
                last.then_inc(qkt_done, 1)
                products_qkv(i + 1, CUT[0], CUT[1], before)
                pe.wait_ge(qkt_ready, at(i + 1))
                pe.wait_ge(z_ready, at(i))
                for s in range(TS):
                    last = nc.tensor.matmul(s_ps[:, off[s]:off[s] + width[s]], qkT[:, 0, s * P:(s + 1) * P],
                                            qkT[:, 1, 0:width[s]], start=True, stop=True)
                last.then_inc(sc_done, 1)
                products_qkv(i + 1, CUT[1], CUT[2], before)
                pe.wait_ge(exp_done, at(i + 1))
                pe.wait_ge(pt_ready, at(i))
                for s in range(TS):
                    for k in range(width[s] // P):
                        last = nc.tensor.transpose(p_ps[:, k * S + s * P:k * S + (s + 1) * P],
                                                   pr[:, off[s] + k * P:off[s] + (k + 1) * P], ident[:, :])
                last.then_inc(pt_done, 1)
                products_qkv(i + 1, CUT[2], CUT[3], before)
                pe.wait_ge(pt_ready, at(i + 1))
                pe.wait_ge(v_ready, at(i + 1))
                pe.wait_ge(ao_ready, at(i))
                for k in range(TS):
                    last = nc.tensor.matmul(a_ps[:, k * P:S], v[:, k, :], prT[:, k, k * P:S],
                                            start=(k == 0), stop=(k == TS - 1), skip_group_check=True)
                last.then_inc(ao_done, 1)
                transpose_x(i + 2)
                pe.wait_ge(ao_ready, at(i + 1))
                for n in range(NO):
                    s, e = unit_out(n)
                    pe.wait_ge(y_used, at(before + NQ + n - RING + 1))
                    nc.tensor.matmul(y_ps[n % RING][:, :], aoT[:, s * P:(s + 1) * P], wo[:, 2 * e:2 * e + 2, :],
                                     start=True, stop=True).then_inc(y_done, 1)

        @block.scalar
        def _(act):
            opened(act, xgt_ready, xt_ready, v_ready, qkt_ready, exp_done, pt_ready, ao_ready)
            act.wait_ge(w_in, 16 * NW)
            nc.scalar.activation(gates[:, :, :], gates[:, :, :], ACT.Sigmoid).then_inc(gates_ready, 1)
            act.wait_ge(norms_var, 1)
            nc.scalar.activation(norms[:, :], norms[:, :], ACT.Sqrt).then_inc(norms_std, 1)
            norm.sqrt_act(act)
            copy = lambda: nc.scalar.activation(xT[:, :, :], t_ps[:, :].rearrange("p (k t) -> p k t", k=KD), ACT.Copy)
            with act.Fori(0, B) as i:
                act.wait_ge(xgt_done, at(i + 1))
                act.wait_ge(lg_done, at(i))
                copy().then_inc(xgt_ready, 1)
            act.wait_ge(ssq_ready, 1)
            nc.scalar.activation(ssq_all[:, :], ssq_all[:, :], ACT.Sqrt).then_inc(len_ready, 1)
            act.wait_ge(less_max, 1)
            nc.scalar.activation(e1[:, :, :], e1[:, :, :], ACT.Exp).then_inc(exps_ready, 1)
            act.wait_ge(lg_done, at(B))
            for n in range(2):
                act.wait_ge(xt_done, at(n + 1))
                if n == 1:
                    act.wait_ge(y_done, at(NQ))
                copy().then_inc(xt_ready, 1)
            with act.Fori(0, B) as i:
                act.wait_ge(acc_ready, at(i + 1))
                act.wait_ge(ao_done, at(i))
                nc.scalar.activation(v[:, :, :], acc[:, :, 2 * HW:QKV], ACT.Copy).then_inc(v_ready, 1)
                act.wait_ge(qkt_done, at(i + 1))
                nc.scalar.activation(qkT[:, :, :], t_ps[:, :].rearrange("p (a t) -> p a t", a=2), ACT.Copy)\
                    .then_inc(qkt_ready, 1)
                act.wait_ge(z_ready, at(i + 1))
                for s in range(TS):
                    c = slice(off[s], off[s] + width[s])
                    last = nc.scalar.activation(pr[:, c], z[:, c], ACT.Exp, bias=bias[:, s:s + 1], scale=-SCALE,
                                                accum_out=psum_of[:, s:s + 1])
                last.then_inc(exp_done, 1)
                act.wait_ge(pt_done, at(i + 1))
                nc.scalar.activation(prT[:, 0, :], p_ps[:, 0:S], ACT.Copy)
                nc.scalar.activation(prT[:, 1, P:S], p_ps[:, S + P:2 * S], ACT.Copy).then_inc(pt_ready, 1)
                act.wait_ge(ao_done, at(i + 1))
                act.wait_ge(y_done, at(NQ + NY * i + NQ))
                nc.scalar.activation(aoT[:, :], a_ps[:, 0:S], ACT.Copy).then_inc(ao_ready, 1)
                act.wait_ge(xt_done, at(i + 3))
                copy().then_inc(xt_ready, 1)

        @block.vector
        def _(dve):
            opened(dve, xg_ready, lg_ready, xn_ready, y_used, acc_ready, z_ready)
            ch = Chain(dve, chain)
            nc.vector.memset(ones[:, :], 1.0)
            nc.vector.memset(rw[:, TILES:TILES + PAD, :], 0.0)
            dve.wait_ge(w_in, 16 * NW)
            nc.vector.tensor_tensor(sim2[:, :, :], sim[:, :, :], sim[:, :, :], ALU.mult).then_inc(sim2_ready, 1)
            dve.wait_ge(norms_done, 1)
            nc.vector.tensor_scalar(norms[:, :], a_ps[:, 0:E], 1e-12, None, ALU.add).then_inc(norms_var, 1)
            dve.wait_ge(norms_std, 1)
            ch.link(nc.vector.reciprocal(norms[:, :], norms[:, :]))
            nc.vector.tensor_tensor(sim[:, :, :], sim[:, :, :],
                                    norms[:, :].rearrange("p (a e) -> p a e", a=1).broadcast_to([P, KD, E]), ALU.mult)\
                .then_inc(sim_ready, 1)
            norm.stats_dve(dve, ch)
            before, per = ch.n, 3
            with dve.Fori(0, B) as i:
                ch = Chain(dve, chain, before, i, per)
                dve.wait_ge(xgt_done, at(i))
                norm.apply_dve(ch, i, lambda s: xn[:, s:s + 1, :]).then_inc(xg_ready, 1)
                dve.wait_ge(xg_ready, at(i + 1))
                for s in range(TS):
                    last = nc.vector.tensor_tensor_reduce(square[:, :], xn[:, s, :], xn[:, s, :], 1.0, 0.0, ALU.mult, ALU.add,
                                                          ssq[:, s:s + 1])
                    ch.link(last)
                nc.vector.tensor_copy(ssq_all[:, ds(TS * i, TS)], ssq[:, :])
                dve.wait_ge(lg_done, at(i + 1))
                nc.vector.tensor_copy(lg[:, ds(TS * i, TS), :], a_ps[:, 0:TS * E].rearrange("p (s e) -> p s e", s=TS))\
                    .then_inc(lg_ready, 1)
                ch.done(before)
            ch = Chain(dve, chain, before + per * B)
            wide = lambda t: t[:, :].rearrange("p (n a) -> p n a", a=1).broadcast_to([P, TILES, E])
            all_ = lambda t: t[:, 0:TILES, :]
            dve.wait_ge(lg_ready, at(B))
            nc.vector.tensor_scalar(ssq_all[:, :], ssq_all[:, :], 1e-12, None, ALU.add).then_inc(ssq_ready, 1)
            dve.wait_ge(len_ready, 1)
            dve.wait_ge(gates_ready, 1)
            ch.link(nc.vector.reciprocal(ssq_all[:, :], ssq_all[:, :]))
            ch.link(nc.vector.tensor_tensor(all_(lg), all_(lg), wide(ssq_all), ALU.mult))
            ch.link(nc.vector.tensor_tensor(all_(lg), all_(lg), gates[:, :, :].broadcast_to([P, TILES, E]), ALU.subtract))
            top, where, none, high = rows
            ch.link(nc.vector.tensor_reduce(top[:, :], all_(lg), AX, ALU.max))
            ch.link(nc.vector.tensor_scalar(high[:, :], top[:, :], 0.0, None, ALU.max))
            ch.link(nc.vector.tensor_scalar(none[:, :], top[:, :], 0.0, None, ALU.is_le))
            ch.link(nc.vector.tensor_copy(all_(e1), all_(lg)))
            for n in range(2):
                if n == 1:
                    ch.link(nc.vector.scalar_tensor_tensor(all_(e1), all_(best), NEG, all_(e1), ALU.mult, ALU.add))
                    ch.link(nc.vector.tensor_reduce(top[:, :], all_(e1), AX, ALU.max))
                ch.link(nc.vector.tensor_tensor(all_(e2), all_(e1), wide(top), ALU.not_equal))
                ch.link(nc.vector.scalar_tensor_tensor(all_(e2), all_(e2), 64.0, index[:, :, :].broadcast_to([P, TILES, E]),
                                                       ALU.mult, ALU.add))
                ch.link(nc.vector.tensor_reduce(where[:, :], all_(e2), AX, ALU.min))
                ch.link(nc.vector.tensor_tensor(all_(e2), index[:, :, :].broadcast_to([P, TILES, E]), wide(where), ALU.is_equal))
                if n == 0:
                    ch.link(nc.vector.tensor_copy(all_(best), all_(e2)))
                else:
                    ch.link(nc.vector.tensor_tensor(all_(best), all_(best), all_(e2), ALU.add))
            ch.link(nc.vector.tensor_tensor(all_(best), all_(best), wide(none), ALU.mult))
            ch.link(nc.vector.scalar_tensor_tensor(all_(best), all_(lg), 0.0, all_(best), ALU.is_gt, ALU.add))
            nc.vector.scalar_tensor_tensor(all_(e1), all_(lg), 0.0, wide(high), ALU.max, ALU.subtract).then_inc(less_max, 1)
            dve.wait_ge(exps_ready, 1)
            ch.link(nc.vector.tensor_tensor(all_(e1), all_(e1), all_(best), ALU.mult))
            ch.link(nc.vector.tensor_reduce(top[:, :], all_(e1), AX, ALU.add))
            ch.link(nc.vector.reciprocal(top[:, :], top[:, :]))
            ch.link(nc.vector.tensor_tensor(all_(rw), all_(e1), wide(top), ALU.mult))

            def accumulate_qkv(ch, n0, n1, before):
                for n in range(n0, n1):
                    e, s = unit_qkv(n)
                    dve.wait_ge(y_done, at(before + n + 1))
                    y = y_ps[n % RING][:, 0:QKV]
                    if e == 0:
                        last = nc.vector.tensor_scalar(acc[:, s, :], y, rw_q[:, s, e:e + 1], None, ALU.mult)
                    else:
                        dve.wait_ge(y_used, at(before + n - TS + 1))
                        last = nc.vector.scalar_tensor_tensor(acc[:, s, :], y, rw_q[:, s, e:e + 1], acc[:, s, :],
                                                              ALU.mult, ALU.add)
                    last.then_inc(y_used, 1)

            norm.apply_dve(ch, 0, lambda s: xn[:, s:s + 1, :]).then_inc(xn_ready, 1)
            ch.link(nc.vector.tensor_copy(rw_q[:, :, :], rw[:, 0:TS, :]))
            dve.wait_ge(xt_done, at(1))
            norm.apply_dve(ch, 1, lambda s: xn[:, s:s + 1, :]).then_inc(xn_ready, 1)
            accumulate_qkv(ch, 0, NQ, 0)
            dve.wait_ge(y_used, at(NQ))
            ch.link(nc.vector.memset(gatew[:, 0:1], 0.0))
            nc.vector.memset(gatew[:, 1:2], 0.0).then_inc(acc_ready, 1)
            before, per = ch.n, 6
            with dve.Fori(0, B) as i:
                ch = Chain(dve, chain, before, i, per)
                y_before = NQ + NY * i
                ch.link(nc.vector.tensor_copy(rw_o[:, :, :], rw_q[:, :, :]))
                ch.link(nc.vector.tensor_copy(rw_q[:, :, :], rw[:, ds(TS * i + TS, TS), :]))
                dve.wait_ge(v_ready, at(i + 1))
                dve.wait_ge(qkt_done, at(i + 1))
                accumulate_qkv(ch, CUT[0], CUT[1], y_before)
                dve.wait_ge(sc_done, at(i + 1))
                dve.wait_ge(exp_done, at(i))
                nc.vector.memset(gatew[:, 0:1], 0.0)
                for s in range(TS):
                    c = slice(off[s], off[s] + width[s])
                    last = nc.vector.tensor_tensor_reduce(z[:, c], s_ps[:, c], mask[:, s, 0:width[s]], -1.0, BIG,
                                                          ALU.add, ALU.min, nmax[:, s:s + 1])
                ch.link(last)
                nc.vector.tensor_scalar(bias[:, :], nmax[:, :], SCALE, None, ALU.mult).then_inc(z_ready, 1)
                accumulate_qkv(ch, CUT[1], CUT[2], y_before)
                dve.wait_ge(xt_done, at(i + 2))
                norm.apply_dve(ch, i + 2, lambda s: xn[:, s:s + 1, :]).then_inc(xn_ready, 1)
                accumulate_qkv(ch, CUT[2], CUT[3], y_before)
                dve.wait_ge(y_used, at(y_before + NQ))
                nc.vector.memset(gatew[:, 1:2], 0.0).then_inc(acc_ready, 1)
                dve.wait_ge(exp_done, at(i + 1))
                ch.link(nc.vector.reciprocal(rsum[:, :], psum_of[:, :]))
                for n in range(NO):
                    s, e = unit_out(n)
                    dve.wait_ge(y_done, at(y_before + NQ + n + 1))
                    for a in range(2):
                        y = y_ps[n % RING][:, a * D:(a + 1) * D]
                        g = rw_o[:, s, 2 * e + a:2 * e + a + 1]
                        o = acco[:, s, :] if a == 0 else acco2[:, s, :]
                        if e == 0:
                            last = nc.vector.tensor_scalar(o, y, g, None, ALU.mult)
                        else:
                            dve.wait_ge(y_used, at(y_before + NQ + n))
                            last = nc.vector.scalar_tensor_tensor(o, y, g, o, ALU.mult, ALU.add)
                    last.then_inc(y_used, 1)
                dve.wait_ge(y_used, at(y_before + NY))
                ch.link(nc.vector.tensor_tensor(acco[:, :, :], acco[:, :, :], acco2[:, :, :], ALU.add))
                for s in range(TS):
                    hs = h[:, ds(TS * i + s, 1), :]
                    last = nc.vector.scalar_tensor_tensor(hs, acco[:, s:s + 1, :], rsum[:, s:s + 1], hs, ALU.mult, ALU.add)
                last.then_inc(h_ready, 1)
                dve.wait_ge(h_ready, i + 1)
                ch.done(before)


def store_out(nc, out, h):
    with Stage(nc, "store") as st:
        stored = st.sem("stored")
        block = st.block()

        @block.sync
        def _(sp):
            sp.dma_start(out.rearrange("b (s p) d -> p (b s) d", p=P), h[:, 0:TILES, :]).then_inc(stored, 16)
            sp.wait_ge(stored, 16)


STAGE_LIST = [
    lambda nc, dram, h, ident: attention(nc, dram, h, ident, "a0", 0.25, causal=True, kind="add"),
    ternary_mlp,
    lambda nc, dram, h, ident: attention(nc, dram, h, ident, "a1", 0.25),
    channel_mixer,
    lambda nc, dram, h, ident: attention(nc, dram, h, ident, "a2", 0.25, causal=True, kind="add", relative=True),
    expert_choice,
    lambda nc, dram, h, ident: attention(nc, dram, h, ident, "a3", 1.0 / 16.0, kind="mult", latent=True),
    attention_experts,
]


def build(nc, dram, out, stages=9):
    with ExitStack() as ctx:
        h = ctx.enter_context(nc.sbuf_tensor("h", [P, TILES + PAD, D], F32))
        ident = ctx.enter_context(nc.sbuf_tensor("ident_sb", [P, P], F32))
        tok_mixer(nc, dram, h, ident)
        for n, stage in enumerate(STAGE_LIST):
            if n + 2 <= stages:
                stage(nc, dram, h, ident)
        store_out(nc, out, h)


STAGES = 9


def kernel(**inputs):
    import numpy as np
    import concourse.bacc as _bacc
    from concourse import mybir as _mybir
    from concourse.bass_utils import run_bass_kernel_spmd as _run

    c = np.ascontiguousarray
    a = {k: np.asarray(v) for k, v in inputs.items()}
    lay = {}
    lay["ident"] = np.eye(128, dtype=np.float32)
    x = a["x"]
    lay["tok_x"] = np.concatenate([x.transpose(0, 1, 3, 2), np.ones((8, 1, 4, 256), np.float32)], axis=1)
    lay["tok_xflat"] = x.transpose(0, 2, 3, 1).reshape(8, 256, 256)
    lay["tok_wqkv"] = np.concatenate(
        [np.concatenate([a[f"L0_tok_W{n}_w"].T, a[f"L0_tok_W{n}_b"][None]], axis=0) for n in "qkv"], axis=1)
    lay["tok_wbT"] = a["L0_tok_w_bias"].T
    mask = np.zeros((256, 256, 4), np.uint8)
    mask[:, :, 0] = a["L0_tok_local_mask"].T.view(np.uint8)
    lay["tok_maskT"] = mask.view(np.int32)[:, :, 0]
    lay["tok_outw"] = a["L0_tok_out_w"]
    lay["tok_vecs"] = np.stack([a["L0_tok_out_b"], a["L0_tok_ln_g"], a["L0_tok_ln_b"]])

    def heads(w, axis=1):
        w = w.T if axis == 0 else w
        n = w.shape[0]
        out = np.zeros((n, 16, 32), np.float32)
        out[:, :, 0:16] = w.reshape(n, 16, 16)
        out = out.reshape(n, 512)
        return out.T if axis == 0 else out

    ones = np.zeros((16, 32), np.float32)
    ones[:, 16] = 1.0
    sumsel = np.zeros((128, 128), np.float32)
    for j in range(4):
        sumsel[32 * j + 16, 32 * j:32 * j + 32] = 1.0
    lay["sumsel"] = sumsel

    def attn(name, wq, wk, wv, wo, bq, bk, bv, bo):
        lay[name + "_wq"], lay[name + "_wk"], lay[name + "_wv"] = (heads(w) if w.shape[1] == 256 and n else w for n, w in ((1, wq), (name != "a3", wk), (name != "a3", wv)))
        lay[name + "_wo"] = heads(wo, 0)
        col = lambda b: heads(b[None]).reshape(4, 128).T
        lay[name + "_bqk"] = np.stack([col(bq), col(bk)], axis=1)
        v = heads(bv[None]).reshape(16, 32)
        v[:, 16:17] = ones[:, 16:17]
        lay[name + "_bv"] = v.reshape(512)
        lay[name + "_bo"] = bo

    def tiles(m):
        return m.reshape(2, 128, -1).transpose(1, 0, 2)

    i, j = np.arange(256)[:, None], np.arange(256)[None, :]
    fenwick = np.zeros((256, 256), bool)
    for t in range(256):
        fenwick[t, t] = True
        step = 1
        while t - step >= 0:
            fenwick[t, t - step] = True
            step *= 2
    w, bb = a["L0_attn_W_qkv"], a["L0_attn_b_qkv"]
    attn("a0", w[:, 0:256], w[:, 256:512], w[:, 512:768], a["L0_attn_W_proj"], bb[0:256], bb[256:512], bb[512:768], a["L0_attn_b_proj"])
    lay["a0_matrix"] = tiles(np.where(fenwick, 0.0, NEG).astype(np.float32))

    lay["f0_wfcT"] = a["L0_ffn_W_fc"].T
    lay["f0_wprojT"] = a["L0_ffn_W_proj"].T
    lay["f0_lnwb"] = np.stack([a["L0_ffn_ln_w"].reshape(8, 128).T, a["L0_ffn_ln_b"].reshape(8, 128).T], axis=1)
    attn("a1", *(a["L1_attn_W" + n].T for n in "qkvo"), *(a["L1_attn_b" + n] for n in "qkvo"))
    for n in "rkv":
        lay[f"f1_w{n}T"] = a["L1_ffn_W_" + n].T
    lay["f1_mu"] = np.stack([a["L1_ffn_mu_" + n].reshape(2, 128).T for n in "rk"], axis=1)
    attn("a2", *(a["L2_attn_W" + n] for n in "qkvo"), *(a["L2_attn_b" + n] for n in "qkvo"))
    lay["a2_matrix"] = tiles(np.where(j <= i, 0.0, NEG).astype(np.float32))
    relT = np.zeros((4, 32, 256), np.float32)
    relT[:, 0:16, :] = a["L2_attn_rel_key"][256:512].T[None]
    lay["a2_relT"] = relT.reshape(128, 256)
    lay["moe_gateT"] = a["L2_ffn_gate_w"].T
    lay["moe_iota"] = np.arange(1, 33, dtype=np.float32)

    def chunks(w):
        return w.reshape(-1, 128, w.shape[1]).transpose(1, 0, 2).reshape(128, -1)

    def expert(wg, wu, wd):
        return np.concatenate([chunks(wg.T), chunks(wu.T), chunks(wd.T)], axis=1)

    shared = expert(a["L2_ffn_Ws_g"], a["L2_ffn_Ws_u"], a["L2_ffn_Ws_d"])
    lay["moe_experts"] = np.stack([expert(a["L2_ffn_Wg"][e], a["L2_ffn_Wu"][e], a["L2_ffn_Wd"][e]) for e in range(16)]
                                  + [shared, shared])

    z256 = np.zeros(256, np.float32)
    attn("a3", a["L3_attn_W_q"], a["L3_attn_W_k"], a["L3_attn_W_v"], a["L3_attn_W_o"], z256, z256, z256, z256)
    lay["a3_wdown"] = a["L3_attn_W_down_kv"]
    lay["a3_wupk"], lay["a3_wupv"] = heads(a["L3_attn_W_up_k"]), heads(a["L3_attn_W_up_v"])
    lay["a3_matrix"] = tiles(np.exp(np.float32(-0.01) * np.abs(i - j).astype(np.float32)))
    lay["f3_sim"], lay["f3_gates"] = a["L3_ffn_sim_matrix"], a["L3_ffn_gates"]
    lay["f3_index"] = np.arange(16, dtype=np.float32)
    lay["f3_mask"] = lay["a2_matrix"]
    lay["f3_wqkv"] = np.concatenate([a[f"L3_ffn_{n}_proj"] for n in "qkv"], axis=2).reshape(16, 2, 128, 384).transpose(2, 0, 1, 3)
    lay["f3_wo"] = a["L3_ffn_o_proj"].transpose(1, 0, 2)

    nc = _bacc.Bacc("TRN2", target_bir_lowering=False, num_devices=1)
    arrays, dram = {}, {}
    for name, v in lay.items():
        v = c(v)
        arrays[f"in_{name}"] = v
        dram[name] = nc.dram_tensor(f"in_{name}", v.shape, _mybir.dt.from_np(v.dtype), kind="ExternalInput").ap()
    out = nc.dram_tensor("out_0_dram", (8, 256, 256), _mybir.dt.float32, kind="ExternalOutput").ap()
    build(nc, dram, out, STAGES)
    r = _run(nc, [arrays], core_ids=[0])
    return r.results[0]["out_0_dram"]
```

```python
from contextlib import ExitStack

import numpy as np

import concourse.bass as bass
from concourse import mybir

ALU = mybir.AluOpType
ACT = mybir.ActivationFunctionType
AX = mybir.AxisListType.X
F32 = mybir.dt.float32
BF16 = mybir.dt.bfloat16

P = 128
B = 8
S = 256
D = 256
TS = S // P
TILES = B * TS
KD = D // P
HEADS = 16
HD = D // HEADS
HG = 4
NG = HEADS // HG
SUMCOL = HD
PAD = 2 * TS
EPS = 1e-5
BIG = 3.0e38
NEG = -1.0e30
ds = bass.ds


class Chain:

    def __init__(self, eng, sem, before=0, turn=0, per=0):
        self.eng, self.sem, self.n, self.per = eng, sem, before, per
        self.base = turn * per if per else 0

    def link(self, ins):
        self.n += 1
        ins.then_inc(self.sem, 1)
        self.eng.wait_ge(self.sem, self.base + self.n if self.per else self.n)

    def done(self, before):
        assert self.n - before == self.per, (self.n, before, self.per)


class Stage:

    def __init__(self, nc, name):
        self.nc, self.name, self.ctx, self.sems, self.work = nc, name, ExitStack(), [], None

    def __enter__(self):
        self.ctx.__enter__()
        return self

    def __exit__(self, *a):
        if a[0] is not None:
            return self.ctx.__exit__(*a)
        self.work.__exit__(*a)
        with self.nc.Block() as clearing:
            @clearing.sync
            def _(sp):
                for s in self.sems:
                    sp.sem_clear(s)
        return self.ctx.__exit__(*a)

    def sem(self, name):
        self.sems.append(self.ctx.enter_context(self.nc.semaphore(f"{self.name}_{name}")))
        return self.sems[-1]

    def sb(self, name, shape, dt=F32):
        return self.ctx.enter_context(self.nc.sbuf_tensor(f"{self.name}_{name}", shape, dt))

    def ps(self, name, shape=(P, 512)):
        return self.ctx.enter_context(self.nc.psum_tensor(f"{self.name}_{name}_ps", list(shape), F32))

    def block(self):
        self.work = self.nc.Block()
        return self.work.__enter__()


class Norm:

    def __init__(self, nc, st, h):
        self.nc, self.h = nc, h
        self.stats = st.sb("ln_stats", [P, TILES, 6])
        self.mr = st.sb("ln_mean_rstd", [P, TILES + PAD, 2])
        self.std = st.sb("ln_std", [P, TILES])
        self.cur = st.sb("ln_cur", [P, TS, 2])
        self.var_ready = st.sem("ln_var_ready")
        self.std_ready = st.sem("ln_std_ready")

    def stats_dve(self, dve, ch):
        nc = self.nc
        for t in range(TILES):
            last = nc.vector.bn_stats(self.stats[:, t, :], self.h[:, t, :])
        ch.link(last)
        for t in range(TILES):
            last = nc.vector.bn_aggr(self.mr[:, t, :], self.stats[:, t, :])
        nc.vector.memset(self.mr[:, TILES:TILES + PAD, :], 0.0)
        ch.link(nc.vector.memset(self.h[:, TILES:TILES + PAD, :], 0.0))
        nc.vector.tensor_scalar(self.std[:, :], self.mr[:, 0:TILES, 1], EPS, None, ALU.add).then_inc(self.var_ready, 1)
        dve.wait_ge(self.std_ready, 1)
        ch.link(nc.vector.reciprocal(self.mr[:, 0:TILES, 1], self.std[:, :]))

    def sqrt_act(self, act):
        act.wait_ge(self.var_ready, 1)
        self.nc.scalar.activation(self.std[:, :], self.std[:, :], ACT.Sqrt).then_inc(self.std_ready, 1)

    def apply_dve(self, ch, b, dst):
        nc = self.nc
        ch.link(nc.vector.tensor_copy(self.cur[:, :, :], self.mr[:, ds(TS * b, TS), :]))
        for s in range(TS):
            last = nc.vector.tensor_scalar(dst(s), self.h[:, ds(TS * b + s, 1), :], self.cur[:, s, 0:1],
                                           self.cur[:, s, 1:2], ALU.subtract, ALU.mult)
        return last

    STATS_LINKS = 3
    APPLY_LINKS = 1


def tok_mixer(nc, dram, h, ident):
    F, H = 64, 4
    QKV = 3 * F
    with Stage(nc, "tok") as st:
        xa = st.sb("xa", [F + 1, 2, H, S])
        xflat = st.sb("xflat", [P, 2, TS, D])
        wqkv = st.sb("wqkv", [F + 1, QKV])
        ewT = st.sb("ewT", [P, TS, S])
        mask_int = st.sb("mask_int", [P, TS, S], mybir.dt.int32)
        maskf = st.sb("maskf", [P, TS, S])
        outw = st.sb("outw", [P, KD, D])
        vecs = st.sb("vecs", [P, 3, D])
        enq = st.sb("enq", [P, TS, D])
        rhs = st.sb("rhs", [P, TS, 2, D])
        dn = st.sb("dn", [P, TS, D])
        y = st.sb("y", [P, TS, D])
        yT = st.sb("yT", [P, KD, S])
        hp = st.sb("hp", [P, TS, D])
        norm = Norm(nc, st, h)
        proj_ps = [st.ps(f"proj{n}") for n in range(4)]
        mix_ps = [st.ps(f"mix{n}") for n in range(2)]
        t_ps = st.ps("t")
        out_ps = st.ps("out")

        w_in = st.sem("w_in")
        x_in = [st.sem(f"x{o}_in") for o in range(2)]
        xf_in = [st.sem(f"xflat{o}_in") for o in range(2)]
        pre = st.sem("pre")
        ew_ready = st.sem("ew_ready")
        proj_done = st.sem("proj_done")
        proj_read = st.sem("proj_read")
        exps = st.sem("exps")
        rhs_ready = st.sem("rhs_ready")
        mix_done = st.sem("mix_done")
        chain = st.sem("chain")
        y_ready = st.sem("y_ready")
        yt_done = st.sem("yt_done")
        yt_ready = st.sem("yt_ready")
        out_done = st.sem("out_done")
        out_read = st.sem("out_read")
        block = st.block()
        NW = 6

        @block.sync
        def _(sp):
            sp.dma_start(wqkv[:, :], dram["tok_wqkv"]).then_inc(w_in, 16)
            sp.dma_start(ewT[:, :, :], dram["tok_wbT"].rearrange("(k p) t -> p k t", p=P)).then_inc(w_in, 16)
            sp.dma_start(mask_int[:, :, :], dram["tok_maskT"].rearrange("(k p) t -> p k t", p=P)).then_inc(w_in, 16)
            sp.dma_start(outw[:, :, :], dram["tok_outw"].rearrange("(k p) t -> p k t", p=P)).then_inc(w_in, 16)
            sp.dma_start(vecs[:, :, :], dram["tok_vecs"].partition_broadcast(P)).then_inc(w_in, 16)
            sp.dma_start(ident[:, :], dram["ident"]).then_inc(w_in, 16)
            with sp.Fori(0, B // 2) as i:
                for o in range(2):
                    sp.wait_ge(proj_done, 4 * i)
                    sp.dma_start(xa[:, o, :, :], dram["tok_x"][ds(2 * i + o, 1)].rearrange("a c h l -> (a c) h l")).then_inc(x_in[o], 16)
                    sp.wait_ge(out_read, 2 * i)
                    sp.dma_start(xflat[:, o, :, :], dram["tok_xflat"][ds(2 * i + o, 1)].rearrange(
                        "a (s p) d -> p (a s) d", p=P)).then_inc(xf_in[o], 16)

        @block.tensor
        def _(pe):
            pe.wait_ge(w_in, 16 * NW)
            pe.wait_ge(ew_ready, 1)
            with pe.Fori(0, B // 2) as i:
                for o in range(2):
                    b = 2 * i + o
                    pe.wait_ge(x_in[o], 16 * i + 16)
                    pe.wait_ge(proj_read, 2 * b)
                    pe.wait_ge(rhs_ready, 2 * b)
                    for s in range(TS):
                        for hh in range(H):
                            last = nc.tensor.matmul(
                                proj_ps[2 * s + hh // 2][:, (hh % 2) * QKV:(hh % 2 + 1) * QKV],
                                xa[:, o, hh, s * P:(s + 1) * P], wqkv[:, :], start=True, stop=True)
                        last.then_inc(proj_done, 1)
                    pe.wait_ge(rhs_ready, 2 * b + 2)
                    pe.wait_ge(y_ready, b)
                    for t in range(TS):
                        for s in range(TS):
                            last = nc.tensor.matmul(mix_ps[t][:, :], ewT[:, s, t * P:(t + 1) * P],
                                                    rhs[:, s, :, :], start=(s == 0), stop=(s == TS - 1))
                        last.then_inc(mix_done, 1)
                    pe.wait_ge(y_ready, b + 1)
                    pe.wait_ge(yt_ready, b)
                    for k in range(KD):
                        for s in range(TS):
                            last = nc.tensor.transpose(t_ps[:, k * S + s * P:k * S + (s + 1) * P],
                                                       y[:, s, k * P:(k + 1) * P], ident[:, :])
                    last.then_inc(yt_done, 1)
                    pe.wait_ge(yt_ready, b + 1)
                    pe.wait_ge(out_read, b)
                    for s in range(TS):
                        for k in range(KD):
                            last = nc.tensor.matmul(out_ps[:, s * D:(s + 1) * D], yT[:, k, s * P:(s + 1) * P],
                                                    outw[:, k, :], start=(k == 0), stop=(k == KD - 1))
                    last.then_inc(out_done, 1)

        @block.scalar
        def _(act):
            act.wait_ge(w_in, 16 * NW)
            act.wait_ge(pre, 2)
            nc.scalar.activation(ewT[:, :, :], ewT[:, :, :], ACT.Exp).then_inc(ew_ready, 1)
            with act.Fori(0, B // 2) as i:
                for o in range(2):
                    b = 2 * i + o
                    act.wait_ge(mix_done, 2 * b)
                    act.wait_ge(y_ready, b)
                    for s in range(TS):
                        act.wait_ge(proj_done, 2 * b + s + 1)
                        for n in range(2):
                            v = proj_ps[2 * s + n][:, 0:2 * QKV].rearrange("p (a r) -> p a r", a=2)
                            nc.scalar.activation(rhs[:, s, 1, n * 128:(n + 1) * 128].rearrange("p (a r) -> p a r", a=2),
                                                 v[:, :, F:2 * F], ACT.Exp)
                            last = nc.scalar.activation(enq[:, s, n * 128:(n + 1) * 128].rearrange("p (a r) -> p a r", a=2),
                                                        v[:, :, 0:F], ACT.Exp, scale=-1.0)
                        last.then_inc(proj_read, 1)
                    act.wait_ge(yt_done, b + 1)
                    act.wait_ge(out_done, b)
                    nc.scalar.activation(yT[:, :, :], t_ps[:, :].rearrange("p (k t) -> p k t", k=KD),
                                         ACT.Copy).then_inc(yt_ready, 1)
            norm.sqrt_act(act)

        @block.vector
        def _(dve):
            dve.wait_ge(w_in, 16 * NW)
            nc.vector.tensor_copy(maskf[:, :, :], mask_int[:, :, :]).then_inc(pre, 1)
            dve.wait_ge(pre, 1)
            nc.vector.tensor_tensor(ewT[:, :, :], ewT[:, :, :], maskf[:, :, :], ALU.mult).then_inc(pre, 1)
            per = 2 * (2 + 1)
            with dve.Fori(0, B // 2) as i:
                ch = Chain(dve, chain, 0, i, per)
                for o in range(2):
                    b = 2 * i + o
                    dve.wait_ge(mix_done, 2 * b)
                    for s in range(TS):
                        dve.wait_ge(proj_read, 2 * b + s + 1)
                        for n in range(2):
                            v = proj_ps[2 * s + n][:, 0:2 * QKV].rearrange("p (a r) -> p a r", a=2)
                            last = nc.vector.tensor_tensor(
                                rhs[:, s, 0, n * 128:(n + 1) * 128].rearrange("p (a r) -> p a r", a=2),
                                rhs[:, s, 1, n * 128:(n + 1) * 128].rearrange("p (a r) -> p a r", a=2),
                                v[:, :, 2 * F:3 * F], ALU.mult)
                        last.then_inc(rhs_ready, 1)
                    for t in range(TS):
                        dve.wait_ge(mix_done, 2 * b + t + 1)
                        last = nc.vector.scalar_tensor_tensor(dn[:, t, :], enq[:, t, :], 1.0, mix_ps[t][:, D:2 * D],
                                                              ALU.add, ALU.mult)
                    ch.link(last)
                    ch.link(nc.vector.reciprocal(dn[:, :, :], dn[:, :, :]))
                    dve.wait_ge(yt_done, b)
                    for t in range(TS):
                        last = nc.vector.tensor_tensor(y[:, t, :], mix_ps[t][:, 0:D], dn[:, t, :], ALU.mult)
                    last.then_inc(y_ready, 1)
                    dve.wait_ge(xf_in[o], 16 * i + 16)
                    for s in range(TS):
                        last = nc.vector.tensor_tensor(hp[:, s, :], xflat[:, o, s, :], vecs[:, 0, :], ALU.add)
                    ch.link(last)
                    dve.wait_ge(out_done, b + 1)
                    for s in range(TS):
                        last = nc.vector.tensor_tensor(
                            h[:, ds(TS * b + s, 1), :], out_ps[:, s * D:(s + 1) * D].rearrange("p (a d) -> p a d", a=1),
                            hp[:, s:s + 1, :], ALU.add)
                    last.then_inc(out_read, 1)
                ch.done(0)
            ch = Chain(dve, chain, per * (B // 2))
            dve.wait_ge(out_read, B)
            norm.stats_dve(dve, ch)
            for t in range(TILES):
                last = nc.vector.tensor_scalar(h[:, t, :], h[:, t, :], norm.mr[:, t, 0:1], norm.mr[:, t, 1:2],
                                               ALU.subtract, ALU.mult)
            ch.link(last)
            for n, op in ((1, ALU.mult), (2, ALU.add)):
                ch.link(nc.vector.tensor_tensor(h[:, 0:TILES, :], h[:, 0:TILES, :],
                                                vecs[:, n:n + 1, :].broadcast_to([P, TILES, D]), op))


def opened(eng, *sems):
    for s in sems:
        eng.sem_inc(s, 1)


def at(n):
    return n + 1


def attention(nc, dram, h_padded, ident, name, scale, causal=False, kind="plain", latent=False, relative=False):
    h = h_padded[:, TS:, :]
    HU = 2
    NU = HEADS // HU
    NSETS = NU // 2
    width = [P, S] if causal else [S, S]
    off = [0, width[0]]
    W = width[0] + width[1]
    cols = [slice(0, S), slice(S + P, 2 * S)] if causal else [slice(0, 2 * S)]
    projections = [("x", "act")] + ([("kv", "act"), ("lat", "act")] if latent else []) + [("q", "act"), ("k", "dve"), ("v", "dve")]
    steps = projections + [("o0", "dve"), ("o1", "dve"), ("t", "act"), ("y", "dve")]
    NP, NS = len(projections), len(steps)
    slot_of = [k * NU // NS for k in range(NS)]

    def reads(e, k):
        return sum(x == e for _, x in steps[:k])

    BEFORE, AFTER = -1, B

    def done(b, k):
        if isinstance(b, int) and b == BEFORE:
            return at(k + 1)
        skipped = NP if isinstance(b, int) and b == AFTER else 0
        return at(NP + NS * b + k + 1 - skipped)

    def read(b, k, e):
        if isinstance(b, int) and b == BEFORE:
            return at(reads(e, k + 1))
        skipped = reads(e, NP) if isinstance(b, int) and b == AFTER else 0
        return at(reads(e, NP) + reads(e, NS) * b + reads(e, k + 1) - skipped)

    with Stage(nc, name) as st:
        wq = st.sb("wq", [P, KD, D])
        wk = st.sb("wk", [P, KD, D])
        wv = st.sb("wv", [P, KD, D])
        wo = st.sb("wo", [P, KD, D])
        bqk = st.sb("bqk", [P, 2, KD])
        parity = st.sb("parity", [P, 2])
        bv = st.sb("bv", [P, D])
        bo = st.sb("bo", [P, D])
        if kind != "plain":
            matrix = st.sb("matrix", [P, TS, S])
        xn = st.sb("xn", [P, TS, D])
        xT = st.sb("xT", [P, KD, S])
        qT = st.sb("qT", [P, 2, KD, S])
        kT = st.sb("kT", [P, 2, 2, KD, S])
        v = st.sb("v", [P, 2, TS, HEADS, 32])
        if kind != "plain":
            z = st.sb("z", [P, 2, HU, W])
        pr = st.sb("pr", [P, 2, HU, W])
        nmax = st.sb("nmax", [P, 2, HU, TS])
        carry = st.sb("carry", [P, NU])
        prT = st.sb("prT", [P, 2, HU, TS, S])
        oT = st.sb("oT", [P, 2, NSETS, S])
        rs = st.sb("rs", [P, TS, HEADS])
        on = st.sb("on", [P, TS, HEADS, HD])
        onT = st.sb("onT", [P, KD, S])
        sc_ps = st.ps("scores", (P, 2 * HU, 512))
        t_ps = st.ps("t", (P, 2, 512))
        o_ps = st.ps("o")
        m_ps = st.ps("m")
        norm = Norm(nc, st, h)

        w_in, chain, xn_ready, set_up, bias_scaled = (st.sem(n) for n in ("w_in", "chain", "xn_ready", "set_up", "bias_scaled"))
        m_done = st.sem("m_done")
        m_read = {e: st.sem(f"m_read_{e}") for e in ("act", "dve")}
        sc_done, max_ready, exp_done = st.sem("sc_done"), st.sem("max_ready"), st.sem("exp_done")
        t_done, t_read_act, t_read_dve = st.sem("t_done"), st.sem("t_read_act"), st.sem("t_read_dve")
        av_done, o_ready, hb_ready = st.sem("av_done"), st.sem("o_ready"), st.sem("hb_ready")
        if latent:
            wdown = st.sb("wdown", [P, KD, 64])
            wupk = st.sb("wupk", [64, D])
            wupv = st.sb("wupv", [64, D])
            kvT = st.sb("kvT", [P, KD, S])
            latT = st.sb("latT", [64, S])
        if relative:
            relT = st.sb("relT", [P, 2, S])
            rel_out = st.sb("rel_out", [P, NU, HU, W])
            bias = st.sb("bias", [P, NU, HU, W])
            rel_dram = nc.dram_tensor(f"{name}_rel", (NU, HU, TS, P, S), F32).ap()
            rel_done, bias_ready = st.sem("rel_done"), st.sem("bias_ready")
            rel_ready = [st.sem(f"rel_ready_{e}") for e in ("dve", "act")]
            rel_sent = [st.sem(f"rel_sent{u}") for u in range(NU)]
            bias_in = [st.sem(f"bias_in{u}") for u in range(NU)]
        sc_free = exp_done if kind == "plain" else max_ready
        block = st.block()
        loads = [(wq, "wq"), (wo, "wo"), (wk, "wk"), (wv, "wv")] + ([(wdown, "wdown")] if latent else [])
        flat = [(bqk, "bqk"), (parity, "parity")] + ([(wupk, "wupk"), (wupv, "wupv")] if latent else [])
        flat += ([(relT, "relT")] if relative else []) + ([(matrix, "matrix")] if kind != "plain" else [])
        NW = len(loads) + len(flat) + 2

        def rows(u, t, ap, first):
            block_u = rel_dram[u, 0, t]
            return bass.AP(block_u.tensor, block_u.offset + first, ap)

        @block.sync
        def _(sp):
            for t, n in loads:
                sp.dma_start(t[:, :, :], dram[f"{name}_{n}"].rearrange("(k p) n -> p k n", p=P)).then_inc(w_in, 16)
            for t, n in flat:
                a = dram[f"{name}_{n}" if n != "parity" else "parity"]
                sp.dma_start(t[(slice(None),) * len(a.shape)], a).then_inc(w_in, 16)
            sp.dma_start(bv[:, :], dram[f"{name}_bv"].partition_broadcast(P)).then_inc(w_in, 16)
            sp.dma_start(bo[:, :], dram[f"{name}_bo"].partition_broadcast(P)).then_inc(w_in, 16)
            if relative:
                with sp.Fori(0, B + 1) as b:
                    for u in range(NU + 2):
                        if u < NU:
                            sp.wait_ge(rel_ready[u % 2], at(NU // 2 * b + u // 2 + 1))
                            for t, w in enumerate(width):
                                sp.dma_start(rows(u, t, [[w, P], [TS * P * S, HU], [1, w]], 0),
                                             rel_out[:, u, :, off[t]:off[t] + w]).then_inc(rel_sent[u], 16)
                        if u >= 2:
                            r = u - 2
                            if r == 0:
                                sp.wait_ge(max_ready, at(NU * b))
                            sp.wait_ge(rel_sent[r], 16 * TS * (b + 1))
                            for t, w in enumerate(width):
                                sp.dma_start(bias[:, r, :, off[t]:off[t] + w],
                                             rows(r, t, [[w - 1, P], [TS * P * S, HU], [1, w]], P - 1)).then_inc(bias_in[r], 16)

        @block.tensor
        def _(pe):
            opened(pe, m_done, sc_done, t_done, av_done)
            if relative:
                opened(pe, rel_done)
            pe.wait_ge(w_in, 16 * NW)

            def step(b, o, k):
                what = steps[k][0]
                if not (isinstance(b, int) and b == BEFORE and k == 0):
                    pe.wait_ge(m_read[steps[k - 1][1]], read(b, k - 1, steps[k - 1][1]))
                need = {"kv": 0, "lat": 1, "q": 0, "k": 2 if latent else 0, "t": NP + 1, "y": NP + 2}.get(what)
                if need is not None and need != k - 1:
                    pe.wait_ge(m_read[steps[need][1]], read(b, need, steps[need][1]))
                if what == "x":
                    pe.wait_ge(xn_ready, at(b + 2))
                    for c in range(KD):
                        for s in range(TS):
                            last = nc.tensor.transpose(m_ps[:, c * S + s * P:c * S + (s + 1) * P],
                                                       xn[:, s, c * P:(c + 1) * P], ident[:, :])
                elif what == "kv":
                    for m in range(KD):
                        for n, w in enumerate((wk, wv)):
                            for c in range(KD):
                                last = nc.tensor.matmul(m_ps[:, m * S:(m + 1) * S], w[:, c, m * P:(m + 1) * P], xT[:, c, :],
                                                        start=(n + c == 0), stop=(n == 1 and c == KD - 1))
                elif what == "lat":
                    for c in range(KD):
                        last = nc.tensor.matmul(m_ps[0:64, 0:S], wdown[:, c, :], kvT[:, c, :], start=(c == 0), stop=(c == KD - 1))
                elif what == "k" and latent:
                    for m in range(KD):
                        last = nc.tensor.matmul(m_ps[:, m * S:(m + 1) * S], wupk[:, m * P:(m + 1) * P], latT[:, :], start=True, stop=True)
                elif what == "v" and latent:
                    for s in range(TS):
                        last = nc.tensor.matmul(m_ps[:, s * D:(s + 1) * D], latT[:, s * P:(s + 1) * P], wupv[:, :], start=True, stop=True)
                elif what in ("q", "k"):
                    w = wq if what == "q" else wk
                    for m in range(KD):
                        for c in range(KD):
                            last = nc.tensor.matmul(m_ps[:, m * S:(m + 1) * S], w[:, c, m * P:(m + 1) * P], xT[:, c, :],
                                                    start=(c == 0), stop=(c == KD - 1))
                elif what == "v":
                    for s in range(TS):
                        for c in range(KD):
                            last = nc.tensor.matmul(m_ps[:, s * D:(s + 1) * D], xT[:, c, s * P:(s + 1) * P], wv[:, c, :],
                                                    start=(c == 0), stop=(c == KD - 1))
                elif what in ("o0", "o1"):
                    s = int(what[1])
                    pe.wait_ge(o_ready, at(NSETS * b))
                    for g in range(NSETS):
                        last = nc.tensor.transpose(m_ps[:, g * P:(g + 1) * P], oT[:, 1 - o, g, s * P:(s + 1) * P], ident[:, :])
                elif what == "t":
                    for c in range(KD):
                        for s in range(TS):
                            last = nc.tensor.transpose(m_ps[:, c * S + s * P:c * S + (s + 1) * P],
                                                       on[:, s, c * 8:(c + 1) * 8, :].rearrange("p h d -> p (h d)"), ident[:, :])
                else:
                    for s in range(TS):
                        for c in range(KD):
                            last = nc.tensor.matmul(m_ps[:, s * D:(s + 1) * D], onT[:, c, s * P:(s + 1) * P], wo[:, c, :],
                                                    start=(c == 0), stop=(c == KD - 1))
                last.then_inc(m_done, 1)

            def tile(u, j):
                r = HU * (u % 2) + j
                return r, slice(32 * r, 32 * r + 32)

            def scores(b, o, u):
                if u == 0:
                    for n in ("q", "k"):
                        k = [x for x, _ in steps].index(n)
                        pe.wait_ge(m_read[steps[k][1]], read(b - 1, k, steps[k][1]))
                if not (isinstance(b, int) and u < 2):
                    pe.wait_ge(sc_free, at(NU * b + u - 1))
                for s in range(TS):
                    for j in range(HU):
                        r, part = tile(u, j)
                        last = nc.tensor.matmul(sc_ps[:, r, off[s]:off[s] + width[s]],
                                                qT[part, o, u // 4, s * P:(s + 1) * P],
                                                kT[part, o, (u // 2) % 2, u // 4, 0:width[s]], start=True, stop=True)
                last.then_inc(sc_done, 1)

            def rel_products(b, o, u):
                if u < 2:
                    if not isinstance(b, int):
                        pe.wait_ge(max_ready, at(NU * b - 1 + u))
                    pe.wait_ge(m_read["act"], read(b - 1, [x for x, _ in steps].index("q"), "act"))
                else:
                    pe.wait_ge(rel_ready[u % 2], at(NU // 2 * b + u // 2))
                for s in range(TS):
                    for j in range(HU):
                        r, part = tile(u, j)
                        last = nc.tensor.matmul(sc_ps[:, r, off[s]:off[s] + width[s]],
                                                qT[part, o, u // 4, s * P:(s + 1) * P],
                                                relT[part, (u // 2) % 2, S - width[s]:S], start=True, stop=True)
                last.then_inc(rel_done, 1)

            def all_rel_read(b):
                for n in range(2):
                    pe.wait_ge(rel_ready[n], at(NU // 2 * (b + 1)))

            def transpose_weights(b, u):
                n = NU * b + u
                pe.wait_ge(exp_done, at(n + 1))
                pe.wait_ge(t_read_act, at(n))
                pe.wait_ge(t_read_dve, at(n))
                for j in range(HU):
                    for s in range(TS):
                        for k in range(width[s] // P):
                            last = nc.tensor.transpose(t_ps[:, j, k * S + s * P:k * S + (s + 1) * P],
                                                       pr[:, u % 2, j, off[s] + k * P:off[s] + (k + 1) * P], ident[:, :])
                last.then_inc(t_done, 1)

            def values(b, o, u):
                n = NU * b + u
                pe.wait_ge(t_read_act, at(n + 1))
                pe.wait_ge(t_read_dve, at(n + 1))
                if u % 2 == 0:
                    pe.wait_ge(o_ready, at(NSETS * b + u // 2))
                for k in range(TS):
                    for j in range(HU):
                        r, part = tile(u, j)
                        head = 8 * (u // 4) + (u // 2) % 2 + 2 * r
                        q0 = P * k if causal else 0
                        last = nc.tensor.matmul(o_ps[part, q0:S], v[:, o, k, head, :], prT[:, u % 2, j, k, q0:S],
                                                start=(k == 0), stop=(k == TS - 1), skip_group_check=True)
                last.then_inc(av_done, 1)

            for k in range(NP):
                step(BEFORE, 1, k)
            if relative:
                for u in range(NU):
                    rel_products(0, 0, u)
                all_rel_read(0)
            scores(0, 0, 0)
            scores(0, 0, 1)
            with pe.Fori(0, B // 2) as t:
                for o in range(2):
                    b = 2 * t + o
                    for u in range(NU):
                        transpose_weights(b, u)
                        here = [k for k in range(NS) if slot_of[k] == u]
                        for k in here[:1]:
                            step(b, o, k)
                        if u + 2 < NU:
                            scores(b, o, u + 2)
                        elif not relative:
                            scores(b + 1, 1 - o, u + 2 - NU)
                        else:
                            for n in range(NU // 2):
                                rel_products(b + 1, 1 - o, NU // 2 * (u + 2 - NU) + n)
                            if u == NU - 1:
                                all_rel_read(b + 1)
                                scores(b + 1, 1 - o, 0)
                                scores(b + 1, 1 - o, 1)
                        for k in here[1:]:
                            step(b, o, k)
                        if u >= 1:
                            values(b, o, u - 1)
                    values(b, o, NU - 1)
            for k in range(NP, NS):
                step(AFTER, 0, k)

        @block.scalar
        def _(act):
            opened(act, exp_done, t_read_act, o_ready, m_read["act"])
            if relative:
                opened(act, rel_ready[1])
            act.wait_ge(w_in, 16 * NW)
            norm.sqrt_act(act)
            act.wait_ge(bias_scaled, 1)

            def step(b, o, k):
                what = steps[k][0]
                act.wait_ge(m_done, done(b, k))
                both = m_ps[:, :].rearrange("p (k t) -> p k t", k=KD)
                if what == "lat":
                    last = nc.scalar.activation(latT[:, :], m_ps[0:64, 0:S], ACT.Copy)
                elif what == "q":
                    for m in range(KD):
                        last = nc.scalar.activation(qT[:, 1 - o, m, :], m_ps[:, m * S:(m + 1) * S], ACT.Identity,
                                                    bias=bqk[:, 0, m:m + 1], scale=scale)
                else:
                    dst = {"x": xT, "t": onT}.get(what) or kvT
                    last = nc.scalar.activation(dst[:, :, :], both, ACT.Copy)
                last.then_inc(m_read["act"], 1)

            def exps(b, u):
                n = NU * b + u
                act.wait_ge(max_ready, at(n + 1))
                if not (isinstance(b, int) and u < 2):
                    act.wait_ge(t_done, at(n - 1))
                for j in range(HU):
                    for s, w in enumerate(width):
                        c = slice(off[s], off[s] + w)
                        if kind == "plain":
                            src, sgn = sc_ps[:, HU * (u % 2) + j, c], 1.0
                        else:
                            src, sgn = z[:, u % 2, j, c], -1.0 if kind == "add" else 1.0
                        last = nc.scalar.activation(pr[:, u % 2, j, c], src, ACT.Exp, bias=nmax[:, u % 2, j, s:s + 1], scale=sgn)
                last.then_inc(exp_done, 1)

            def copy_weights(b, u):
                n = NU * b + u
                act.wait_ge(t_done, at(n + 1))
                act.wait_ge(av_done, at(NU * b + max(0, u - 1)))
                for c in cols:
                    last = nc.scalar.activation(prT[:, u % 2, 0, :, :].rearrange("p k q -> p (k q)")[:, c], t_ps[:, 0, c], ACT.Copy)
                last.then_inc(t_read_act, 1)

            def copy_o(b, o, g):
                act.wait_ge(av_done, at(NU * b + 2 * g + 2))
                nc.scalar.activation(oT[:, o, g, :], o_ps[:, 0:S], ACT.Copy).then_inc(o_ready, 1)

            def copy_rel(b, u):
                act.wait_ge(rel_done, at(NU * b + u + 1))
                act.wait_ge(bias_ready, at(NU * b))
                nc.scalar.activation(rel_out[:, u, :, :], sc_ps[:, 2:4, 0:W], ACT.Copy).then_inc(rel_ready[1], 1)

            for k in range(NP):
                if steps[k][1] == "act":
                    step(BEFORE, 1, k)
            if relative:
                for u in range(1, NU, 2):
                    copy_rel(0, u)
            exps(0, 0)
            with act.Fori(0, B // 2) as t:
                for o in range(2):
                    b = 2 * t + o
                    for u in range(NU):
                        if relative and u >= NU - 2:
                            if u == NU - 2:
                                exps(b, u + 1)
                            copy_weights(b, u)
                            for n in range(NU // 2):
                                r = NU // 2 * (u + 2 - NU) + n
                                if r % 2 == 1:
                                    copy_rel(b + 1, r)
                            if u == NU - 1:
                                exps(b + 1, 0)
                        else:
                            copy_weights(b, u)
                            exps(b + (u + 1) // NU, (u + 1) % NU)
                        for k in range(NS):
                            if slot_of[k] == u and steps[k][1] == "act":
                                step(b, o, k)
                        if u % 2 == 0 and u >= 2:
                            copy_o(b, o, u // 2 - 1)
                    copy_o(b, o, NSETS - 1)
            for k in range(NP, NS):
                if steps[k][1] == "act":
                    step(AFTER, 0, k)

        @block.vector
        def _(dve):
            opened(dve, xn_ready, max_ready, t_read_dve, m_read["dve"])
            if relative:
                opened(dve, rel_ready[0])
            ch = Chain(dve, chain)
            nc.vector.memset(v[:, :, :, :, :], 0.0)
            nc.vector.memset(oT[:, :, :, :], 1.0)
            ch.link(nc.vector.memset(h_padded[:, 0:TS, :], 0.0))
            ch.link(nc.vector.memset(v[:, :, :, :, HD:HD + 1], 1.0))
            dve.wait_ge(w_in, 16 * NW)
            nc.vector.tensor_scalar(bqk[:, 0, :], bqk[:, 0, :], scale, None, ALU.mult).then_inc(bias_scaled, 1)
            norm.stats_dve(dve, ch)
            norm.apply_dve(ch, 0, lambda s: xn[:, s:s + 1, :]).then_inc(xn_ready, 1)

            def step(ch, b, o, k):
                what = steps[k][0]
                dve.wait_ge(m_done, done(b, k))
                if what == "k":
                    for m in range(KD):
                        for e in range(2):
                            last = nc.vector.tensor_scalar(kT[:, 1 - o, e, m, :], m_ps[:, m * S:(m + 1) * S],
                                                           bqk[:, 1, m:m + 1], parity[:, e:e + 1], ALU.add, ALU.mult)
                elif what == "v":
                    for s in range(TS):
                        last = nc.vector.tensor_tensor(v[:, 1 - o, s, :, 0:HD], m_ps[:, s * D:(s + 1) * D].rearrange("p (h d) -> p h d", d=HD),
                                                       bv[:, :].rearrange("p (h d) -> p h d", d=HD), ALU.add)
                elif what in ("o0", "o1"):
                    s = int(what[1])
                    heads = m_ps[:, :].rearrange("p (h c) -> p h c", c=32)
                    ch.link(nc.vector.reciprocal(rs[:, s, :], heads[:, :, HD]))
                    last = nc.vector.tensor_tensor(on[:, s, :, :], heads[:, :, 0:HD],
                                                   rs[:, s, :].rearrange("p (h a) -> p h a", a=1).broadcast_to([P, HEADS, HD]), ALU.mult)
                else:
                    dve.wait_ge(hb_ready, at(b + 1))
                    hs = h_padded[:, ds(TS * b, TS), :]
                    last = nc.vector.tensor_tensor(hs, m_ps[:, :].rearrange("p (s d) -> p s d", s=TS), hs, ALU.add)
                last.then_inc(m_read["dve"], 1)

            def maxima(ch, b, u):
                n = NU * b + u
                dve.wait_ge(sc_done, at(n + 1))
                if not (isinstance(b, int) and u < 2):
                    dve.wait_ge(exp_done, at(n - 1))
                if relative:
                    dve.wait_ge(bias_ready, at(n + 1))
                if kind == "plain":
                    nc.vector.tensor_reduce(nmax[:, u % 2, :, :], sc_ps[:, HU * (u % 2):HU * (u % 2) + HU, :].rearrange(
                        "p j (s k) -> p j s k", s=TS), AX, ALU.max, negate=True).then_inc(max_ready, 1)
                    return
                nc.vector.memset(carry[:, u:u + 1], 0.0)
                op0, op1, sgn, start = (ALU.add, ALU.min, -1.0, BIG) if kind == "add" else (ALU.mult, ALU.max, 1.0, -BIG)
                for j in range(HU):
                    for s, w in enumerate(width):
                        c = slice(off[s], off[s] + w)
                        m = bias[:, u, j, c] if relative else matrix[:, s, 0:w]
                        last = nc.vector.tensor_tensor_reduce(z[:, u % 2, j, c], sc_ps[:, HU * (u % 2) + j, c], m,
                                                              sgn, start, op0, op1, nmax[:, u % 2, j, s:s + 1])
                if kind == "mult":
                    ch.link(last)
                    last = nc.vector.tensor_scalar(nmax[:, u % 2, :, :], nmax[:, u % 2, :, :], -1.0, None, ALU.mult)
                last.then_inc(max_ready, 1)

            def copy_weights(b, u):
                n = NU * b + u
                dve.wait_ge(t_done, at(n + 1))
                dve.wait_ge(av_done, at(NU * b + max(0, u - 1)))
                for c in cols:
                    last = nc.vector.tensor_copy(prT[:, u % 2, 1, :, :].rearrange("p k q -> p (k q)")[:, c], t_ps[:, 1, c])
                last.then_inc(t_read_dve, 1)

            def copy_rel(b, u):
                dve.wait_ge(rel_done, at(NU * b + u + 1))
                dve.wait_ge(bias_ready, at(NU * b))
                nc.vector.tensor_copy(rel_out[:, u, :, :], sc_ps[:, 0:2, 0:W]).then_inc(rel_ready[0], 1)

            dve.wait_ge(m_done, at(1))
            norm.apply_dve(ch, 1, lambda s: xn[:, s:s + 1, :]).then_inc(xn_ready, 1)
            for k in range(NP):
                if steps[k][1] == "dve":
                    step(ch, BEFORE, 1, k)
            if relative:
                for u in range(0, NU, 2):
                    copy_rel(0, u)
            maxima(ch, 0, 0)
            before = ch.n
            per = 2 * (1 + 2 + (NU if kind == "mult" else 0))
            with dve.Fori(0, B // 2) as t:
                ch = Chain(dve, chain, before, t, per)
                for o in range(2):
                    b = 2 * t + o
                    for u in range(NU):
                        if relative and u >= NU - 2:
                            if u == NU - 2:
                                maxima(ch, b, u + 1)
                            copy_weights(b, u)
                            for n in range(NU // 2):
                                r = NU // 2 * (u + 2 - NU) + n
                                if r % 2 == 0:
                                    copy_rel(b + 1, r)
                            if u == NU - 1:
                                maxima(ch, b + 1, 0)
                        else:
                            maxima(ch, b + (u + 1) // NU, (u + 1) % NU)
                            copy_weights(b, u)
                        for k in range(NS):
                            if slot_of[k] == u and steps[k][1] == "dve":
                                step(ch, b, o, k)
                        if u == 2:
                            dve.wait_ge(m_done, done(b, 0))
                            norm.apply_dve(ch, b + 2, lambda s: xn[:, s:s + 1, :]).then_inc(xn_ready, 1)
                ch.done(before)
            ch = Chain(dve, chain, before + per * (B // 2))
            for k in range(NP, NS):
                if steps[k][1] == "dve":
                    step(ch, AFTER, 0, k)

        @block.gpsimd
        def _(pool):
            opened(pool, hb_ready)
            if relative:
                opened(pool, bias_ready)
            pool.wait_ge(w_in, 16 * NW)

            def add_mask(b):
                for u in range(NU):
                    pool.wait_ge(bias_in[u], 16 * TS * (b + 1))
                    for s, w in enumerate(width):
                        c = slice(off[s], off[s] + w)
                        last = nc.gpsimd.tensor_tensor(bias[:, u, :, c], bias[:, u, :, c],
                                                       matrix[:, s:s + 1, 0:w].broadcast_to([P, HU, w]), ALU.add)
                    last.then_inc(bias_ready, 1)

            with pool.Fori(0, B + 1) as b:
                pool.wait_ge(xn_ready, at(b + 1))
                for s in range(TS):
                    hs = h_padded[:, ds(TS * b + s, 1), :]
                    last = nc.gpsimd.tensor_tensor(hs, hs, bo[:, :].rearrange("p (a d) -> p a d", a=1), ALU.add)
                last.then_inc(hb_ready, 1)
                if relative:
                    add_mask(b)


def ternary_mlp(nc, dram, h, ident):
    FF = 4 * D
    KF = FF // P
    with Stage(nc, "f0") as st:
        wfc = st.sb("wfc", [P, KD, FF])
        wproj = st.sb("wproj", [P, KF, D])
        low = st.sb("low", [P, 2048])
        lnwb = st.sb("lnwb", [P, 2, KF])
        ones = st.sb("ones", [P, P])
        sizes = st.sb("sizes", [P, 2])
        limit = st.sb("limit", [P, 2, 2])
        xn = st.sb("xn", [P, TS, D])
        xT = st.sb("xT", [P, KD, S])
        g = st.sb("g", [P, TILES + PAD, FF])
        gstats = st.sb("gstats", [P, 2, TS, 2, 6])
        gmv = st.sb("gmv", [P, 2, TS, 2])
        gmr = st.sb("gmr", [P, TILES + PAD, 2])
        gstd = st.sb("gstd", [P, TILES])
        gcur = st.sb("gcur", [P, TS, 2])
        gate = st.sb("gate", [P, 1])
        gn = st.sb("gn", [P, TS, FF])
        gT = st.sb("gT", [P, 2, KF, S])
        b_ps = [st.ps(f"b{n}") for n in range(4)]
        t_ps = st.ps("t")
        y_ps = st.ps("y")
        norm = Norm(nc, st, h)

        w_in, chain, sizes_ready, total_done, w_ready = (st.sem(n) for n in ("w_in", "chain", "sizes_ready", "total_done", "w_ready"))
        xn_ready, xt_done, xt_ready, fc_done, g_ready = (st.sem(n) for n in ("xn_ready", "xt_done", "xt_ready", "fc_done", "g_ready"))
        gvar_ready, gstd_ready, stats_read = st.sem("gvar_ready"), st.sem("gstd_ready"), st.sem("stats_read")
        gn_ready, gt_done, gt_act, gt_dve, y_done, h_ready = (
            st.sem(n) for n in ("gn_ready", "gt_done", "gt_act", "gt_dve", "y_done", "h_ready"))
        block = st.block()
        NW = 3

        @block.sync
        def _(sp):
            sp.dma_start(wfc[:, :, :], dram["f0_wfcT"].rearrange("(k p) n -> p k n", p=P)).then_inc(w_in, 16)
            sp.dma_start(wproj[:, :, :], dram["f0_wprojT"].rearrange("(k p) n -> p k n", p=P)).then_inc(w_in, 16)
            sp.dma_start(lnwb[:, :, :], dram["f0_lnwb"]).then_inc(w_in, 16)

        @block.tensor
        def _(pe):
            opened(pe, xt_done, fc_done, gt_done, y_done)
            pe.wait_ge(sizes_ready, 1)
            nc.tensor.matmul(y_ps[:, 0:2], ones[:, :], sizes[:, :], start=True, stop=True).then_inc(total_done, 1)

            def transpose_x(n):
                pe.wait_ge(xn_ready, at(n + 1))
                pe.wait_ge(xt_ready, at(n))
                for k in range(KD):
                    for s in range(TS):
                        last = nc.tensor.transpose(t_ps[:, k * S + s * P:k * S + (s + 1) * P],
                                                   xn[:, s, k * P:(k + 1) * P], ident[:, :])
                last.then_inc(xt_done, 1)

            transpose_x(0)
            pe.wait_ge(w_ready, 1)
            with pe.Fori(0, B) as i:
                pe.wait_ge(xt_ready, at(i + 1))
                for s in range(TS):
                    pe.wait_ge(g_ready, at(TS * i))
                    for n in range(2):
                        for k in range(KD):
                            last = nc.tensor.matmul(b_ps[2 * s + n][:, :], xT[:, k, s * P:(s + 1) * P],
                                                    wfc[:, k, n * 512:(n + 1) * 512], start=(k == 0), stop=(k == KD - 1))
                    last.then_inc(fc_done, 1)
                transpose_x(i + 1)
            pe.wait_ge(g_ready, at(TILES))

            def transpose_g(n, o):
                pe.wait_ge(gn_ready, at(n + 1))
                pe.wait_ge(gt_act, at(n))
                pe.wait_ge(gt_dve, at(n))
                for k in range(KF):
                    for s in range(TS):
                        last = nc.tensor.transpose(b_ps[k // 2][:, (k % 2) * S + s * P:(k % 2) * S + (s + 1) * P],
                                                   gn[:, s, k * P:(k + 1) * P], ident[:, :])
                last.then_inc(gt_done, 1)

            transpose_g(0, 0)
            with pe.Fori(0, B // 2) as i:
                for o in range(2):
                    b = 2 * i + o
                    transpose_g(b + 1, 1 - o)
                    pe.wait_ge(h_ready, at(b))
                    for s in range(TS):
                        for k in range(KF):
                            last = nc.tensor.matmul(y_ps[:, s * D:(s + 1) * D], gT[:, o, k, s * P:(s + 1) * P],
                                                    wproj[:, k, :], start=(k == 0), stop=(k == KF - 1))
                    last.then_inc(y_done, 1)

        @block.scalar
        def _(act):
            opened(act, xt_ready, g_ready, gt_act)
            norm.sqrt_act(act)

            def copy_x(n):
                act.wait_ge(xt_done, at(n + 1))
                act.wait_ge(fc_done, at(TS * n))
                nc.scalar.activation(xT[:, :, :], t_ps[:, :].rearrange("p (k t) -> p k t", k=KD), ACT.Copy)\
                    .then_inc(xt_ready, 1)

            copy_x(0)
            with act.Fori(0, B) as i:
                for s in range(TS):
                    act.wait_ge(fc_done, at(TS * i + s + 1))
                    for n in range(2):
                        last = nc.scalar.activation(g[:, ds(TS * i + s, 1), n * 512:(n + 1) * 512],
                                                    b_ps[2 * s + n][:, :].rearrange("p (a n) -> p a n", a=1), ACT.Gelu)
                    last.then_inc(g_ready, 1)
                copy_x(i + 1)
            act.wait_ge(gvar_ready, 1)
            nc.scalar.activation(gstd[:, :], gstd[:, :], ACT.Sqrt).then_inc(gstd_ready, 1)

            def copy_g(n, o):
                act.wait_ge(gt_done, at(n + 1))
                if not isinstance(n, int):
                    act.wait_ge(y_done, at(n - 1))
                for k in range(KF // 2):
                    last = nc.scalar.activation(gT[:, o, k, :], b_ps[k // 2][:, (k % 2) * S:(k % 2 + 1) * S], ACT.Identity,
                                                bias=lnwb[:, 1, k:k + 1], scale=lnwb[:, 0, k:k + 1])
                last.then_inc(gt_act, 1)

            copy_g(0, 0)
            with act.Fori(0, B // 2) as i:
                for o in range(2):
                    copy_g(2 * i + o + 1, 1 - o)

        @block.vector
        def _(dve):
            opened(dve, xn_ready, gn_ready, gt_dve, h_ready)
            ch = Chain(dve, chain)
            nc.vector.memset(ones[:, :], 1.0)
            nc.vector.memset(g[:, TILES:TILES + PAD, :], 0.0)
            nc.vector.memset(gmr[:, TILES:TILES + PAD, :], 0.0)
            dve.wait_ge(w_in, 16 * NW)
            for n, w in enumerate((wfc, wproj)):
                last = nc.vector.tensor_reduce(sizes[:, n:n + 1], w[:, :, :].rearrange("p k n -> p (k n)"), AX, ALU.add,
                                               apply_absolute_value=True)
            last.then_inc(sizes_ready, 1)
            norm.stats_dve(dve, ch)
            norm.apply_dve(ch, 0, lambda s: xn[:, s:s + 1, :]).then_inc(xn_ready, 1)
            dve.wait_ge(total_done, 1)
            ch.link(nc.vector.tensor_scalar(limit[:, 0, :], y_ps[:, 0:2], 1.0 / (D * FF), 1e-6, ALU.mult, ALU.add))
            ch.link(nc.vector.tensor_scalar(limit[:, 0, :], limit[:, 0, :], 0.5, None, ALU.mult))
            ch.link(nc.vector.tensor_scalar(limit[:, 1, :], limit[:, 0, :], -1.0, None, ALU.mult))
            for n, w in enumerate((wfc, wproj)):
                flat = w[:, :, :].rearrange("p k n -> p (k n)")
                ch.link(nc.vector.tensor_scalar(low[:, :], flat, limit[:, 1, n:n + 1], None, ALU.is_lt))
                last = nc.vector.scalar_tensor_tensor(flat, flat, limit[:, 0, n:n + 1], low[:, :], ALU.is_gt, ALU.subtract)
                if n == 0:
                    ch.link(last)
            last.then_inc(w_ready, 1)
            before = ch.n
            per = 1 + 3
            with dve.Fori(0, B) as i:
                ch = Chain(dve, chain, before, i, per)
                dve.wait_ge(xt_done, at(i + 1))
                norm.apply_dve(ch, i + 1, lambda s: xn[:, s:s + 1, :]).then_inc(xn_ready, 1)
                for s in range(TS):
                    dve.wait_ge(g_ready, at(TS * i + s + 1))
                    for n in range(2):
                        last = nc.vector.bn_stats(gstats[:, 0, s, n, :], g[:, ds(TS * i + s, 1), n * 512:(n + 1) * 512])
                ch.link(last)
                nc.vector.memset(gate[:, :], 0.0)
                for s in range(TS):
                    last = nc.vector.bn_aggr(gmv[:, 0, s, :], gstats[:, 0, s, :, :])
                ch.link(last)
                ch.link(nc.vector.tensor_copy(gmr[:, ds(TS * i, TS), :], gmv[:, 0, :, :]))
                ch.done(before)
            before2 = before + per * B
            ch = Chain(dve, chain, before2)
            nc.vector.tensor_scalar(gstd[:, :], gmr[:, 0:TILES, 1], EPS, None, ALU.add).then_inc(gvar_ready, 1)
            dve.wait_ge(gstd_ready, 1)
            ch.link(nc.vector.reciprocal(gmr[:, 0:TILES, 1], gstd[:, :]))

            def normalize_g(n):
                ch.link(nc.vector.tensor_copy(gcur[:, :, :], gmr[:, ds(TS * n, TS), :]))
                dve.wait_ge(gt_done, at(n))
                for s in range(TS):
                    last = nc.vector.tensor_scalar(gn[:, s:s + 1, :], g[:, ds(TS * n + s, 1), :], gcur[:, s, 0:1],
                                                   gcur[:, s, 1:2], ALU.subtract, ALU.mult)
                last.then_inc(gn_ready, 1)

            def copy_g(n, o):
                dve.wait_ge(gt_done, at(n + 1))
                if not isinstance(n, int):
                    dve.wait_ge(y_done, at(n - 1))
                for k in range(KF // 2, KF):
                    last = nc.vector.tensor_scalar(gT[:, o, k, :], b_ps[k // 2][:, (k % 2) * S:(k % 2 + 1) * S],
                                                   lnwb[:, 0, k:k + 1], lnwb[:, 1, k:k + 1], ALU.mult, ALU.add)
                last.then_inc(gt_dve, 1)

            normalize_g(0)
            copy_g(0, 0)
            normalize_g(1)
            before3 = ch.n
            per = 2
            with dve.Fori(0, B // 2) as i:
                ch = Chain(dve, chain, before3, i, per)
                for o in range(2):
                    b = 2 * i + o
                    copy_g(b + 1, 1 - o)
                    normalize_g(b + 2)
                    dve.wait_ge(y_done, at(b + 1))
                    for s in range(TS):
                        hs = h[:, ds(TS * b + s, 1), :]
                        last = nc.vector.tensor_tensor(hs, y_ps[:, s * D:(s + 1) * D].rearrange("p (a d) -> p a d", a=1),
                                                       hs, ALU.add)
                    last.then_inc(h_ready, 1)
                ch.done(before3)


def channel_mixer(nc, dram, h, ident):
    with Stage(nc, "f1") as st:
        w = st.sb("w", [P, 3, KD, D])
        mu = st.sb("mu", [P, 2, 2, KD])
        xn = st.sb("xn", [P, TS, D])
        xT = st.sb("xT", [P, KD, S + 1])
        part = st.sb("part", [P, 2, KD, S])
        mixed = st.sb("mixed", [P, 2, KD, S])
        r = st.sb("r", [P, TS, D])
        kr = st.sb("kr", [P, KD, S])
        k2 = st.sb("k2", [P, KD, S])
        o = st.sb("o", [P, TS, D])
        t_ps, r_ps, k_ps, v_ps = (st.ps(n) for n in ("t", "r", "k", "v"))
        norm = Norm(nc, st, h)
        w_in, chain, xn_ready, xt_done, xt_ready, mixed_ready = (
            st.sem(n) for n in ("w_in", "chain", "xn_ready", "xt_done", "xt_ready", "mixed_ready"))
        r_done, k_done, r_ready, kr_ready, k2_ready, v_done, o_ready, h_ready = (
            st.sem(n) for n in ("r_done", "k_done", "r_ready", "kr_ready", "k2_ready", "v_done", "o_ready", "h_ready"))
        block = st.block()
        NW = 4

        @block.sync
        def _(sp):
            for n, name in enumerate(("wr", "wk", "wv")):
                sp.dma_start(w[:, n, :, :], dram[f"f1_{name}T"].rearrange("(k p) n -> p k n", p=P)).then_inc(w_in, 16)
            sp.dma_start(mu[:, 0, :, :], dram["f1_mu"]).then_inc(w_in, 16)

        @block.tensor
        def _(pe):
            opened(pe, xt_done, r_done, k_done, v_done)
            pe.wait_ge(w_in, 16 * NW)

            def transpose_x(n):
                pe.wait_ge(xn_ready, at(n + 1))
                pe.wait_ge(xt_ready, at(n))
                for k in range(KD):
                    for s in range(TS):
                        last = nc.tensor.transpose(t_ps[:, k * S + s * P:k * S + (s + 1) * P],
                                                   xn[:, s, k * P:(k + 1) * P], ident[:, :])
                last.then_inc(xt_done, 1)

            transpose_x(0)
            with pe.Fori(0, B) as i:
                transpose_x(i + 1)
                pe.wait_ge(mixed_ready, at(i + 1))
                pe.wait_ge(kr_ready, at(i))
                for m in range(KD):
                    for k in range(KD):
                        last = nc.tensor.matmul(k_ps[:, m * S:(m + 1) * S], w[:, 1, k, m * P:(m + 1) * P],
                                                mixed[:, 1, k, :], start=(k == 0), stop=(k == KD - 1))
                last.then_inc(k_done, 1)
                pe.wait_ge(r_ready, at(i))
                for s in range(TS):
                    for k in range(KD):
                        last = nc.tensor.matmul(r_ps[:, s * D:(s + 1) * D], mixed[:, 0, k, s * P:(s + 1) * P],
                                                w[:, 0, k, :], start=(k == 0), stop=(k == KD - 1))
                last.then_inc(r_done, 1)
                pe.wait_ge(k2_ready, at(i + 1))
                pe.wait_ge(o_ready, at(i))
                for s in range(TS):
                    for k in range(KD):
                        last = nc.tensor.matmul(v_ps[:, s * D:(s + 1) * D], k2[:, k, s * P:(s + 1) * P],
                                                w[:, 2, k, :], start=(k == 0), stop=(k == KD - 1))
                last.then_inc(v_done, 1)

        @block.scalar
        def _(act):
            opened(act, xt_ready, kr_ready, r_ready)
            norm.sqrt_act(act)

            def copy_x(n):
                act.wait_ge(xt_done, at(n + 1))
                act.wait_ge(mixed_ready, at(n))
                nc.scalar.activation(xT[:, :, 1:S + 1], t_ps[:, :].rearrange("p (k t) -> p k t", k=KD), ACT.Copy)\
                    .then_inc(xt_ready, 1)

            copy_x(0)
            with act.Fori(0, B) as i:
                copy_x(i + 1)
                act.wait_ge(k_done, at(i + 1))
                act.wait_ge(k2_ready, at(i))
                nc.scalar.activation(kr[:, :, :], k_ps[:, :].rearrange("p (k t) -> p k t", k=KD), ACT.Relu)\
                    .then_inc(kr_ready, 1)
                act.wait_ge(r_done, at(i + 1))
                act.wait_ge(o_ready, at(i))
                nc.scalar.activation(r[:, :, :], r_ps[:, :].rearrange("p (s d) -> p s d", s=TS), ACT.Sigmoid)\
                    .then_inc(r_ready, 1)

        @block.vector
        def _(dve):
            opened(dve, xn_ready, mixed_ready, o_ready)
            ch = Chain(dve, chain)
            nc.vector.memset(xT[:, :, 0:1], 0.0)
            dve.wait_ge(w_in, 16 * NW)
            ch.link(nc.vector.tensor_scalar(mu[:, 1, :, :], mu[:, 0, :, :], -1.0, 1.0, ALU.mult, ALU.add))
            norm.stats_dve(dve, ch)
            norm.apply_dve(ch, 0, lambda s: xn[:, s:s + 1, :]).then_inc(xn_ready, 1)

            def mix(n):
                dve.wait_ge(xt_ready, at(n + 1))
                for m in range(2):
                    for k in range(KD):
                        last = nc.vector.tensor_scalar(part[:, m, k, :], xT[:, k, 0:S], mu[:, 1, m, k:k + 1], None, ALU.mult)
                ch.link(last)
                dve.wait_ge(r_done, at(n))
                for m in range(2):
                    for k in range(KD):
                        last = nc.vector.scalar_tensor_tensor(mixed[:, m, k, :], xT[:, k, 1:S + 1], mu[:, 0, m, k:k + 1],
                                                              part[:, m, k, :], ALU.mult, ALU.add)
                last.then_inc(mixed_ready, 1)

            def next_x(n):
                dve.wait_ge(xt_done, at(n))
                norm.apply_dve(ch, n, lambda s: xn[:, s:s + 1, :]).then_inc(xn_ready, 1)

            dve.wait_ge(xt_done, at(1))
            norm.apply_dve(ch, 1, lambda s: xn[:, s:s + 1, :]).then_inc(xn_ready, 1)
            mix(0)
            before = ch.n
            per = 2
            with dve.Fori(0, B) as i:
                ch = Chain(dve, chain, before, i, per)
                next_x(i + 2)
                mix(i + 1)
                dve.wait_ge(v_done, at(i + 1))
                dve.wait_ge(r_ready, at(i + 1))
                dve.wait_ge(h_ready, at(i))
                nc.vector.tensor_tensor(o[:, :, :], v_ps[:, :].rearrange("p (s d) -> p s d", s=TS), r[:, :, :], ALU.mult)\
                    .then_inc(o_ready, 1)
                ch.done(before)

        @block.gpsimd
        def _(pool):
            opened(pool, k2_ready, h_ready)
            with pool.Fori(0, B) as i:
                pool.wait_ge(kr_ready, at(i + 1))
                pool.wait_ge(v_done, at(i))
                nc.gpsimd.tensor_tensor(k2[:, :, :], kr[:, :, :], kr[:, :, :], ALU.mult).then_inc(k2_ready, 1)
                pool.wait_ge(o_ready, at(i + 1))
                hs = h[:, ds(TS * i, TS), :]
                nc.gpsimd.tensor_tensor(hs, hs, o[:, :, :], ALU.add).then_inc(h_ready, 1)


def expert_choice(nc, dram, h, ident):
    E = 16
    CAP = int(S * 2.0 / E)
    FF = 512
    KF = FF // P
    EG = P // CAP
    NEG_E = E // EG
    BG = P // CAP
    SLOTS = B * CAP
    with Stage(nc, "moe") as st:
        gate = st.sb("gate", [P, KD, E])
        iota = st.sb("iota", [P, 1, CAP])
        xn = st.sb("xn", [P, TS, D])
        xTb = st.sb("xTb", [P, KD, S])
        xT = st.sb("xT", [P, KD, B * S])
        sc = st.sb("sc", [P, TS, B, E])
        smax = st.sb("smax", [P, TS * B])
        ssum = st.sb("ssum", [P, TS * B])
        work = st.sb("work", [P, S])
        top8 = st.sb("top8", [P, 8])
        taken = st.sb("taken", [P, S])
        zeros = st.sb("zeros", [P, S])
        slot = st.sb("slot", [P, S])
        slotT = st.sb("slotT", [P, TS, B, E])
        pick = st.sb("pick", [P, TS, E, CAP])
        pickw = st.sb("pickw", [P, TS, E, CAP])
        xg = st.sb("xg", [P, KD, E, B, CAP])
        back = st.sb("back", [P, B, NEG_E, S])
        backb = st.sb("backb", [P, NEG_E, S])
        wx = [st.sb(f"wx{n}", [P, 2 * KD * FF + KF * D]) for n in range(2)]
        act_g = st.sb("act_g", [P, KF, S])
        hT = st.sb("hT", [P, KF, S])
        eo = st.sb("eo", [P, 2, B // BG, D])
        eo2 = st.sb("eo2", [P, NEG_E, B, D])
        g_ps = [st.ps(f"g{n}") for n in range(2)]
        u_ps = [st.ps(f"u{n}") for n in range(2)]
        e_ps = st.ps("e")
        t_ps = st.ps("t")
        l_ps = st.ps("l")
        norm = Norm(nc, st, h)

        w_in, chain, xn_ready, xt_done, xt_ready, xall_ready, lg_done, lg_ready = (
            st.sem(n) for n in ("w_in", "chain", "xn_ready", "xt_done", "xt_ready", "xall_ready", "lg_done", "lg_ready"))
        less_max, exp_ready, sc_ready, scT_done, slot_ready, slotT_done = (
            st.sem(n) for n in ("less_max", "exp_ready", "sc_ready", "scT_done", "slot_ready", "slotT_done"))
        xg_xn_ready, pick_ready, pickw_ready, gather_done, gather_act, gather_dve, back_done, back_act, back_dve = (
            st.sem(n) for n in ("xg_xn_ready", "pick_ready", "pickw_ready", "gather_done", "gather_act", "gather_dve",
                                "back_done", "back_act", "back_dve"))
        gu_done, gelu_ready, hT_ready, eo_done, eo_ready = (
            st.sem(n) for n in ("gu_done", "gelu_ready", "hT_ready", "eo_done", "eo_ready"))
        wx_in = [st.sem(f"wx{n}_in") for n in range(2)]
        eo_sent = [st.sem(f"eo_sent{n}") for n in range(2)]
        backb_ready, y_done, h_ready = st.sem("backb_ready"), st.sem("y_done"), st.sem("h_ready")
        block = st.block()
        NW = 2

        def weights(n):
            a = KD * FF
            return (wx[n][:, 0:a].rearrange("p (k f) -> p k f", k=KD), wx[n][:, a:2 * a].rearrange("p (k f) -> p k f", k=KD),
                    wx[n][:, 2 * a:].rearrange("p (k d) -> p k d", k=KF))

        @block.sync
        def _(sp):
            sp.dma_start(gate[:, :, :], dram["moe_gateT"].rearrange("(k p) n -> p k n", p=P)).then_inc(w_in, 16)
            sp.dma_start(iota[:, 0, :], dram["moe_iota"].partition_broadcast(P)).then_inc(w_in, 16)
            for e in range(2):
                sp.dma_start(wx[e][:, :], dram["moe_experts"][e]).then_inc(wx_in[e], 16)
            for s in eo_sent:
                sp.sem_inc(s, 16)
            with sp.Fori(0, NEG_E) as q:
                for e in range(EG):
                    sp.wait_ge(eo_ready, at(EG * q + e + 1))
                    for b in range(BG):
                        sp.dma_start(eo2[CAP * e:CAP * (e + 1), ds(q, 1), b:B:BG, :],
                                     eo[CAP * b:CAP * (b + 1), e % 2, :, :].rearrange("p (a b) d -> p a b d", a=1))\
                            .then_inc(eo_sent[e % 2], 16)
                    sp.dma_start(wx[e % 2][:, :], dram["moe_experts"][ds(EG * q + e + 2, 1)].rearrange("a p n -> (a p) n"))\
                        .then_inc(wx_in[e % 2], 16)

        @block.tensor
        def _(pe):
            opened(pe, xt_done, lg_done, gather_done, back_done, gu_done, eo_done, y_done)
            pe.wait_ge(w_in, 16 * NW)
            with pe.Fori(0, B) as i:
                pe.wait_ge(xn_ready, at(i + 1))
                for k in range(KD):
                    for s in range(TS):
                        last = nc.tensor.transpose(t_ps[:, k * S + s * P:k * S + (s + 1) * P],
                                                   xn[:, s, k * P:(k + 1) * P], ident[:, :])
                last.then_inc(xt_done, 1)
                pe.wait_ge(xt_ready, at(i + 1))
                pe.wait_ge(lg_ready, at(i))
                for s in range(TS):
                    for k in range(KD):
                        last = nc.tensor.matmul(l_ps[:, s * E:(s + 1) * E], xTb[:, k, s * P:(s + 1) * P], gate[:, k, :],
                                                start=(k == 0), stop=(k == KD - 1))
                last.then_inc(lg_done, 1)
            pe.wait_ge(sc_ready, 1)
            for s in range(TS):
                last = nc.tensor.transpose(l_ps[:, s * P:(s + 1) * P], sc[:, s, :, :].rearrange("p b e -> p (b e)"), ident[:, :])
            last.then_inc(scT_done, 1)
            pe.wait_ge(slot_ready, 1)
            for s in range(TS):
                last = nc.tensor.transpose(l_ps[:, s * P:(s + 1) * P], slot[:, s * P:(s + 1) * P], ident[:, :])
            last.then_inc(slotT_done, 1)
            with pe.Fori(0, B) as i:
                pe.wait_ge(xg_xn_ready, at(i + 1))
                pe.wait_ge(pick_ready, at(i + 1))
                pe.wait_ge(gather_act, at(i))
                pe.wait_ge(gather_dve, at(i))
                for k in range(KD):
                    for s in range(TS):
                        last = nc.tensor.matmul(g_ps[k][:, :], xn[:, s, k * P:(k + 1) * P],
                                                pick[:, s, :, :].rearrange("p e c -> p (e c)"),
                                                start=(s == 0), stop=(s == TS - 1))
                last.then_inc(gather_done, 1)
                pe.wait_ge(pickw_ready, at(i + 1))
                pe.wait_ge(back_act, at(i))
                pe.wait_ge(back_dve, at(i))
                for q in range(NEG_E):
                    for s in range(TS):
                        last = nc.tensor.transpose(
                            u_ps[q // 2][:, (q % 2) * S + s * P:(q % 2) * S + (s + 1) * P],
                            pickw[:, s, EG * q:EG * (q + 1), :].rearrange("p e c -> p (e c)"), ident[:, :])
                last.then_inc(back_done, 1)

            def gate_up(w, x, n):
                for m in range(2):
                    pe.wait_ge(gelu_ready, at(2 * n))
                    pe.wait_ge(hT_ready, at(2 * n))
                    for ps, wn in ((g_ps[m], w[0]), (u_ps[m], w[1])):
                        for f in range(2):
                            for k in range(KD):
                                c = (2 * m + f) * P
                                last = nc.tensor.matmul(ps[:, f * S:(f + 1) * S], wn[:, k, c:c + P], x(k),
                                                        start=(k == 0), stop=(k == KD - 1))
                    last.then_inc(gu_done, 1)

            pe.wait_ge(gather_act, at(B))
            pe.wait_ge(gather_dve, at(B))
            pe.wait_ge(back_act, at(B))
            pe.wait_ge(back_dve, at(B))
            with pe.Fori(0, NEG_E) as q:
                for e in range(EG):
                    n = EG * q + e
                    w = weights(e % 2)
                    pe.wait_ge(wx_in[e % 2], 32 * q + 16 * (e // 2) + 16)
                    gate_up(w, lambda k: xg[:, k, ds(n, 1), :, :].rearrange("p a b c -> p (a b c)"), n)
                    pe.wait_ge(hT_ready, at(2 * n + 2))
                    pe.wait_ge(eo_ready, at(n))
                    for g in range(B // BG):
                        for k in range(KF):
                            last = nc.tensor.matmul(e_ps[:, g * D:(g + 1) * D], hT[:, k, g * P:(g + 1) * P], w[2][:, k, :],
                                                    start=(k == 0), stop=(k == KF - 1))
                    last.then_inc(eo_done, 1)
            w = weights(0)
            pe.wait_ge(wx_in[0], 16 * (E // 2 + 1))
            pe.wait_ge(wx_in[1], 16 * (E // 2 + 1))
            pe.wait_ge(eo_ready, at(E))
            for o in range(2):
                pe.wait_ge(eo_sent[o], 16 * BG * E // 2 + 16)
            with pe.Fori(0, B) as i:
                gate_up(w, lambda k: xT[:, k, ds(S * i, S)], i + E)
                pe.wait_ge(hT_ready, at(2 * (i + E) + 2))
                pe.wait_ge(backb_ready, at(i + 1))
                pe.wait_ge(h_ready, at(i))
                for s in range(TS):
                    for k in range(KF):
                        nc.tensor.matmul(e_ps[:, s * D:(s + 1) * D], hT[:, k, s * P:(s + 1) * P], w[2][:, k, :],
                                         start=(k == 0), stop=False)
                    for q in range(NEG_E):
                        last = nc.tensor.matmul(e_ps[:, s * D:(s + 1) * D], backb[:, q, s * P:(s + 1) * P],
                                                eo2[:, q, ds(i, 1), :].rearrange("p a d -> p (a d)"),
                                                start=False, stop=(q == NEG_E - 1))
                last.then_inc(y_done, 1)

        @block.scalar
        def _(act):
            opened(act, xt_ready, gather_act, back_act, gelu_ready, eo_ready)
            norm.sqrt_act(act)
            with act.Fori(0, B) as i:
                act.wait_ge(xt_done, at(i + 1))
                act.wait_ge(xall_ready, at(i))
                act.wait_ge(lg_done, at(i))
                nc.scalar.activation(xTb[:, :, :], t_ps[:, :].rearrange("p (k t) -> p k t", k=KD), ACT.Copy)\
                    .then_inc(xt_ready, 1)
            act.wait_ge(less_max, 1)
            nc.scalar.activation(sc[:, :, :, :], sc[:, :, :, :], ACT.Exp).then_inc(exp_ready, 1)
            with act.Fori(0, B) as i:
                act.wait_ge(gather_done, at(i + 1))
                nc.scalar.activation(xg[:, 0, :, ds(i, 1), :], g_ps[0][:, :].rearrange("p (e a c) -> p e a c", e=E, a=1),
                                     ACT.Copy).then_inc(gather_act, 1)
                act.wait_ge(back_done, at(i + 1))
                nc.scalar.activation(back[:, ds(i, 1), 0:2, :], u_ps[0][:, :].rearrange("p (a q t) -> p a q t", a=1, q=2),
                                     ACT.Copy).then_inc(back_act, 1)

            def gelus(n):
                for m in range(2):
                    act.wait_ge(gu_done, at(2 * n + m + 1))
                    act.wait_ge(hT_ready, at(2 * n))
                    nc.scalar.activation(act_g[:, 2 * m:2 * m + 2, :], g_ps[m][:, :].rearrange("p (f t) -> p f t", f=2),
                                         ACT.Gelu).then_inc(gelu_ready, 1)

            with act.Fori(0, NEG_E) as q:
                for e in range(EG):
                    n = EG * q + e
                    gelus(n)
                    act.wait_ge(eo_done, at(n + 1))
                    act.wait_ge(eo_sent[e % 2], 16 * BG * (2 * q + e // 2) + 16)
                    nc.scalar.activation(eo[:, e % 2, :, :], e_ps[:, :].rearrange("p (g d) -> p g d", g=B // BG), ACT.Copy)\
                        .then_inc(eo_ready, 1)
            with act.Fori(0, B) as i:
                gelus(i + E)

        @block.vector
        def _(dve):
            opened(dve, xn_ready, lg_ready, xg_xn_ready, pick_ready, gather_dve, back_dve, hT_ready, h_ready)
            ch = Chain(dve, chain)
            nc.vector.memset(zeros[:, :], 0.0)
            norm.stats_dve(dve, ch)
            before, per = ch.n, 1
            with dve.Fori(0, B) as i:
                ch = Chain(dve, chain, before, i, per)
                dve.wait_ge(xt_done, at(i))
                norm.apply_dve(ch, i, lambda s: xn[:, s:s + 1, :]).then_inc(xn_ready, 1)
                dve.wait_ge(lg_done, at(i + 1))
                nc.vector.tensor_copy(sc[:, :, ds(i, 1), :], l_ps[:, 0:TS * E].rearrange("p (s a e) -> p s a e", s=TS, a=1))\
                    .then_inc(lg_ready, 1)
                ch.done(before)
            ch = Chain(dve, chain, before + per * B)
            dve.wait_ge(lg_ready, at(B))
            rows = sc[:, :, :, :].rearrange("p s b e -> p (s b) e")
            wide = lambda t: t[:, :].rearrange("p (n a) -> p n a", a=1).broadcast_to([P, TS * B, E])
            ch.link(nc.vector.tensor_reduce(smax[:, :], rows, AX, ALU.max))
            nc.vector.tensor_tensor(rows, rows, wide(smax), ALU.subtract).then_inc(less_max, 1)
            dve.wait_ge(exp_ready, 1)
            ch.link(nc.vector.tensor_reduce(ssum[:, :], rows, AX, ALU.add))
            ch.link(nc.vector.reciprocal(ssum[:, :], ssum[:, :]))
            nc.vector.tensor_tensor(rows, rows, wide(ssum), ALU.mult).then_inc(sc_ready, 1)
            dve.wait_ge(scT_done, 1)
            ch.link(nc.vector.tensor_copy(work[:, :], l_ps[:, 0:S]))
            for _ in range(CAP // 8):
                ch.link(nc.vector.max(out=top8[:, :], in_=work[:, :]))
                ch.link(nc.vector.match_replace(out=work[:, :], in_to_replace=top8[:, :], in_values=work[:, :], imm_value=-1.0))
            ch.link(nc.vector.tensor_scalar(taken[:, :], work[:, :], 0.0, None, ALU.is_lt))
            ch.link(nc.vector.tensor_tensor_scan(slot[:, :], taken[:, :], zeros[:, :], 0.0, ALU.add, ALU.add))
            nc.vector.tensor_tensor(slot[:, :], slot[:, :], taken[:, :], ALU.mult).then_inc(slot_ready, 1)
            dve.wait_ge(slotT_done, 1)
            ch.link(nc.vector.tensor_copy(slotT[:, :, :, :].rearrange("p s b e -> p s (b e)"),
                                          l_ps[:, 0:S].rearrange("p (s n) -> p s n", s=TS)))
            before = ch.n
            with dve.Fori(0, B) as i:
                ch = Chain(dve, chain, before, i, per)
                dve.wait_ge(gather_done, at(i))
                norm.apply_dve(ch, i, lambda s: xn[:, s:s + 1, :]).then_inc(xg_xn_ready, 1)
                dve.wait_ge(pickw_ready, at(i))
                for s in range(TS):
                    last = nc.vector.tensor_tensor(
                        pick[:, s, :, :], iota[:, :, :].broadcast_to([P, E, CAP]),
                        slotT[:, s, ds(i, 1), :].rearrange("p a e -> p e a").broadcast_to([P, E, CAP]), ALU.is_equal)
                last.then_inc(pick_ready, 1)
                dve.wait_ge(gather_done, at(i + 1))
                nc.vector.tensor_copy(xg[:, 1, :, ds(i, 1), :], g_ps[1][:, :].rearrange("p (e a c) -> p e a c", e=E, a=1))\
                    .then_inc(gather_dve, 1)
                dve.wait_ge(back_done, at(i + 1))
                nc.vector.tensor_copy(back[:, ds(i, 1), 2:4, :], u_ps[1][:, :].rearrange("p (a q t) -> p a q t", a=1, q=2))\
                    .then_inc(back_dve, 1)
                ch.done(before)

            def times_half(n, m):
                dve.wait_ge(gelu_ready, at(2 * n + m + 1))
                nc.vector.tensor_tensor(hT[:, 2 * m:2 * m + 2, :], act_g[:, 2 * m:2 * m + 2, :],
                                        u_ps[m][:, :].rearrange("p (f t) -> p f t", f=2), ALU.mult).then_inc(hT_ready, 1)

            with dve.Fori(0, NEG_E) as q:
                for e in range(EG):
                    n = EG * q + e
                    dve.wait_ge(eo_done, at(n))
                    for m in range(2):
                        times_half(n, m)
            with dve.Fori(0, B) as i:
                dve.wait_ge(eo_done, at(E))
                dve.wait_ge(y_done, at(i))
                for m in range(2):
                    times_half(i + E, m)
                dve.wait_ge(y_done, at(i + 1))
                hs = h[:, ds(TS * i, TS), :]
                nc.vector.tensor_tensor(hs, e_ps[:, :].rearrange("p (s d) -> p s d", s=TS), hs, ALU.add).then_inc(h_ready, 1)

        @block.gpsimd
        def _(pool):
            opened(pool, xall_ready, pickw_ready, backb_ready)
            with pool.Fori(0, B) as i:
                pool.wait_ge(xt_ready, at(i + 1))
                nc.gpsimd.tensor_copy(xT[:, :, ds(S * i, S)], xTb[:, :, :]).then_inc(xall_ready, 1)
            with pool.Fori(0, B) as i:
                pool.wait_ge(pick_ready, at(i + 1))
                pool.wait_ge(back_done, at(i))
                for s in range(TS):
                    last = nc.gpsimd.tensor_tensor(
                        pickw[:, s, :, :], pick[:, s, :, :],
                        sc[:, s, ds(i, 1), :].rearrange("p a e -> p e a").broadcast_to([P, E, CAP]), ALU.mult)
                last.then_inc(pickw_ready, 1)
            with pool.Fori(0, B) as i:
                pool.wait_ge(back_act, at(B))
                pool.wait_ge(back_dve, at(B))
                pool.wait_ge(y_done, at(i))
                nc.gpsimd.tensor_copy(backb[:, :, :], back[:, ds(i, 1), :, :].rearrange("p a q t -> p (a q) t"))\
                    .then_inc(backb_ready, 1)


def attention_experts(nc, dram, h, ident):
    E = 16
    HW = 128
    QKV = 3 * HW
    SCALE = 1.0 / float(np.sqrt(HW))
    NQ = E * TS
    NO = E // 2 * TS
    NY = NQ + NO
    RING = 4
    CUT = [0, 12, 22, NQ]
    WG = 4
    width = [P, S]
    off = [0, P]
    W = P + S
    with Stage(nc, "f3") as st:
        sim = st.sb("sim", [P, KD, E])
        sim2 = st.sb("sim2", [P, KD, E])
        gates = st.sb("gates", [P, 1, E])
        index = st.sb("index", [P, 1, E])
        ones = st.sb("ones", [P, P])
        mask = st.sb("mask", [P, TS, S])
        wqkv = st.sb("wqkv", [P, E, KD, QKV])
        wo = st.sb("wo", [P, E, D])
        xn = st.sb("xn", [P, TS, D])
        xT = st.sb("xT", [P, KD, S])
        square = st.sb("square", [P, D])
        ssq = st.sb("ssq", [P, TS])
        ssq_all = st.sb("ssq_all", [P, TILES])
        norms = st.sb("norms", [P, E])
        rows = [st.sb(f"rows{n}", [P, TILES]) for n in range(4)]
        lg = st.sb("lg", [P, TILES, E])
        e1 = st.sb("e1", [P, TILES, E])
        e2 = st.sb("e2", [P, TILES, E])
        best = st.sb("best", [P, TILES, E])
        rw = st.sb("rw", [P, TILES + PAD, E])
        rw_q = st.sb("rw_q", [P, TS, E])
        rw_o = st.sb("rw_o", [P, TS, E])
        acc = st.sb("acc", [P, TS, QKV])
        v = st.sb("v", [P, TS, HW])
        qkT = st.sb("qkT", [P, 2, S])
        gatew = st.sb("gatew", [P, TS])
        z = st.sb("z", [P, W])
        nmax = st.sb("nmax", [P, TS])
        bias = st.sb("bias", [P, TS])
        pr = st.sb("pr", [P, W])
        psum_of = st.sb("psum_of", [P, TS])
        rsum = st.sb("rsum", [P, TS])
        prT = st.sb("prT", [P, TS, S])
        aoT = st.sb("aoT", [P, S])
        acco = st.sb("acco", [P, TS, D])
        acco2 = st.sb("acco2", [P, TS, D])
        y_ps = [st.ps(f"y{n}") for n in range(RING)]
        t_ps, s_ps, p_ps, a_ps = (st.ps(n) for n in ("t", "s", "p", "a"))
        norm = Norm(nc, st, h)

        w_in, chain = st.sem("w_in"), st.sem("chain")
        wq_in = [st.sem(f"wq{n}_in") for n in range(E // WG)]
        wo_in = st.sem("wo_in")
        gates_ready, sim2_ready, norms_done, norms_var, norms_std, sim_ready = (
            st.sem(n) for n in ("gates_ready", "sim2_ready", "norms_done", "norms_var", "norms_std", "sim_ready"))
        xg_ready, xgt_done, xgt_ready, lg_done, lg_ready = (
            st.sem(n) for n in ("xg_ready", "xgt_done", "xgt_ready", "lg_done", "lg_ready"))
        ssq_ready, len_ready, less_max, exps_ready = (
            st.sem(n) for n in ("ssq_ready", "len_ready", "less_max", "exps_ready"))
        xn_ready, xt_done, xt_ready = st.sem("xn_ready"), st.sem("xt_done"), st.sem("xt_ready")
        y_done, y_used, acc_ready, v_ready, qkt_done, qkt_ready = (
            st.sem(n) for n in ("y_done", "y_used", "acc_ready", "v_ready", "qkt_done", "qkt_ready"))
        sc_done, z_ready, exp_done, pt_done, pt_ready, ao_done, ao_ready = (
            st.sem(n) for n in ("sc_done", "z_ready", "exp_done", "pt_done", "pt_ready", "ao_done", "ao_ready"))
        h_ready = st.sem("h_ready")
        block = st.block()
        NW = 4

        @block.sync
        def _(sp):
            sp.dma_start(sim[:, :, :], dram["f3_sim"].rearrange("(k p) n -> p k n", p=P)).then_inc(w_in, 16)
            sp.dma_start(gates[:, 0, :], dram["f3_gates"].partition_broadcast(P)).then_inc(w_in, 16)
            sp.dma_start(index[:, 0, :], dram["f3_index"].partition_broadcast(P)).then_inc(w_in, 16)
            sp.dma_start(mask[:, :, :], dram["f3_mask"]).then_inc(w_in, 16)
            for n in range(E // WG):
                sp.dma_start(wqkv[:, WG * n:WG * (n + 1), :, :], dram["f3_wqkv"][:, WG * n:WG * (n + 1)]).then_inc(wq_in[n], 16)
            sp.dma_start(wo[:, :, :], dram["f3_wo"]).then_inc(wo_in, 16)

        def unit_qkv(n):
            return n // TS, n % TS

        def unit_out(n):
            return n // (E // 2), n % (E // 2)

        @block.tensor
        def _(pe):
            opened(pe, xgt_done, lg_done, xt_done, y_done, qkt_done, sc_done, pt_done, ao_done)
            pe.wait_ge(sim2_ready, 1)
            for k in range(KD):
                last = nc.tensor.matmul(a_ps[:, 0:E], ones[:, :], sim2[:, k, :], start=(k == 0), stop=(k == KD - 1))
            last.then_inc(norms_done, 1)
            pe.wait_ge(sim_ready, 1)

            def transposes(done):
                for k in range(KD):
                    for s in range(TS):
                        last = nc.tensor.transpose(t_ps[:, k * S + s * P:k * S + (s + 1) * P],
                                                   xn[:, s, k * P:(k + 1) * P], ident[:, :])
                last.then_inc(done, 1)

            with pe.Fori(0, B) as i:
                pe.wait_ge(xg_ready, at(i + 1))
                transposes(xgt_done)
                pe.wait_ge(xgt_ready, at(i + 1))
                pe.wait_ge(lg_ready, at(i))
                for s in range(TS):
                    for k in range(KD):
                        last = nc.tensor.matmul(a_ps[:, s * E:(s + 1) * E], xT[:, k, s * P:(s + 1) * P], sim[:, k, :],
                                                start=(k == 0), stop=(k == KD - 1))
                last.then_inc(lg_done, 1)

            def transpose_x(n):
                pe.wait_ge(xn_ready, at(n + 1))
                transposes(xt_done)

            def products_qkv(b, n0, n1, before):
                for n in range(n0, n1):
                    e, s = unit_qkv(n)
                    if before is None:
                        if n % (TS * WG) == 0:
                            pe.wait_ge(wq_in[e // WG], 16)
                        if n >= RING:
                            pe.wait_ge(y_used, at(n - RING + 1))
                    else:
                        pe.wait_ge(y_used, at(before + n - RING + 1))
                    for k in range(KD):
                        last = nc.tensor.matmul(y_ps[n % RING][:, 0:QKV], xT[:, k, s * P:(s + 1) * P], wqkv[:, e, k, :],
                                                start=(k == 0), stop=(k == KD - 1))
                    last.then_inc(y_done, 1)

            transpose_x(0)
            pe.wait_ge(xt_ready, at(1))
            products_qkv(0, 0, NQ, None)
            transpose_x(1)
            pe.wait_ge(wo_in, 16)
            with pe.Fori(0, B) as i:
                before = NQ + NY * i
                pe.wait_ge(acc_ready, at(i + 1))
                pe.wait_ge(xt_ready, at(i + 2))
                for a in range(2):
                    for s in range(TS):
                        last = nc.tensor.transpose(t_ps[:, a * S + s * P:a * S + (s + 1) * P],
                                                   acc[:, s, a * HW:(a + 1) * HW], ident[:, :])
                last.then_inc(qkt_done, 1)
                products_qkv(i + 1, CUT[0], CUT[1], before)
                pe.wait_ge(qkt_ready, at(i + 1))
                pe.wait_ge(z_ready, at(i))
                for s in range(TS):
                    last = nc.tensor.matmul(s_ps[:, off[s]:off[s] + width[s]], qkT[:, 0, s * P:(s + 1) * P],
                                            qkT[:, 1, 0:width[s]], start=True, stop=True)
                last.then_inc(sc_done, 1)
                products_qkv(i + 1, CUT[1], CUT[2], before)
                pe.wait_ge(exp_done, at(i + 1))
                pe.wait_ge(pt_ready, at(i))
                for s in range(TS):
                    for k in range(width[s] // P):
                        last = nc.tensor.transpose(p_ps[:, k * S + s * P:k * S + (s + 1) * P],
                                                   pr[:, off[s] + k * P:off[s] + (k + 1) * P], ident[:, :])
                last.then_inc(pt_done, 1)
                products_qkv(i + 1, CUT[2], CUT[3], before)
                pe.wait_ge(pt_ready, at(i + 1))
                pe.wait_ge(v_ready, at(i + 1))
                pe.wait_ge(ao_ready, at(i))
                for k in range(TS):
                    last = nc.tensor.matmul(a_ps[:, k * P:S], v[:, k, :], prT[:, k, k * P:S],
                                            start=(k == 0), stop=(k == TS - 1), skip_group_check=True)
                last.then_inc(ao_done, 1)
                transpose_x(i + 2)
                pe.wait_ge(ao_ready, at(i + 1))
                for n in range(NO):
                    s, e = unit_out(n)
                    pe.wait_ge(y_used, at(before + NQ + n - RING + 1))
                    nc.tensor.matmul(y_ps[n % RING][:, :], aoT[:, s * P:(s + 1) * P], wo[:, 2 * e:2 * e + 2, :],
                                     start=True, stop=True).then_inc(y_done, 1)

        @block.scalar
        def _(act):
            opened(act, xgt_ready, xt_ready, v_ready, qkt_ready, exp_done, pt_ready, ao_ready)
            act.wait_ge(w_in, 16 * NW)
            nc.scalar.activation(gates[:, :, :], gates[:, :, :], ACT.Sigmoid).then_inc(gates_ready, 1)
            act.wait_ge(norms_var, 1)
            nc.scalar.activation(norms[:, :], norms[:, :], ACT.Sqrt).then_inc(norms_std, 1)
            norm.sqrt_act(act)
            copy = lambda: nc.scalar.activation(xT[:, :, :], t_ps[:, :].rearrange("p (k t) -> p k t", k=KD), ACT.Copy)
            with act.Fori(0, B) as i:
                act.wait_ge(xgt_done, at(i + 1))
                act.wait_ge(lg_done, at(i))
                copy().then_inc(xgt_ready, 1)
            act.wait_ge(ssq_ready, 1)
            nc.scalar.activation(ssq_all[:, :], ssq_all[:, :], ACT.Sqrt).then_inc(len_ready, 1)
            act.wait_ge(less_max, 1)
            nc.scalar.activation(e1[:, :, :], e1[:, :, :], ACT.Exp).then_inc(exps_ready, 1)
            act.wait_ge(lg_done, at(B))
            for n in range(2):
                act.wait_ge(xt_done, at(n + 1))
                if n == 1:
                    act.wait_ge(y_done, at(NQ))
                copy().then_inc(xt_ready, 1)
            with act.Fori(0, B) as i:
                act.wait_ge(acc_ready, at(i + 1))
                act.wait_ge(ao_done, at(i))
                nc.scalar.activation(v[:, :, :], acc[:, :, 2 * HW:QKV], ACT.Copy).then_inc(v_ready, 1)
                act.wait_ge(qkt_done, at(i + 1))
                nc.scalar.activation(qkT[:, :, :], t_ps[:, :].rearrange("p (a t) -> p a t", a=2), ACT.Copy)\
                    .then_inc(qkt_ready, 1)
                act.wait_ge(z_ready, at(i + 1))
                for s in range(TS):
                    c = slice(off[s], off[s] + width[s])
                    last = nc.scalar.activation(pr[:, c], z[:, c], ACT.Exp, bias=bias[:, s:s + 1], scale=-SCALE,
                                                accum_out=psum_of[:, s:s + 1])
                last.then_inc(exp_done, 1)
                act.wait_ge(pt_done, at(i + 1))
                nc.scalar.activation(prT[:, 0, :], p_ps[:, 0:S], ACT.Copy)
                nc.scalar.activation(prT[:, 1, P:S], p_ps[:, S + P:2 * S], ACT.Copy).then_inc(pt_ready, 1)
                act.wait_ge(ao_done, at(i + 1))
                act.wait_ge(y_done, at(NQ + NY * i + NQ))
                nc.scalar.activation(aoT[:, :], a_ps[:, 0:S], ACT.Copy).then_inc(ao_ready, 1)
                act.wait_ge(xt_done, at(i + 3))
                copy().then_inc(xt_ready, 1)

        @block.vector
        def _(dve):
            opened(dve, xg_ready, lg_ready, xn_ready, y_used, acc_ready, z_ready)
            ch = Chain(dve, chain)
            nc.vector.memset(ones[:, :], 1.0)
            nc.vector.memset(rw[:, TILES:TILES + PAD, :], 0.0)
            dve.wait_ge(w_in, 16 * NW)
            nc.vector.tensor_tensor(sim2[:, :, :], sim[:, :, :], sim[:, :, :], ALU.mult).then_inc(sim2_ready, 1)
            dve.wait_ge(norms_done, 1)
            nc.vector.tensor_scalar(norms[:, :], a_ps[:, 0:E], 1e-12, None, ALU.add).then_inc(norms_var, 1)
            dve.wait_ge(norms_std, 1)
            ch.link(nc.vector.reciprocal(norms[:, :], norms[:, :]))
            nc.vector.tensor_tensor(sim[:, :, :], sim[:, :, :],
                                    norms[:, :].rearrange("p (a e) -> p a e", a=1).broadcast_to([P, KD, E]), ALU.mult)\
                .then_inc(sim_ready, 1)
            norm.stats_dve(dve, ch)
            before, per = ch.n, 3
            with dve.Fori(0, B) as i:
                ch = Chain(dve, chain, before, i, per)
                dve.wait_ge(xgt_done, at(i))
                norm.apply_dve(ch, i, lambda s: xn[:, s:s + 1, :]).then_inc(xg_ready, 1)
                dve.wait_ge(xg_ready, at(i + 1))
                for s in range(TS):
                    last = nc.vector.tensor_tensor_reduce(square[:, :], xn[:, s, :], xn[:, s, :], 1.0, 0.0, ALU.mult, ALU.add,
                                                          ssq[:, s:s + 1])
                    ch.link(last)
                nc.vector.tensor_copy(ssq_all[:, ds(TS * i, TS)], ssq[:, :])
                dve.wait_ge(lg_done, at(i + 1))
                nc.vector.tensor_copy(lg[:, ds(TS * i, TS), :], a_ps[:, 0:TS * E].rearrange("p (s e) -> p s e", s=TS))\
                    .then_inc(lg_ready, 1)
                ch.done(before)
            ch = Chain(dve, chain, before + per * B)
            wide = lambda t: t[:, :].rearrange("p (n a) -> p n a", a=1).broadcast_to([P, TILES, E])
            all_ = lambda t: t[:, 0:TILES, :]
            dve.wait_ge(lg_ready, at(B))
            nc.vector.tensor_scalar(ssq_all[:, :], ssq_all[:, :], 1e-12, None, ALU.add).then_inc(ssq_ready, 1)
            dve.wait_ge(len_ready, 1)
            dve.wait_ge(gates_ready, 1)
            ch.link(nc.vector.reciprocal(ssq_all[:, :], ssq_all[:, :]))
            ch.link(nc.vector.tensor_tensor(all_(lg), all_(lg), wide(ssq_all), ALU.mult))
            ch.link(nc.vector.tensor_tensor(all_(lg), all_(lg), gates[:, :, :].broadcast_to([P, TILES, E]), ALU.subtract))
            top, where, none, high = rows
            ch.link(nc.vector.tensor_reduce(top[:, :], all_(lg), AX, ALU.max))
            ch.link(nc.vector.tensor_scalar(high[:, :], top[:, :], 0.0, None, ALU.max))
            ch.link(nc.vector.tensor_scalar(none[:, :], top[:, :], 0.0, None, ALU.is_le))
            ch.link(nc.vector.tensor_copy(all_(e1), all_(lg)))
            for n in range(2):
                if n == 1:
                    ch.link(nc.vector.scalar_tensor_tensor(all_(e1), all_(best), NEG, all_(e1), ALU.mult, ALU.add))
                    ch.link(nc.vector.tensor_reduce(top[:, :], all_(e1), AX, ALU.max))
                ch.link(nc.vector.tensor_tensor(all_(e2), all_(e1), wide(top), ALU.not_equal))
                ch.link(nc.vector.scalar_tensor_tensor(all_(e2), all_(e2), 64.0, index[:, :, :].broadcast_to([P, TILES, E]),
                                                       ALU.mult, ALU.add))
                ch.link(nc.vector.tensor_reduce(where[:, :], all_(e2), AX, ALU.min))
                ch.link(nc.vector.tensor_tensor(all_(e2), index[:, :, :].broadcast_to([P, TILES, E]), wide(where), ALU.is_equal))
                if n == 0:
                    ch.link(nc.vector.tensor_copy(all_(best), all_(e2)))
                else:
                    ch.link(nc.vector.tensor_tensor(all_(best), all_(best), all_(e2), ALU.add))
            ch.link(nc.vector.tensor_tensor(all_(best), all_(best), wide(none), ALU.mult))
            ch.link(nc.vector.scalar_tensor_tensor(all_(best), all_(lg), 0.0, all_(best), ALU.is_gt, ALU.add))
            nc.vector.scalar_tensor_tensor(all_(e1), all_(lg), 0.0, wide(high), ALU.max, ALU.subtract).then_inc(less_max, 1)
            dve.wait_ge(exps_ready, 1)
            ch.link(nc.vector.tensor_tensor(all_(e1), all_(e1), all_(best), ALU.mult))
            ch.link(nc.vector.tensor_reduce(top[:, :], all_(e1), AX, ALU.add))
            ch.link(nc.vector.reciprocal(top[:, :], top[:, :]))
            ch.link(nc.vector.tensor_tensor(all_(rw), all_(e1), wide(top), ALU.mult))

            def accumulate_qkv(ch, n0, n1, before):
                for n in range(n0, n1):
                    e, s = unit_qkv(n)
                    dve.wait_ge(y_done, at(before + n + 1))
                    y = y_ps[n % RING][:, 0:QKV]
                    if e == 0:
                        last = nc.vector.tensor_scalar(acc[:, s, :], y, rw_q[:, s, e:e + 1], None, ALU.mult)
                    else:
                        dve.wait_ge(y_used, at(before + n - TS + 1))
                        last = nc.vector.scalar_tensor_tensor(acc[:, s, :], y, rw_q[:, s, e:e + 1], acc[:, s, :],
                                                              ALU.mult, ALU.add)
                    last.then_inc(y_used, 1)

            norm.apply_dve(ch, 0, lambda s: xn[:, s:s + 1, :]).then_inc(xn_ready, 1)
            ch.link(nc.vector.tensor_copy(rw_q[:, :, :], rw[:, 0:TS, :]))
            dve.wait_ge(xt_done, at(1))
            norm.apply_dve(ch, 1, lambda s: xn[:, s:s + 1, :]).then_inc(xn_ready, 1)
            accumulate_qkv(ch, 0, NQ, 0)
            dve.wait_ge(y_used, at(NQ))
            ch.link(nc.vector.memset(gatew[:, 0:1], 0.0))
            nc.vector.memset(gatew[:, 1:2], 0.0).then_inc(acc_ready, 1)
            before, per = ch.n, 6
            with dve.Fori(0, B) as i:
                ch = Chain(dve, chain, before, i, per)
                y_before = NQ + NY * i
                ch.link(nc.vector.tensor_copy(rw_o[:, :, :], rw_q[:, :, :]))
                ch.link(nc.vector.tensor_copy(rw_q[:, :, :], rw[:, ds(TS * i + TS, TS), :]))
                dve.wait_ge(v_ready, at(i + 1))
                dve.wait_ge(qkt_done, at(i + 1))
                accumulate_qkv(ch, CUT[0], CUT[1], y_before)
                dve.wait_ge(sc_done, at(i + 1))
                dve.wait_ge(exp_done, at(i))
                nc.vector.memset(gatew[:, 0:1], 0.0)
                for s in range(TS):
                    c = slice(off[s], off[s] + width[s])
                    last = nc.vector.tensor_tensor_reduce(z[:, c], s_ps[:, c], mask[:, s, 0:width[s]], -1.0, BIG,
                                                          ALU.add, ALU.min, nmax[:, s:s + 1])
                ch.link(last)
                nc.vector.tensor_scalar(bias[:, :], nmax[:, :], SCALE, None, ALU.mult).then_inc(z_ready, 1)
                accumulate_qkv(ch, CUT[1], CUT[2], y_before)
                dve.wait_ge(xt_done, at(i + 2))
                norm.apply_dve(ch, i + 2, lambda s: xn[:, s:s + 1, :]).then_inc(xn_ready, 1)
                accumulate_qkv(ch, CUT[2], CUT[3], y_before)
                dve.wait_ge(y_used, at(y_before + NQ))
                nc.vector.memset(gatew[:, 1:2], 0.0).then_inc(acc_ready, 1)
                dve.wait_ge(exp_done, at(i + 1))
                ch.link(nc.vector.reciprocal(rsum[:, :], psum_of[:, :]))
                for n in range(NO):
                    s, e = unit_out(n)
                    dve.wait_ge(y_done, at(y_before + NQ + n + 1))
                    for a in range(2):
                        y = y_ps[n % RING][:, a * D:(a + 1) * D]
                        g = rw_o[:, s, 2 * e + a:2 * e + a + 1]
                        o = acco[:, s, :] if a == 0 else acco2[:, s, :]
                        if e == 0:
                            last = nc.vector.tensor_scalar(o, y, g, None, ALU.mult)
                        else:
                            dve.wait_ge(y_used, at(y_before + NQ + n))
                            last = nc.vector.scalar_tensor_tensor(o, y, g, o, ALU.mult, ALU.add)
                    last.then_inc(y_used, 1)
                dve.wait_ge(y_used, at(y_before + NY))
                ch.link(nc.vector.tensor_tensor(acco[:, :, :], acco[:, :, :], acco2[:, :, :], ALU.add))
                for s in range(TS):
                    hs = h[:, ds(TS * i + s, 1), :]
                    last = nc.vector.scalar_tensor_tensor(hs, acco[:, s:s + 1, :], rsum[:, s:s + 1], hs, ALU.mult, ALU.add)
                last.then_inc(h_ready, 1)
                dve.wait_ge(h_ready, i + 1)
                ch.done(before)


def store_out(nc, out, h):
    with Stage(nc, "store") as st:
        stored = st.sem("stored")
        block = st.block()

        @block.sync
        def _(sp):
            sp.dma_start(out.rearrange("b (s p) d -> p (b s) d", p=P), h[:, 0:TILES, :]).then_inc(stored, 16)
            sp.wait_ge(stored, 16)


def attention_of(name, scale, **kinds):
    return (lambda nc, dram, h_padded, ident: attention(nc, dram, h_padded, ident, name, scale, **kinds)), True


STAGE_LIST = [
    attention_of("a0", 0.25, causal=True, kind="add"),
    (ternary_mlp, False),
    attention_of("a1", 0.25),
    (channel_mixer, False),
    attention_of("a2", 0.25, causal=True, kind="add", relative=True),
    (expert_choice, False),
    attention_of("a3", 1.0 / 16.0, kind="mult", latent=True),
    (attention_experts, False),
]


def build(nc, dram, out, stages=9):
    with ExitStack() as ctx:
        padded = ctx.enter_context(nc.sbuf_tensor("h", [P, TS + TILES + PAD, D], F32))
        h = padded[:, TS:, :]
        ident = ctx.enter_context(nc.sbuf_tensor("ident_sb", [P, P], F32))
        tok_mixer(nc, dram, h, ident)
        for n, (stage, whole) in enumerate(STAGE_LIST):
            if n + 2 <= stages:
                stage(nc, dram, padded if whole else h, ident)
        store_out(nc, out, h)


STAGES = 9


def kernel(**inputs):
    import numpy as np
    import concourse.bacc as _bacc
    from concourse import mybir as _mybir
    from concourse.bass_utils import run_bass_kernel_spmd as _run

    c = np.ascontiguousarray
    a = {k: np.asarray(v) for k, v in inputs.items()}
    lay = {}
    lay["ident"] = np.eye(128, dtype=np.float32)
    x = a["x"]
    lay["tok_x"] = np.concatenate([x.transpose(0, 1, 3, 2), np.ones((8, 1, 4, 256), np.float32)], axis=1)
    lay["tok_xflat"] = x.transpose(0, 2, 3, 1).reshape(8, 256, 256)
    lay["tok_wqkv"] = np.concatenate(
        [np.concatenate([a[f"L0_tok_W{n}_w"].T, a[f"L0_tok_W{n}_b"][None]], axis=0) for n in "qkv"], axis=1)
    lay["tok_wbT"] = a["L0_tok_w_bias"].T
    mask = np.zeros((256, 256, 4), np.uint8)
    mask[:, :, 0] = a["L0_tok_local_mask"].T.view(np.uint8)
    lay["tok_maskT"] = mask.view(np.int32)[:, :, 0]
    lay["tok_outw"] = a["L0_tok_out_w"]
    lay["tok_vecs"] = np.stack([a["L0_tok_out_b"], a["L0_tok_ln_g"], a["L0_tok_ln_b"]])

    row = np.arange(128)
    lay["parity"] = np.stack([(row // 16) % 2 == 0, (row // 16) % 2 == 1], axis=1).astype(np.float32)
    order = np.concatenate([np.arange(16) + 16 * (8 * (g // 2) + g % 2 + 2 * j) for g in range(4) for j in range(4)])

    def attn(name, wq, wk, wv, wo, bq, bk, bv, bo):
        lay[name + "_wq"], lay[name + "_wk"], lay[name + "_wv"], lay[name + "_wo"] = wq, wk, wv, wo[order]
        lay[name + "_bqk"] = np.stack([bq.reshape(2, 128).T, bk.reshape(2, 128).T], axis=1)
        lay[name + "_bv"], lay[name + "_bo"] = bv, bo

    def tiles(m):
        return m.reshape(2, 128, -1).transpose(1, 0, 2)

    i, j = np.arange(256)[:, None], np.arange(256)[None, :]
    fenwick = np.zeros((256, 256), bool)
    for t in range(256):
        fenwick[t, t] = True
        step = 1
        while t - step >= 0:
            fenwick[t, t - step] = True
            step *= 2
    w, bb = a["L0_attn_W_qkv"], a["L0_attn_b_qkv"]
    attn("a0", w[:, 0:256], w[:, 256:512], w[:, 512:768], a["L0_attn_W_proj"], bb[0:256], bb[256:512], bb[512:768], a["L0_attn_b_proj"])
    lay["a0_matrix"] = tiles(np.where(fenwick, 0.0, NEG).astype(np.float32))

    lay["f0_wfcT"] = a["L0_ffn_W_fc"].T
    lay["f0_wprojT"] = a["L0_ffn_W_proj"].T
    lay["f0_lnwb"] = np.stack([a["L0_ffn_ln_w"].reshape(8, 128).T, a["L0_ffn_ln_b"].reshape(8, 128).T], axis=1)
    attn("a1", *(a["L1_attn_W" + n].T for n in "qkvo"), *(a["L1_attn_b" + n] for n in "qkvo"))
    for n in "rkv":
        lay[f"f1_w{n}T"] = a["L1_ffn_W_" + n].T
    lay["f1_mu"] = np.stack([a["L1_ffn_mu_" + n].reshape(2, 128).T for n in "rk"], axis=1)
    attn("a2", *(a["L2_attn_W" + n] for n in "qkvo"), *(a["L2_attn_b" + n] for n in "qkvo"))
    lay["a2_matrix"] = tiles(np.where(j <= i, 0.0, NEG).astype(np.float32))
    relT = np.zeros((8, 16, 2, 256), np.float32)
    relT[0::2, :, 0], relT[1::2, :, 1] = a["L2_attn_rel_key"][256:512].T, a["L2_attn_rel_key"][256:512].T
    lay["a2_relT"] = relT.reshape(128, 2, 256)
    lay["moe_gateT"] = a["L2_ffn_gate_w"].T
    lay["moe_iota"] = np.arange(1, 33, dtype=np.float32)

    def chunks(w):
        return w.reshape(-1, 128, w.shape[1]).transpose(1, 0, 2).reshape(128, -1)

    def expert(wg, wu, wd):
        return np.concatenate([chunks(wg.T), chunks(wu.T), chunks(wd.T)], axis=1)

    shared = expert(a["L2_ffn_Ws_g"], a["L2_ffn_Ws_u"], a["L2_ffn_Ws_d"])
    lay["moe_experts"] = np.stack([expert(a["L2_ffn_Wg"][e], a["L2_ffn_Wu"][e], a["L2_ffn_Wd"][e]) for e in range(16)]
                                  + [shared, shared])

    z256 = np.zeros(256, np.float32)
    attn("a3", a["L3_attn_W_q"], a["L3_attn_W_k"], a["L3_attn_W_v"], a["L3_attn_W_o"], z256, z256, z256, z256)
    lay["a3_wdown"] = a["L3_attn_W_down_kv"]
    lay["a3_wupk"], lay["a3_wupv"] = a["L3_attn_W_up_k"], a["L3_attn_W_up_v"]
    lay["a3_matrix"] = tiles(np.exp(np.float32(-0.01) * np.abs(i - j).astype(np.float32)))
    lay["f3_sim"], lay["f3_gates"] = a["L3_ffn_sim_matrix"], a["L3_ffn_gates"]
    lay["f3_index"] = np.arange(16, dtype=np.float32)
    lay["f3_mask"] = lay["a2_matrix"]
    lay["f3_wqkv"] = np.concatenate([a[f"L3_ffn_{n}_proj"] for n in "qkv"], axis=2).reshape(16, 2, 128, 384).transpose(2, 0, 1, 3)
    lay["f3_wo"] = a["L3_ffn_o_proj"].transpose(1, 0, 2)

    nc = _bacc.Bacc("TRN2", target_bir_lowering=False, num_devices=1)
    arrays, dram = {}, {}
    for name, v in lay.items():
        v = c(v)
        arrays[f"in_{name}"] = v
        dram[name] = nc.dram_tensor(f"in_{name}", v.shape, _mybir.dt.from_np(v.dtype), kind="ExternalInput").ap()
    out = nc.dram_tensor("out_0_dram", (8, 256, 256), _mybir.dt.float32, kind="ExternalOutput").ap()
    build(nc, dram, out, STAGES)
    r = _run(nc, [arrays], core_ids=[0])
    return r.results[0]["out_0_dram"]
```

```python
from contextlib import ExitStack

import numpy as np

import concourse.bass as bass
from concourse import mybir

ALU = mybir.AluOpType
ACT = mybir.ActivationFunctionType
AX = mybir.AxisListType.X
F32 = mybir.dt.float32
F32R = mybir.dt.float32r

P = 128
B = 8
S = 256
D = 256
TS = S // P
TILES = B * TS
KD = D // P
HEADS = 16
HD = D // HEADS
PAD = 2 * TS
EPS = 1e-5
BIG = 3.0e38
NEG = -1.0e30
ds = bass.ds


def opened(eng, *sems):
    for s in sems:
        eng.sem_inc(s, 1)


def at(n):
    return n + 1


class Chain:

    def __init__(self, eng, sem, before=0, turn=0, per=0):
        self.eng, self.sem, self.n, self.per = eng, sem, before, per
        self.base = turn * per if per else 0

    def link(self, ins):
        self.n += 1
        ins.then_inc(self.sem, 1)
        self.eng.wait_ge(self.sem, self.base + self.n if self.per else self.n)

    def done(self, before):
        assert self.n - before == self.per, (self.n, before, self.per)


class Stage:

    def __init__(self, nc, name):
        self.nc, self.name, self.ctx, self.sems, self.work = nc, name, ExitStack(), [], None

    def __enter__(self):
        self.ctx.__enter__()
        return self

    def __exit__(self, *a):
        if a[0] is not None:
            return self.ctx.__exit__(*a)
        self.work.__exit__(*a)
        with self.nc.Block() as clearing:
            @clearing.sync
            def _(sp):
                for s in self.sems:
                    sp.sem_clear(s)
        return self.ctx.__exit__(*a)

    def sem(self, name):
        self.sems.append(self.ctx.enter_context(self.nc.semaphore(f"{self.name}_{name}")))
        return self.sems[-1]

    def sb(self, name, shape, dt=F32):
        return self.ctx.enter_context(self.nc.sbuf_tensor(f"{self.name}_{name}", shape, dt))

    def ps(self, name, shape=(P, 512)):
        return self.ctx.enter_context(self.nc.psum_tensor(f"{self.name}_{name}_ps", list(shape), F32))

    def block(self):
        self.work = self.nc.Block()
        return self.work.__enter__()


class Norm:

    def __init__(self, nc, st, h):
        self.nc, self.h = nc, h
        self.stats = st.sb("ln_stats", [P, TILES, 6])
        self.mr = st.sb("ln_mean_rstd", [P, TILES + PAD, 2])
        self.std = st.sb("ln_std", [P, TILES])
        self.cur = st.sb("ln_cur", [P, TS, 2])
        self.var_ready = st.sem("ln_var_ready")
        self.std_ready = st.sem("ln_std_ready")

    def stats_dve(self, dve, ch):
        nc = self.nc
        nc.vector.memset(self.mr[:, TILES:TILES + PAD, :], 0.0)
        for t in range(TILES):
            last = nc.vector.bn_stats(self.stats[:, t, :], self.h[:, t, :])
        ch.link(last)
        for t in range(TILES):
            last = nc.vector.bn_aggr(self.mr[:, t, :], self.stats[:, t, :])
        ch.link(last)
        nc.vector.tensor_scalar(self.std[:, :], self.mr[:, 0:TILES, 1], EPS, None, ALU.add).then_inc(self.var_ready, 1)
        dve.wait_ge(self.std_ready, 1)
        ch.link(nc.vector.reciprocal(self.mr[:, 0:TILES, 1], self.std[:, :]))

    def sqrt_act(self, act):
        act.wait_ge(self.var_ready, 1)
        self.nc.scalar.activation(self.std[:, :], self.std[:, :], ACT.Sqrt).then_inc(self.std_ready, 1)

    def apply_dve(self, ch, b, dst):
        nc = self.nc
        ch.link(nc.vector.tensor_copy(self.cur[:, :, :], self.mr[:, ds(TS * b, TS), :]))
        for s in range(TS):
            last = nc.vector.tensor_scalar(dst(s), self.h[:, ds(TS * b + s, 1), :], self.cur[:, s, 0:1],
                                           self.cur[:, s, 1:2], ALU.subtract, ALU.mult)
        return last



def tok_mixer(nc, dram, h, ident):
    F, H = 64, 4
    QKV = 3 * F
    with Stage(nc, "tok") as st:
        xa = st.sb("xa", [F + 1, 2, H, S])
        wqkv = st.sb("wqkv", [F + 1, QKV])
        ewT = st.sb("ewT", [P, TS, S])
        mask_int = st.sb("mask_int", [P, TS, S], mybir.dt.int32)
        maskf = st.sb("maskf", [P, TS, S])
        outw = st.sb("outw", [P, KD, D])
        vecs = st.sb("vecs", [P, 3, D])
        enq = st.sb("enq", [P, 2, TS, D])
        rhs = st.sb("rhs", [P, 2, TS, 2, D])
        dn = st.sb("dn", [P, TS, D])
        y = st.sb("y", [P, TS, D])
        yT = st.sb("yT", [P, KD, S])
        stats = st.sb("stats", [P, TS, 6])
        mean_var = st.sb("mean_var", [P, TS, 2])
        std = st.sb("std", [P, TS])
        rstd = st.sb("rstd", [P, TS])
        gate = st.sb("gate", [P, 2])
        proj_ps = [st.ps(f"proj{n}") for n in range(4)]
        mix_ps = [st.ps(f"mix{n}") for n in range(2)]
        t_ps = st.ps("t")
        out_ps = st.ps("out")

        w_in = st.sem("w_in")
        x_in = [st.sem(f"x{o}_in") for o in range(2)]
        res_in, res_ready = st.sem("res_in"), st.sem("res_ready")
        pre = st.sem("pre")
        ew_ready = st.sem("ew_ready")
        proj_done = st.sem("proj_done")
        proj_read = st.sem("proj_read")
        rhs_ready = st.sem("rhs_ready")
        mix_done = st.sem("mix_done")
        chain = st.sem("chain")
        y_ready = st.sem("y_ready")
        yt_done = st.sem("yt_done")
        yt_ready = st.sem("yt_ready")
        out_done = st.sem("out_done")
        out_read = st.sem("out_read")
        var_ready, std_ready, h_ready = st.sem("var_ready"), st.sem("std_ready"), st.sem("h_ready")
        block = st.block()
        NW = 6

        @block.sync
        def _(sp):
            sp.dma_start(wqkv[:, :], dram["tok_wqkv"]).then_inc(w_in, 16)
            sp.dma_start(ewT[:, :, :], dram["tok_wbT"].rearrange("(k p) t -> p k t", p=P)).then_inc(w_in, 16)
            sp.dma_start(mask_int[:, :, :], dram["tok_maskT"].rearrange("(k p) t -> p k t", p=P)).then_inc(w_in, 16)
            sp.dma_start(outw[:, :, :], dram["tok_outw"].rearrange("(k p) t -> p k t", p=P)).then_inc(w_in, 16)
            sp.dma_start(vecs[:, :, :], dram["tok_vecs"].partition_broadcast(P)).then_inc(w_in, 16)
            sp.dma_start(ident[:, :], dram["ident"]).then_inc(w_in, 16)
            for o in range(2):
                sp.dma_start(xa[:, o, :, :], dram["tok_x"][o]).then_inc(x_in[o], 16)
            sp.dma_start(h[:, 0:TILES, :], dram["tok_xflat"].rearrange("b (s p) d -> p (b s) d", p=P)).then_inc(res_in, 16)
            with sp.Fori(0, B // 2 - 1) as i:
                for o in range(2):
                    b = 2 * i + 2 + o
                    sp.wait_ge(proj_done, at(TS * (b - 1)))
                    sp.dma_start(xa[:, o, :, :], dram["tok_x"][ds(b, 1)].rearrange("a c h l -> (a c) h l")).then_inc(x_in[o], 16)

        @block.tensor
        def _(pe):
            opened(pe, proj_done, mix_done, yt_done, out_done)
            pe.wait_ge(w_in, 16 * NW)

            def project(b, o):
                pe.wait_ge(x_in[o], 16 * (b // 2) + 16 if isinstance(b, int) else 8 * (b - o) + 16)
                pe.wait_ge(proj_read, at(TS * b))
                pe.wait_ge(rhs_ready, at(TS * b))
                for s in range(TS):
                    for hh in range(H):
                        last = nc.tensor.matmul(
                            proj_ps[2 * s + hh // 2][:, (hh % 2) * QKV:(hh % 2 + 1) * QKV],
                            xa[:, o, hh, s * P:(s + 1) * P], wqkv[:, :], start=True, stop=True)
                    last.then_inc(proj_done, 1)

            def mix(b, o):
                pe.wait_ge(rhs_ready, at(TS * (b + 1)))
                pe.wait_ge(y_ready, at(b))
                for t in range(TS):
                    for s in range(TS):
                        last = nc.tensor.matmul(mix_ps[t][:, :], ewT[:, s, t * P:(t + 1) * P],
                                                rhs[:, o, s, :, :], start=(s == 0), stop=(s == TS - 1))
                    last.then_inc(mix_done, 1)

            def finish(b):
                pe.wait_ge(y_ready, at(b + 1))
                pe.wait_ge(yt_ready, at(b))
                for k in range(KD):
                    for s in range(TS):
                        last = nc.tensor.transpose(t_ps[:, k * S + s * P:k * S + (s + 1) * P],
                                                   y[:, s, k * P:(k + 1) * P], ident[:, :])
                last.then_inc(yt_done, 1)
                pe.wait_ge(yt_ready, at(b + 1))
                pe.wait_ge(out_read, at(b))
                for s in range(TS):
                    for k in range(KD):
                        last = nc.tensor.matmul(out_ps[:, s * D:(s + 1) * D], yT[:, k, s * P:(s + 1) * P],
                                                outw[:, k, :], start=(k == 0), stop=(k == KD - 1))
                last.then_inc(out_done, 1)

            project(0, 0)
            pe.wait_ge(ew_ready, 1)
            mix(0, 0)
            project(1, 1)
            with pe.Fori(0, B // 2 - 1) as i:
                for o in (1, 0):
                    b = 2 * i + 2 - o
                    mix(b, o)
                    project(b + 1, 1 - o)
                    finish(b - 1)
            mix(B - 1, 1)
            finish(B - 2)
            finish(B - 1)

        @block.scalar
        def _(act):
            opened(act, proj_read, yt_ready, std_ready)
            act.wait_ge(w_in, 16 * NW)
            act.wait_ge(pre, 2)
            nc.scalar.activation(ewT[:, :, :], ewT[:, :, :], ACT.Exp).then_inc(ew_ready, 1)

            def exps(b, o):
                if not (isinstance(b, int) and b < 2):
                    act.wait_ge(mix_done, at(TS * (b - 1)))
                    act.wait_ge(y_ready, at(b - 1))
                for s in range(TS):
                    act.wait_ge(proj_done, at(TS * b + s + 1))
                    for n in range(2):
                        v = proj_ps[2 * s + n][:, 0:2 * QKV].rearrange("p (a r) -> p a r", a=2)
                        nc.scalar.activation(rhs[:, o, s, 1, n * 128:(n + 1) * 128].rearrange("p (a r) -> p a r", a=2),
                                             v[:, :, F:2 * F], ACT.Exp)
                        last = nc.scalar.activation(enq[:, o, s, n * 128:(n + 1) * 128].rearrange("p (a r) -> p a r", a=2),
                                                    v[:, :, 0:F], ACT.Exp, scale=-1.0)
                    last.then_inc(proj_read, 1)

            def finish(b):
                act.wait_ge(yt_done, at(b + 1))
                act.wait_ge(out_done, at(b))
                nc.scalar.activation(yT[:, :, :], t_ps[:, :].rearrange("p (k t) -> p k t", k=KD), ACT.Copy).then_inc(yt_ready, 1)

            def sqrt(b):
                act.wait_ge(var_ready, at(b + 1))
                nc.scalar.activation(std[:, :], std[:, :], ACT.Sqrt).then_inc(std_ready, 1)

            exps(0, 0)
            exps(1, 1)
            with act.Fori(0, B // 2 - 1) as i:
                for o in (1, 0):
                    b = 2 * i + 2 - o
                    exps(b + 1, 1 - o)
                    finish(b - 1)
                    sqrt(b - 1)
            for b in (B - 2, B - 1):
                finish(b)
                sqrt(b)

        @block.vector
        def _(dve):
            opened(dve, rhs_ready, y_ready, out_read, var_ready, h_ready)
            nc.vector.memset(h[:, TILES:TILES + PAD, :], 0.0)
            dve.wait_ge(w_in, 16 * NW)
            nc.vector.tensor_copy(maskf[:, :, :], mask_int[:, :, :]).then_inc(pre, 1)
            dve.wait_ge(pre, 1)
            nc.vector.tensor_tensor(ewT[:, :, :], ewT[:, :, :], maskf[:, :, :], ALU.mult).then_inc(pre, 1)

            def weighted(b, o):
                if not (isinstance(b, int) and b < 2):
                    dve.wait_ge(mix_done, at(TS * (b - 1)))
                for s in range(TS):
                    dve.wait_ge(proj_read, at(TS * b + s + 1))
                    for n in range(2):
                        v = proj_ps[2 * s + n][:, 0:2 * QKV].rearrange("p (a r) -> p a r", a=2)
                        last = nc.vector.tensor_tensor(
                            rhs[:, o, s, 0, n * 128:(n + 1) * 128].rearrange("p (a r) -> p a r", a=2),
                            rhs[:, o, s, 1, n * 128:(n + 1) * 128].rearrange("p (a r) -> p a r", a=2),
                            v[:, :, 2 * F:3 * F], ALU.mult)
                    last.then_inc(rhs_ready, 1)

            def quotient(ch, b, o):
                for t in range(TS):
                    dve.wait_ge(mix_done, at(TS * b + t + 1))
                    last = nc.vector.scalar_tensor_tensor(dn[:, t, :], enq[:, o, t, :], 1.0, mix_ps[t][:, D:2 * D],
                                                          ALU.add, ALU.mult)
                ch.link(last)
                ch.link(nc.vector.reciprocal(dn[:, :, :], dn[:, :, :]))
                dve.wait_ge(yt_done, at(b))
                for t in range(TS):
                    last = nc.vector.tensor_tensor(y[:, t, :], mix_ps[t][:, 0:D], dn[:, t, :], ALU.mult)
                last.then_inc(y_ready, 1)

            def add_out(ch, b):
                dve.wait_ge(res_ready, 1)
                dve.wait_ge(out_done, at(b + 1))
                hs = h[:, ds(TS * b, TS), :]
                nc.vector.tensor_tensor(hs, out_ps[:, :].rearrange("p (s d) -> p s d", s=TS), hs, ALU.add).then_inc(out_read, 1)
                dve.wait_ge(out_read, at(b + 1))
                nc.vector.memset(gate[:, 0:1], 0.0)
                for s in range(TS):
                    last = nc.vector.bn_stats(stats[:, s:s + 1, :], h[:, ds(TS * b + s, 1), :])
                ch.link(last)
                nc.vector.memset(gate[:, 1:2], 0.0)
                for s in range(TS):
                    last = nc.vector.bn_aggr(mean_var[:, s, :], stats[:, s, :])
                ch.link(last)
                nc.vector.tensor_scalar(std[:, :], mean_var[:, :, 1], EPS, None, ALU.add).then_inc(var_ready, 1)

            def normalize(ch, b):
                dve.wait_ge(std_ready, at(b + 1))
                ch.link(nc.vector.reciprocal(rstd[:, :], std[:, :]))
                for s in range(TS):
                    hs = h[:, ds(TS * b + s, 1), :]
                    last = nc.vector.tensor_scalar(hs, hs, mean_var[:, s, 0:1], rstd[:, s:s + 1], ALU.subtract, ALU.mult)
                ch.link(last)
                hs = h[:, ds(TS * b, TS), :]
                ch.link(nc.vector.tensor_tensor(hs, hs, vecs[:, 1:2, :].broadcast_to([P, TS, D]), ALU.mult))
                nc.vector.tensor_tensor(hs, hs, vecs[:, 2:3, :].broadcast_to([P, TS, D]), ALU.add).then_inc(h_ready, 1)
                dve.wait_ge(h_ready, at(b + 1))

            ch = Chain(dve, chain)
            weighted(0, 0)
            quotient(ch, 0, 0)
            weighted(1, 1)
            before, per = ch.n, 2 * (2 + 2 + 3)
            with dve.Fori(0, B // 2 - 1) as i:
                ch = Chain(dve, chain, before, i, per)
                for o in (1, 0):
                    b = 2 * i + 2 - o
                    quotient(ch, b, o)
                    weighted(b + 1, 1 - o)
                    add_out(ch, b - 1)
                    normalize(ch, b - 1)
                ch.done(before)
            ch = Chain(dve, chain, before + per * (B // 2 - 1))
            quotient(ch, B - 1, 1)
            for b in (B - 2, B - 1):
                add_out(ch, b)
                normalize(ch, b)

        @block.gpsimd
        def _(pool):
            pool.wait_ge(res_in, 16)
            pool.wait_ge(w_in, 16 * NW)
            nc.gpsimd.tensor_tensor(h[:, 0:TILES, :], h[:, 0:TILES, :], vecs[:, 0:1, :].broadcast_to([P, TILES, D]), ALU.add)\
                .then_inc(res_ready, 1)



def attention(nc, dram, h_padded, ident, name, scale, causal=False, kind="plain", latent=False, relative=False):
    h = h_padded[:, TS:, :]
    HU = 2
    NU = HEADS // HU
    NSETS = NU // 2
    width = [P, S] if causal else [S, S]
    off = [0, width[0]]
    W = width[0] + width[1]
    cols = [slice(0, S), slice(S + P, 2 * S)] if causal else [slice(0, 2 * S)]
    PARTS = ((0, 0),) if relative else ((1, 0), (0, 1), (0, 0))
    NPARTS, PART = (1, F32) if relative else (2, F32R)
    copies = "act" if relative else "dve"
    projections = [("x", copies)] + ([("kv", "act"), ("lat", "act")] if latent else []) + [("q", "act"), ("k", "dve"), ("v", "dve")]
    steps = projections + [("o0", "dve"), ("o1", "dve"), ("t", copies), ("y", "dve")]
    NP, NS = len(projections), len(steps)
    slot_of = [k * NU // NS for k in range(NS)]

    def reads(e, k):
        return sum(x == e for _, x in steps[:k])

    BEFORE, AFTER = -1, B

    def done(b, k):
        if isinstance(b, int) and b == BEFORE:
            return at(k + 1)
        skipped = NP if isinstance(b, int) and b == AFTER else 0
        return at(NP + NS * b + k + 1 - skipped)

    def read(b, k, e):
        if isinstance(b, int) and b == BEFORE:
            return at(reads(e, k + 1))
        skipped = reads(e, NP) if isinstance(b, int) and b == AFTER else 0
        return at(reads(e, NP) + reads(e, NS) * b + reads(e, k + 1) - skipped)

    with Stage(nc, name) as st:
        weights = st.sb("weights", [P, 4, KD, D])
        w_parts = [weights] if relative else [st.sb(f"w{part}", [P, 4, KD, D], F32R) for part in range(2)]
        WQ, WK, WV, WO = range(4)
        bqk = st.sb("bqk", [P, 2, KD])
        parity = st.sb("parity", [P, 2])
        bv = st.sb("bv", [P, D])
        bo = st.sb("bo", [P, D])
        if kind != "plain":
            matrix = st.sb("matrix", [P, TS, S])
        xn = st.sb("xn", [P, TS, D])
        xT = [st.sb(f"xT{part}", [P, KD, S], PART) for part in range(NPARTS)]
        qT = st.sb("qT", [P, 2, KD, S])
        kT = st.sb("kT", [P, 2, 2, KD, S])
        v = st.sb("v", [P, 2, TS, HEADS, 32])
        if kind != "plain":
            z = st.sb("z", [P, 2, HU, W])
        pr = st.sb("pr", [P, 2, HU, W])
        nmax = st.sb("nmax", [P, 2, HU, TS])
        carry = st.sb("carry", [P, NU])
        prT = st.sb("prT", [P, 2, HU, TS, S])
        oT = st.sb("oT", [P, 2, NSETS, S])
        rs = st.sb("rs", [P, TS, HEADS])
        on = st.sb("on", [P, TS, HEADS, HD])
        onT = [st.sb(f"onT{part}", [P, KD, S], PART) for part in range(NPARTS)]
        sc_ps = st.ps("scores", (P, 2 * HU, 512))
        t_ps = st.ps("t", (P, 2, 512))
        o_ps = st.ps("o")
        m_ps = st.ps("m")
        norm = Norm(nc, st, h)

        w_in, chain, xn_ready, bias_scaled = (st.sem(n) for n in ("w_in", "chain", "xn_ready", "bias_scaled"))
        cleared, w_rounded, w_split = st.sem("cleared"), st.sem("w_rounded"), st.sem("w_split")
        m_done = st.sem("m_done")
        m_read = {e: st.sem(f"m_read_{e}") for e in ("act", "dve")}
        sc_done, max_ready, exp_done = st.sem("sc_done"), st.sem("max_ready"), st.sem("exp_done")
        t_done, t_read_act, t_read_dve = st.sem("t_done"), st.sem("t_read_act"), st.sem("t_read_dve")
        av_done, o_ready, hb_ready = st.sem("av_done"), st.sem("o_ready"), st.sem("hb_ready")
        if latent:
            wdown = st.sb("wdown", [P, KD, 64])
            wupk = st.sb("wupk", [64, D])
            wupv = st.sb("wupv", [64, D])
            kvT = st.sb("kvT", [P, KD, S])
            latT = st.sb("latT", [64, S])
        if relative:
            relT = st.sb("relT", [P, 2, S])
            rel_out = st.sb("rel_out", [P, NU, HU, W])
            bias = st.sb("bias", [P, NU, HU, W])
            rel_dram = nc.dram_tensor(f"{name}_rel", (NU, HU, TS, P, S), F32).ap()
            rel_done, bias_ready = st.sem("rel_done"), st.sem("bias_ready")
            rel_ready = [st.sem(f"rel_ready_{e}") for e in ("dve", "act")]
            rel_sent = [st.sem(f"rel_sent{u}") for u in range(NU)]
            bias_in = [st.sem(f"bias_in{u}") for u in range(NU)]
        sc_free = exp_done if kind == "plain" else max_ready
        block = st.block()
        loads = [(weights[:, n, :, :], f"w{m}") for n, m in enumerate("qkvo")] + ([(wdown[:, :, :], "wdown")] if latent else [])
        flat = [(bqk, "bqk"), (parity, "parity")] + ([(wupk, "wupk"), (wupv, "wupv")] if latent else [])
        flat += ([(relT, "relT")] if relative else []) + ([(matrix, "matrix")] if kind != "plain" else [])
        NW = len(loads) + len(flat) + 2

        def rows(u, t, ap, first):
            block_u = rel_dram[u, 0, t]
            return bass.AP(block_u.tensor, block_u.offset + first, ap)

        @block.sync
        def _(sp):
            for t, n in loads:
                sp.dma_start(t, dram[f"{name}_{n}"].rearrange("(k p) n -> p k n", p=P)).then_inc(w_in, 16)
            for t, n in flat:
                a = dram[f"{name}_{n}" if n != "parity" else "parity"]
                sp.dma_start(t[(slice(None),) * len(a.shape)], a).then_inc(w_in, 16)
            sp.dma_start(bv[:, :], dram[f"{name}_bv"].partition_broadcast(P)).then_inc(w_in, 16)
            sp.dma_start(bo[:, :], dram[f"{name}_bo"].partition_broadcast(P)).then_inc(w_in, 16)
            if relative:
                with sp.Fori(0, B + 1) as b:
                    for u in range(NU + 2):
                        if u < NU:
                            sp.wait_ge(rel_ready[u % 2], at(NU // 2 * b + u // 2 + 1))
                            for t, w in enumerate(width):
                                sp.dma_start(rows(u, t, [[w, P], [TS * P * S, HU], [1, w]], 0),
                                             rel_out[:, u, :, off[t]:off[t] + w]).then_inc(rel_sent[u], 16)
                        if u >= 2:
                            r = u - 2
                            if r == 0:
                                sp.wait_ge(max_ready, at(NU * b))
                            sp.wait_ge(rel_sent[r], 16 * TS * (b + 1))
                            for t, w in enumerate(width):
                                sp.dma_start(bias[:, r, :, off[t]:off[t] + w],
                                             rows(r, t, [[w - 1, P], [TS * P * S, HU], [1, w]], P - 1)).then_inc(bias_in[r], 16)

        @block.tensor
        def _(pe):
            opened(pe, m_done, sc_done, t_done, av_done)
            if relative:
                opened(pe, rel_done)
            pe.wait_ge(w_in, 16 * NW)

            def product(out, lhs, rhs, first=True, last_one=True):
                for n, (a, b) in enumerate(PARTS):
                    ins = nc.tensor.matmul(out, lhs(a), rhs(b), start=first and n == 0, stop=last_one and n == len(PARTS) - 1)
                return ins

            def step(b, o, k):
                what = steps[k][0]
                if not (isinstance(b, int) and b == BEFORE and k == 0):
                    pe.wait_ge(m_read[steps[k - 1][1]], read(b, k - 1, steps[k - 1][1]))
                need = {"kv": 0, "lat": 1, "q": 0, "k": 2 if latent else 0, "t": NP + 1, "y": NP + 2}.get(what)
                if need is not None and need != k - 1:
                    pe.wait_ge(m_read[steps[need][1]], read(b, need, steps[need][1]))
                if what == "x":
                    pe.wait_ge(xn_ready, at(b + 2))
                    for c in range(KD):
                        for s in range(TS):
                            last = nc.tensor.transpose(m_ps[:, c * S + s * P:c * S + (s + 1) * P],
                                                       xn[:, s, c * P:(c + 1) * P], ident[:, :])
                elif what == "kv":
                    for m in range(KD):
                        for n, w in enumerate((WK, WV)):
                            for c in range(KD):
                                last = product(m_ps[:, m * S:(m + 1) * S], lambda a: w_parts[a][:, w, c, m * P:(m + 1) * P],
                                               lambda b: xT[b][:, c, :], n + c == 0, n == 1 and c == KD - 1)
                elif what == "lat":
                    for c in range(KD):
                        last = nc.tensor.matmul(m_ps[0:64, 0:S], wdown[:, c, :], kvT[:, c, :], start=(c == 0), stop=(c == KD - 1))
                elif what == "k" and latent:
                    for m in range(KD):
                        last = nc.tensor.matmul(m_ps[:, m * S:(m + 1) * S], wupk[:, m * P:(m + 1) * P], latT[:, :], start=True, stop=True)
                elif what == "v" and latent:
                    for s in range(TS):
                        last = nc.tensor.matmul(m_ps[:, s * D:(s + 1) * D], latT[:, s * P:(s + 1) * P], wupv[:, :], start=True, stop=True)
                elif what in ("q", "k"):
                    w = WQ if what == "q" else WK
                    for m in range(KD):
                        for c in range(KD):
                            last = product(m_ps[:, m * S:(m + 1) * S], lambda a: w_parts[a][:, w, c, m * P:(m + 1) * P],
                                           lambda b: xT[b][:, c, :], c == 0, c == KD - 1)
                elif what == "v":
                    for s in range(TS):
                        for c in range(KD):
                            last = product(m_ps[:, s * D:(s + 1) * D], lambda a: xT[a][:, c, s * P:(s + 1) * P],
                                           lambda b: w_parts[b][:, WV, c, :], c == 0, c == KD - 1)
                elif what in ("o0", "o1"):
                    s = int(what[1])
                    pe.wait_ge(o_ready, at(NSETS * b))
                    for g in range(NSETS):
                        last = nc.tensor.transpose(m_ps[:, g * P:(g + 1) * P], oT[:, 1 - o, g, s * P:(s + 1) * P], ident[:, :])
                elif what == "t":
                    for c in range(KD):
                        for s in range(TS):
                            last = nc.tensor.transpose(m_ps[:, c * S + s * P:c * S + (s + 1) * P],
                                                       on[:, s, c * 8:(c + 1) * 8, :].rearrange("p h d -> p (h d)"), ident[:, :])
                else:
                    for s in range(TS):
                        for c in range(KD):
                            last = product(m_ps[:, s * D:(s + 1) * D], lambda a: onT[a][:, c, s * P:(s + 1) * P],
                                           lambda b: w_parts[b][:, WO, c, :], c == 0, c == KD - 1)
                last.then_inc(m_done, 1)

            def tile(u, j):
                r = HU * (u % 2) + j
                return r, slice(32 * r, 32 * r + 32)

            def scores(b, o, u):
                if u == 0:
                    for n in ("q", "k"):
                        k = [x for x, _ in steps].index(n)
                        pe.wait_ge(m_read[steps[k][1]], read(b - 1, k, steps[k][1]))
                if not (isinstance(b, int) and u < 2):
                    pe.wait_ge(sc_free, at(NU * b + u - 1))
                for s in range(TS):
                    for j in range(HU):
                        r, part = tile(u, j)
                        last = nc.tensor.matmul(sc_ps[:, r, off[s]:off[s] + width[s]],
                                                qT[part, o, u // 4, s * P:(s + 1) * P],
                                                kT[part, o, (u // 2) % 2, u // 4, 0:width[s]], start=True, stop=True)
                last.then_inc(sc_done, 1)

            def rel_products(b, o, u):
                if u < 2:
                    if not isinstance(b, int):
                        pe.wait_ge(max_ready, at(NU * b - 1 + u))
                    pe.wait_ge(m_read["act"], read(b - 1, [x for x, _ in steps].index("q"), "act"))
                else:
                    pe.wait_ge(rel_ready[u % 2], at(NU // 2 * b + u // 2))
                for s in range(TS):
                    for j in range(HU):
                        r, part = tile(u, j)
                        last = nc.tensor.matmul(sc_ps[:, r, off[s]:off[s] + width[s]],
                                                qT[part, o, u // 4, s * P:(s + 1) * P],
                                                relT[part, (u // 2) % 2, S - width[s]:S], start=True, stop=True)
                last.then_inc(rel_done, 1)

            def all_rel_read(b):
                for n in range(2):
                    pe.wait_ge(rel_ready[n], at(NU // 2 * (b + 1)))

            def transpose_weights(b, u):
                n = NU * b + u
                pe.wait_ge(exp_done, at(n + 1))
                pe.wait_ge(t_read_act, at(n))
                pe.wait_ge(t_read_dve, at(n))
                for j in range(HU):
                    for s in range(TS):
                        for k in range(width[s] // P):
                            last = nc.tensor.transpose(t_ps[:, j, k * S + s * P:k * S + (s + 1) * P],
                                                       pr[:, u % 2, j, off[s] + k * P:off[s] + (k + 1) * P], ident[:, :])
                last.then_inc(t_done, 1)

            def values(b, o, u):
                n = NU * b + u
                pe.wait_ge(t_read_act, at(n + 1))
                pe.wait_ge(t_read_dve, at(n + 1))
                if u % 2 == 0:
                    pe.wait_ge(o_ready, at(NSETS * b + u // 2))
                for k in range(TS):
                    for j in range(HU):
                        r, part = tile(u, j)
                        head = 8 * (u // 4) + (u // 2) % 2 + 2 * r
                        q0 = P * k if causal else 0
                        last = nc.tensor.matmul(o_ps[part, q0:S], v[:, o, k, head, :], prT[:, u % 2, j, k, q0:S],
                                                start=(k == 0), stop=(k == TS - 1), skip_group_check=True)
                last.then_inc(av_done, 1)

            step(BEFORE, 1, 0)
            if NPARTS == 2:
                pe.wait_ge(w_split, 1)
            for k in range(1, NP):
                step(BEFORE, 1, k)
            if relative:
                for u in range(NU):
                    rel_products(0, 0, u)
                all_rel_read(0)
            scores(0, 0, 0)
            scores(0, 0, 1)
            with pe.Fori(0, B // 2) as t:
                for o in range(2):
                    b = 2 * t + o
                    for u in range(NU):
                        transpose_weights(b, u)
                        here = [k for k in range(NS) if slot_of[k] == u]
                        for k in here[:1]:
                            step(b, o, k)
                        if u + 2 < NU:
                            scores(b, o, u + 2)
                        elif not relative:
                            scores(b + 1, 1 - o, u + 2 - NU)
                        else:
                            for n in range(NU // 2):
                                rel_products(b + 1, 1 - o, NU // 2 * (u + 2 - NU) + n)
                            if u == NU - 1:
                                all_rel_read(b + 1)
                                scores(b + 1, 1 - o, 0)
                                scores(b + 1, 1 - o, 1)
                        for k in here[1:]:
                            step(b, o, k)
                        if u >= 1:
                            values(b, o, u - 1)
                    values(b, o, NU - 1)
            for k in range(NP, NS):
                step(AFTER, 0, k)

        @block.scalar
        def _(act):
            opened(act, exp_done, t_read_act, o_ready, m_read["act"])
            if relative:
                opened(act, rel_ready[1])
            act.wait_ge(w_in, 16 * NW)
            if NPARTS == 2:
                nc.scalar.activation(w_parts[0][:, :, :, :], weights[:, :, :, :], ACT.Copy).then_inc(w_rounded, 1)
            norm.sqrt_act(act)
            act.wait_ge(cleared, 3)
            act.wait_ge(bias_scaled, 1)

            def step(b, o, k):
                what = steps[k][0]
                act.wait_ge(m_done, done(b, k))
                both = m_ps[:, :].rearrange("p (k t) -> p k t", k=KD)
                if what == "lat":
                    last = nc.scalar.activation(latT[:, :], m_ps[0:64, 0:S], ACT.Copy)
                elif what == "q":
                    for m in range(KD):
                        last = nc.scalar.activation(qT[:, 1 - o, m, :], m_ps[:, m * S:(m + 1) * S], ACT.Identity,
                                                    bias=bqk[:, 0, m:m + 1], scale=scale)
                else:
                    to = kvT if what == "kv" else xT[0] if what == "x" else onT[0]
                    last = nc.scalar.activation(to[:, :, :], both, ACT.Copy)
                last.then_inc(m_read["act"], 1)

            def exps(b, u):
                n = NU * b + u
                act.wait_ge(max_ready, at(n + 1))
                if not (isinstance(b, int) and u < 2):
                    act.wait_ge(t_done, at(n - 1))
                for j in range(HU):
                    for s, w in enumerate(width):
                        c = slice(off[s], off[s] + w)
                        if kind == "plain":
                            src, sgn = sc_ps[:, HU * (u % 2) + j, c], 1.0
                        else:
                            src, sgn = z[:, u % 2, j, c], -1.0 if kind == "add" else 1.0
                        last = nc.scalar.activation(pr[:, u % 2, j, c], src, ACT.Exp, bias=nmax[:, u % 2, j, s:s + 1], scale=sgn)
                last.then_inc(exp_done, 1)

            def copy_weights(b, u):
                n = NU * b + u
                act.wait_ge(t_done, at(n + 1))
                act.wait_ge(av_done, at(NU * b + max(0, u - 1)))
                for c in cols:
                    last = nc.scalar.activation(prT[:, u % 2, 0, :, :].rearrange("p k q -> p (k q)")[:, c], t_ps[:, 0, c], ACT.Copy)
                last.then_inc(t_read_act, 1)

            def copy_o(b, o, g):
                act.wait_ge(av_done, at(NU * b + 2 * g + 2))
                nc.scalar.activation(oT[:, o, g, :], o_ps[:, 0:S], ACT.Copy).then_inc(o_ready, 1)

            def copy_rel(b, u):
                act.wait_ge(rel_done, at(NU * b + u + 1))
                act.wait_ge(bias_ready, at(NU * b))
                nc.scalar.activation(rel_out[:, u, :, :], sc_ps[:, 2:4, 0:W], ACT.Copy).then_inc(rel_ready[1], 1)

            for k in range(NP):
                if steps[k][1] == "act":
                    step(BEFORE, 1, k)
            if relative:
                for u in range(1, NU, 2):
                    copy_rel(0, u)
            exps(0, 0)
            with act.Fori(0, B // 2) as t:
                for o in range(2):
                    b = 2 * t + o
                    for u in range(NU):
                        if relative and u >= NU - 2:
                            if u == NU - 2:
                                exps(b, u + 1)
                            copy_weights(b, u)
                            for n in range(NU // 2):
                                r = NU // 2 * (u + 2 - NU) + n
                                if r % 2 == 1:
                                    copy_rel(b + 1, r)
                            if u == NU - 1:
                                exps(b + 1, 0)
                        else:
                            copy_weights(b, u)
                            exps(b + (u + 1) // NU, (u + 1) % NU)
                        for k in range(NS):
                            if slot_of[k] == u and steps[k][1] == "act":
                                step(b, o, k)
                        if u % 2 == 0 and u >= 2:
                            copy_o(b, o, u // 2 - 1)
                    copy_o(b, o, NSETS - 1)
            for k in range(NP, NS):
                if steps[k][1] == "act":
                    step(AFTER, 0, k)

        @block.vector
        def _(dve):
            opened(dve, xn_ready, max_ready, t_read_dve, m_read["dve"])
            if relative:
                opened(dve, rel_ready[0])
            ch = Chain(dve, chain)
            norm.stats_dve(dve, ch)
            norm.apply_dve(ch, 0, lambda s: xn[:, s:s + 1, :]).then_inc(xn_ready, 1)
            dve.wait_ge(w_in, 16 * NW)
            nc.vector.tensor_scalar(bqk[:, 0, :], bqk[:, 0, :], scale, None, ALU.mult).then_inc(bias_scaled, 1)
            dve.wait_ge(cleared, 3)

            def step(ch, b, o, k):
                what = steps[k][0]
                dve.wait_ge(m_done, done(b, k))
                if what in ("x", "t"):
                    to = xT if what == "x" else onT
                    both = m_ps[:, :].rearrange("p (k t) -> p k t", k=KD)
                    ch.link(nc.vector.tensor_copy(to[0][:, :, :], both))
                    last = nc.vector.tensor_tensor(to[1][:, :, :], both, to[0][:, :, :].bitcast(F32), ALU.subtract)
                elif what == "k":
                    for m in range(KD):
                        for e in range(2):
                            last = nc.vector.tensor_scalar(kT[:, 1 - o, e, m, :], m_ps[:, m * S:(m + 1) * S],
                                                           bqk[:, 1, m:m + 1], parity[:, e:e + 1], ALU.add, ALU.mult)
                elif what == "v":
                    for s in range(TS):
                        last = nc.vector.tensor_tensor(v[:, 1 - o, s, :, 0:HD], m_ps[:, s * D:(s + 1) * D].rearrange("p (h d) -> p h d", d=HD),
                                                       bv[:, :].rearrange("p (h d) -> p h d", d=HD), ALU.add)
                elif what in ("o0", "o1"):
                    s = int(what[1])
                    heads = m_ps[:, :].rearrange("p (h c) -> p h c", c=32)
                    ch.link(nc.vector.reciprocal(rs[:, s, :], heads[:, :, HD]))
                    last = nc.vector.tensor_tensor(on[:, s, :, :], heads[:, :, 0:HD],
                                                   rs[:, s, :].rearrange("p (h a) -> p h a", a=1).broadcast_to([P, HEADS, HD]), ALU.mult)
                else:
                    dve.wait_ge(hb_ready, at(b + 1))
                    hs = h_padded[:, ds(TS * b, TS), :]
                    last = nc.vector.tensor_tensor(hs, m_ps[:, :].rearrange("p (s d) -> p s d", s=TS), hs, ALU.add)
                last.then_inc(m_read["dve"], 1)

            def maxima(ch, b, u):
                n = NU * b + u
                dve.wait_ge(sc_done, at(n + 1))
                if not (isinstance(b, int) and u < 2):
                    dve.wait_ge(exp_done, at(n - 1))
                if relative:
                    dve.wait_ge(bias_ready, at(n + 1))
                if kind == "plain":
                    nc.vector.tensor_reduce(nmax[:, u % 2, :, :], sc_ps[:, HU * (u % 2):HU * (u % 2) + HU, :].rearrange(
                        "p j (s k) -> p j s k", s=TS), AX, ALU.max, negate=True).then_inc(max_ready, 1)
                    return
                nc.vector.memset(carry[:, u:u + 1], 0.0)
                op0, op1, sgn, start = (ALU.add, ALU.min, -1.0, BIG) if kind == "add" else (ALU.mult, ALU.max, 1.0, -BIG)
                for j in range(HU):
                    for s, w in enumerate(width):
                        c = slice(off[s], off[s] + w)
                        m = bias[:, u, j, c] if relative else matrix[:, s, 0:w]
                        last = nc.vector.tensor_tensor_reduce(z[:, u % 2, j, c], sc_ps[:, HU * (u % 2) + j, c], m,
                                                              sgn, start, op0, op1, nmax[:, u % 2, j, s:s + 1])
                if kind == "mult":
                    ch.link(last)
                    last = nc.vector.tensor_scalar(nmax[:, u % 2, :, :], nmax[:, u % 2, :, :], -1.0, None, ALU.mult)
                last.then_inc(max_ready, 1)

            def copy_weights(b, u):
                n = NU * b + u
                dve.wait_ge(t_done, at(n + 1))
                dve.wait_ge(av_done, at(NU * b + max(0, u - 1)))
                for c in cols:
                    last = nc.vector.tensor_copy(prT[:, u % 2, 1, :, :].rearrange("p k q -> p (k q)")[:, c], t_ps[:, 1, c])
                last.then_inc(t_read_dve, 1)

            def copy_rel(b, u):
                dve.wait_ge(rel_done, at(NU * b + u + 1))
                dve.wait_ge(bias_ready, at(NU * b))
                nc.vector.tensor_copy(rel_out[:, u, :, :], sc_ps[:, 0:2, 0:W]).then_inc(rel_ready[0], 1)

            dve.wait_ge(m_done, at(1))
            norm.apply_dve(ch, 1, lambda s: xn[:, s:s + 1, :]).then_inc(xn_ready, 1)
            for k in range(NP):
                if steps[k][1] == "dve":
                    step(ch, BEFORE, 1, k)
            if relative:
                for u in range(0, NU, 2):
                    copy_rel(0, u)
            maxima(ch, 0, 0)
            before = ch.n
            per = 2 * (1 + 2 + (2 if NPARTS == 2 else 0) + (NU if kind == "mult" else 0))
            with dve.Fori(0, B // 2) as t:
                ch = Chain(dve, chain, before, t, per)
                for o in range(2):
                    b = 2 * t + o
                    for u in range(NU):
                        if relative and u >= NU - 2:
                            if u == NU - 2:
                                maxima(ch, b, u + 1)
                            copy_weights(b, u)
                            for n in range(NU // 2):
                                r = NU // 2 * (u + 2 - NU) + n
                                if r % 2 == 0:
                                    copy_rel(b + 1, r)
                            if u == NU - 1:
                                maxima(ch, b + 1, 0)
                        else:
                            maxima(ch, b + (u + 1) // NU, (u + 1) % NU)
                            copy_weights(b, u)
                        for k in range(NS):
                            if slot_of[k] == u and steps[k][1] == "dve":
                                step(ch, b, o, k)
                        if u == 2:
                            dve.wait_ge(m_done, done(b, 0))
                            norm.apply_dve(ch, b + 2, lambda s: xn[:, s:s + 1, :]).then_inc(xn_ready, 1)
                ch.done(before)
            ch = Chain(dve, chain, before + per * (B // 2))
            for k in range(NP, NS):
                if steps[k][1] == "dve":
                    step(ch, AFTER, 0, k)

        @block.gpsimd
        def _(pool):
            opened(pool, hb_ready)
            if relative:
                opened(pool, bias_ready)
            nc.gpsimd.memset(v[:, :, :, :, :], 0.0).then_inc(cleared, 1)
            nc.gpsimd.memset(h_padded[:, 0:TS, :], 0.0)
            nc.gpsimd.memset(oT[:, :, :, :], 1.0).then_inc(cleared, 1)
            pool.wait_ge(cleared, 2)
            nc.gpsimd.memset(v[:, :, :, :, HD:HD + 1], 1.0).then_inc(cleared, 1)
            pool.wait_ge(w_in, 16 * NW)
            if NPARTS == 2:
                pool.wait_ge(w_rounded, 1)
                nc.gpsimd.tensor_tensor(w_parts[1][:, :, :, :], weights[:, :, :, :], w_parts[0][:, :, :, :].bitcast(F32),
                                        ALU.subtract).then_inc(w_split, 1)

            def add_mask(b):
                for u in range(NU):
                    pool.wait_ge(bias_in[u], 16 * TS * (b + 1))
                    for s, w in enumerate(width):
                        c = slice(off[s], off[s] + w)
                        last = nc.gpsimd.tensor_tensor(bias[:, u, :, c], bias[:, u, :, c],
                                                       matrix[:, s:s + 1, 0:w].broadcast_to([P, HU, w]), ALU.add)
                    last.then_inc(bias_ready, 1)

            with pool.Fori(0, B + 1) as b:
                pool.wait_ge(xn_ready, at(b + 1))
                for s in range(TS):
                    hs = h_padded[:, ds(TS * b + s, 1), :]
                    last = nc.gpsimd.tensor_tensor(hs, hs, bo[:, :].rearrange("p (a d) -> p a d", a=1), ALU.add)
                last.then_inc(hb_ready, 1)
                if relative:
                    add_mask(b)


def ternary_mlp(nc, dram, h, ident):
    FF = 4 * D
    KF = FF // P
    with Stage(nc, "f0") as st:
        fc3 = st.sb("fc3", [P, KD, FF], F32R)
        proj3 = st.sb("proj3", [P, KF, D], F32R)
        low = st.sb("low", [P, KF * S])
        gT_full = st.sb("gT_full", [P, 2, KF, S])
        lnwb = st.sb("lnwb", [P, 2, KF])
        ones = st.sb("ones", [P, P])
        sizes = st.sb("sizes", [P, 2])
        limit = st.sb("limit", [P, 2, 2])
        xn = st.sb("xn", [P, TS, D])
        xT = [st.sb(f"xT{part}", [P, 2, KD, S], F32R) for part in range(2)]
        g = st.sb("g", [P, TILES + PAD, FF])
        gstats = st.sb("gstats", [P, 2, TS, 2, 6])
        gmv = st.sb("gmv", [P, 2, TS, 2])
        gmr = st.sb("gmr", [P, TILES + PAD, 2])
        gstd = st.sb("gstd", [P, TILES])
        gcur = st.sb("gcur", [P, TS, 2])
        gate = st.sb("gate", [P, 1])
        gn = st.sb("gn", [P, TS, FF])
        wfc = g[:, 0:2, :]
        wproj = g[:, 2:4, :].rearrange("p a n -> p (a n)").rearrange("p (k n) -> p k n", k=KF)
        gT = [st.sb(f"gT{part}", [P, 2, KF, S], F32R) for part in range(2)]
        b_ps = [st.ps(f"b{n}") for n in range(4)]
        t_ps = st.ps("t")
        y_ps = st.ps("y")
        norm = Norm(nc, st, h)

        w_in, chain, sizes_ready, total_done, w_ready = (st.sem(n) for n in ("w_in", "chain", "sizes_ready", "total_done", "w_ready"))
        xn_ready, xt_done, xt_ready, fc_done, g_ready = (st.sem(n) for n in ("xn_ready", "xt_done", "xt_ready", "fc_done", "g_ready"))
        gvar_ready, gstd_ready = st.sem("gvar_ready"), st.sem("gstd_ready")
        gn_ready, gt_done, gt_full, gt_act, gt_parts, y_done, h_ready = (
            st.sem(n) for n in ("gn_ready", "gt_done", "gt_full", "gt_act", "gt_parts", "y_done", "h_ready"))
        block = st.block()
        NW = 3

        @block.sync
        def _(sp):
            sp.dma_start(wfc[:, :, :], dram["f0_wfcT"].rearrange("(k p) n -> p k n", p=P)).then_inc(w_in, 16)
            sp.dma_start(wproj[:, :, :], dram["f0_wprojT"].rearrange("(k p) n -> p k n", p=P)).then_inc(w_in, 16)
            sp.dma_start(lnwb[:, :, :], dram["f0_lnwb"]).then_inc(w_in, 16)

        @block.tensor
        def _(pe):
            opened(pe, xt_done, fc_done, gt_done, y_done)
            pe.wait_ge(sizes_ready, 1)
            nc.tensor.matmul(y_ps[:, 0:2], ones[:, :], sizes[:, :], start=True, stop=True).then_inc(total_done, 1)

            def transpose_x(n):
                pe.wait_ge(xn_ready, at(n + 1))
                pe.wait_ge(xt_ready, at(n))
                for k in range(KD):
                    for s in range(TS):
                        last = nc.tensor.transpose(t_ps[:, k * S + s * P:k * S + (s + 1) * P],
                                                   xn[:, s, k * P:(k + 1) * P], ident[:, :])
                last.then_inc(xt_done, 1)

            transpose_x(0)
            pe.wait_ge(w_ready, 1)
            with pe.Fori(0, B // 2) as t:
                for o in range(2):
                    i = 2 * t + o
                    transpose_x(i + 1)
                    for s in range(TS):
                        pe.wait_ge(g_ready, at(TS * i))
                        for n in range(2):
                            for k in range(KD):
                                for part in range(2):
                                    last = nc.tensor.matmul(b_ps[2 * s + n][:, :], xT[part][:, o, k, s * P:(s + 1) * P],
                                                            fc3[:, k, n * 512:(n + 1) * 512],
                                                            start=(k + part == 0), stop=(k + part == KD))
                        last.then_inc(fc_done, 1)
            pe.wait_ge(g_ready, at(TILES))

            def transpose_g(n, o):
                pe.wait_ge(gn_ready, at(n + 1))
                pe.wait_ge(gt_full, at(n))
                for k in range(KF):
                    for s in range(TS):
                        last = nc.tensor.transpose(b_ps[k // 2][:, (k % 2) * S + s * P:(k % 2) * S + (s + 1) * P],
                                                   gn[:, s, k * P:(k + 1) * P], ident[:, :])
                last.then_inc(gt_done, 1)

            transpose_g(0, 0)
            with pe.Fori(0, B // 2) as i:
                for o in range(2):
                    b = 2 * i + o
                    transpose_g(b + 1, 1 - o)
                    pe.wait_ge(h_ready, at(b))
                    pe.wait_ge(gt_parts, at(b + 1))
                    for s in range(TS):
                        for k in range(KF):
                            for part in range(2):
                                last = nc.tensor.matmul(y_ps[:, s * D:(s + 1) * D], gT[part][:, o, k, s * P:(s + 1) * P],
                                                        proj3[:, k, :], start=(k + part == 0), stop=(k + part == KF))
                    last.then_inc(y_done, 1)

        @block.scalar
        def _(act):
            opened(act, g_ready, gt_full, gt_act)
            norm.sqrt_act(act)

            with act.Fori(0, B) as i:
                for s in range(TS):
                    act.wait_ge(fc_done, at(TS * i + s + 1))
                    for n in range(2):
                        last = nc.scalar.activation(g[:, ds(TS * i + s, 1), n * 512:(n + 1) * 512],
                                                    b_ps[2 * s + n][:, :].rearrange("p (a n) -> p a n", a=1), ACT.Gelu)
                    last.then_inc(g_ready, 1)
            act.wait_ge(gvar_ready, 1)
            nc.scalar.activation(gstd[:, :], gstd[:, :], ACT.Sqrt).then_inc(gstd_ready, 1)

            def copy_g(n, o):
                act.wait_ge(gt_done, at(n + 1))
                if not isinstance(n, int):
                    act.wait_ge(gt_parts, at(n - 1))
                for k in range(KF):
                    last = nc.scalar.activation(gT_full[:, o, k, :], b_ps[k // 2][:, (k % 2) * S:(k % 2 + 1) * S], ACT.Identity,
                                                bias=lnwb[:, 1, k:k + 1], scale=lnwb[:, 0, k:k + 1])
                last.then_inc(gt_full, 1)
                act.wait_ge(gt_full, at(n + 1))
                if not isinstance(n, int):
                    act.wait_ge(y_done, at(n - 1))
                nc.scalar.activation(gT[0][:, o, :, :], gT_full[:, o, :, :], ACT.Copy).then_inc(gt_act, 1)

            copy_g(0, 0)
            with act.Fori(0, B // 2) as i:
                for o in range(2):
                    copy_g(2 * i + o + 1, 1 - o)

        @block.vector
        def _(dve):
            opened(dve, xt_ready, xn_ready, gn_ready, gt_parts, h_ready)
            ch = Chain(dve, chain)
            nc.vector.memset(ones[:, :], 1.0)
            nc.vector.memset(g[:, TILES:TILES + PAD, :], 0.0)
            nc.vector.memset(gmr[:, TILES:TILES + PAD, :], 0.0)
            norm.stats_dve(dve, ch)
            dve.wait_ge(w_in, 16 * NW)
            for n, w in enumerate((wfc, wproj)):
                last = nc.vector.tensor_reduce(sizes[:, n:n + 1], w[:, :, :].rearrange("p k n -> p (k n)"), AX, ALU.add,
                                               apply_absolute_value=True)
            last.then_inc(sizes_ready, 1)
            norm.apply_dve(ch, 0, lambda s: xn[:, s:s + 1, :]).then_inc(xn_ready, 1)
            dve.wait_ge(total_done, 1)
            ch.link(nc.vector.tensor_scalar(limit[:, 0, :], y_ps[:, 0:2], 1.0 / (D * FF), 1e-6, ALU.mult, ALU.add))
            ch.link(nc.vector.tensor_scalar(limit[:, 0, :], limit[:, 0, :], 0.5, None, ALU.mult))
            ch.link(nc.vector.tensor_scalar(limit[:, 1, :], limit[:, 0, :], -1.0, None, ALU.mult))
            for n, (w, w3) in enumerate(((wfc, fc3), (wproj, proj3))):
                flat = w[:, :, :].rearrange("p k n -> p (k n)")
                ch.link(nc.vector.tensor_scalar(low[:, :], flat, limit[:, 1, n:n + 1], None, ALU.is_lt))
                last = nc.vector.scalar_tensor_tensor(w3[:, :, :].rearrange("p k n -> p (k n)"), flat, limit[:, 0, n:n + 1], low[:, :],
                                                      ALU.is_gt, ALU.subtract)
                if n == 0:
                    ch.link(last)
            last.then_inc(w_ready, 1)

            def parts_of_x(ch, n, o):
                x_ps = t_ps[:, :].rearrange("p (k t) -> p k t", k=KD)
                dve.wait_ge(xt_done, at(n + 1))
                if not isinstance(n, int):
                    dve.wait_ge(fc_done, at(TS * (n - 1)))
                ch.link(nc.vector.tensor_copy(xT[0][:, o, :, :], x_ps))
                nc.vector.tensor_tensor(xT[1][:, o, :, :], x_ps, xT[0][:, o, :, :].bitcast(F32), ALU.subtract).then_inc(xt_ready, 1)

            parts_of_x(ch, 0, 0)
            norm.apply_dve(ch, 1, lambda s: xn[:, s:s + 1, :]).then_inc(xn_ready, 1)
            before = ch.n
            per = 2 * (2 + 3)
            with dve.Fori(0, B // 2) as t:
                ch = Chain(dve, chain, before, t, per)
                for o in range(2):
                    i = 2 * t + o
                    parts_of_x(ch, i + 1, 1 - o)
                    norm.apply_dve(ch, i + 2, lambda s: xn[:, s:s + 1, :]).then_inc(xn_ready, 1)
                    for s in range(TS):
                        dve.wait_ge(g_ready, at(TS * i + s + 1))
                        for n in range(2):
                            last = nc.vector.bn_stats(gstats[:, 0, s, n, :], g[:, ds(TS * i + s, 1), n * 512:(n + 1) * 512])
                    ch.link(last)
                    nc.vector.memset(gate[:, :], 0.0)
                    for s in range(TS):
                        last = nc.vector.bn_aggr(gmv[:, 0, s, :], gstats[:, 0, s, :, :])
                    ch.link(last)
                    ch.link(nc.vector.tensor_copy(gmr[:, ds(TS * i, TS), :], gmv[:, 0, :, :]))
                ch.done(before)
            before2 = before + per * (B // 2)
            ch = Chain(dve, chain, before2)
            nc.vector.tensor_scalar(gstd[:, :], gmr[:, 0:TILES, 1], EPS, None, ALU.add).then_inc(gvar_ready, 1)
            dve.wait_ge(gstd_ready, 1)
            ch.link(nc.vector.reciprocal(gmr[:, 0:TILES, 1], gstd[:, :]))

            def normalize_g(n):
                dve.wait_ge(gn_ready, at(n))
                ch.link(nc.vector.tensor_copy(gcur[:, :, :], gmr[:, ds(TS * n, TS), :]))
                dve.wait_ge(gt_done, at(n))
                for s in range(TS):
                    last = nc.vector.tensor_scalar(gn[:, s:s + 1, :], g[:, ds(TS * n + s, 1), :], gcur[:, s, 0:1],
                                                   gcur[:, s, 1:2], ALU.subtract, ALU.mult)
                last.then_inc(gn_ready, 1)

            def parts_of_g(n, o):
                dve.wait_ge(gt_act, at(n + 1))
                if not isinstance(n, int):
                    dve.wait_ge(y_done, at(n - 1))
                nc.vector.tensor_tensor(gT[1][:, o, :, :], gT_full[:, o, :, :], gT[0][:, o, :, :].bitcast(F32), ALU.subtract).then_inc(gt_parts, 1)

            normalize_g(0)
            parts_of_g(0, 0)
            normalize_g(1)
            before3 = ch.n
            per = 2
            with dve.Fori(0, B // 2) as i:
                ch = Chain(dve, chain, before3, i, per)
                for o in range(2):
                    b = 2 * i + o
                    normalize_g(b + 2)
                    parts_of_g(b + 1, 1 - o)
                    dve.wait_ge(y_done, at(b + 1))
                    for s in range(TS):
                        hs = h[:, ds(TS * b + s, 1), :]
                        last = nc.vector.tensor_tensor(hs, y_ps[:, s * D:(s + 1) * D].rearrange("p (a d) -> p a d", a=1),
                                                       hs, ALU.add)
                    last.then_inc(h_ready, 1)
                ch.done(before3)


def channel_mixer(nc, dram, h, ident):
    with Stage(nc, "f1") as st:
        w = st.sb("w", [P, 3, KD, D])
        mu = st.sb("mu", [P, 2, 2, KD])
        xn = st.sb("xn", [P, TS, D])
        xT = st.sb("xT", [P, KD, S + 1])
        part = st.sb("part", [P, 2, KD, S])
        mixed = st.sb("mixed", [P, 2, KD, S])
        r = st.sb("r", [P, TS, D])
        kr = st.sb("kr", [P, KD, S])
        k2 = st.sb("k2", [P, KD, S])
        o = st.sb("o", [P, TS, D])
        t_ps, r_ps, k_ps, v_ps = (st.ps(n) for n in ("t", "r", "k", "v"))
        norm = Norm(nc, st, h)
        w_in, chain, xn_ready, xt_done, xt_ready, mixed_ready = (
            st.sem(n) for n in ("w_in", "chain", "xn_ready", "xt_done", "xt_ready", "mixed_ready"))
        r_done, k_done, r_ready, kr_ready, k2_ready, v_done, o_ready, h_ready = (
            st.sem(n) for n in ("r_done", "k_done", "r_ready", "kr_ready", "k2_ready", "v_done", "o_ready", "h_ready"))
        block = st.block()
        NW = 4

        @block.sync
        def _(sp):
            for n, name in enumerate(("wr", "wk", "wv")):
                sp.dma_start(w[:, n, :, :], dram[f"f1_{name}T"].rearrange("(k p) n -> p k n", p=P)).then_inc(w_in, 16)
            sp.dma_start(mu[:, 0, :, :], dram["f1_mu"]).then_inc(w_in, 16)

        @block.tensor
        def _(pe):
            opened(pe, xt_done, r_done, k_done, v_done)
            pe.wait_ge(w_in, 16 * NW)

            def transpose_x(n):
                pe.wait_ge(xn_ready, at(n + 1))
                pe.wait_ge(xt_ready, at(n))
                for k in range(KD):
                    for s in range(TS):
                        last = nc.tensor.transpose(t_ps[:, k * S + s * P:k * S + (s + 1) * P],
                                                   xn[:, s, k * P:(k + 1) * P], ident[:, :])
                last.then_inc(xt_done, 1)

            transpose_x(0)
            with pe.Fori(0, B) as i:
                transpose_x(i + 1)
                pe.wait_ge(mixed_ready, at(i + 1))
                pe.wait_ge(kr_ready, at(i))
                for m in range(KD):
                    for k in range(KD):
                        last = nc.tensor.matmul(k_ps[:, m * S:(m + 1) * S], w[:, 1, k, m * P:(m + 1) * P],
                                                mixed[:, 1, k, :], start=(k == 0), stop=(k == KD - 1))
                last.then_inc(k_done, 1)
                pe.wait_ge(r_ready, at(i))
                for s in range(TS):
                    for k in range(KD):
                        last = nc.tensor.matmul(r_ps[:, s * D:(s + 1) * D], mixed[:, 0, k, s * P:(s + 1) * P],
                                                w[:, 0, k, :], start=(k == 0), stop=(k == KD - 1))
                last.then_inc(r_done, 1)
                pe.wait_ge(k2_ready, at(i + 1))
                pe.wait_ge(o_ready, at(i))
                for s in range(TS):
                    for k in range(KD):
                        last = nc.tensor.matmul(v_ps[:, s * D:(s + 1) * D], k2[:, k, s * P:(s + 1) * P],
                                                w[:, 2, k, :], start=(k == 0), stop=(k == KD - 1))
                last.then_inc(v_done, 1)

        @block.scalar
        def _(act):
            opened(act, xt_ready, kr_ready, r_ready)
            norm.sqrt_act(act)

            def copy_x(n):
                act.wait_ge(xt_done, at(n + 1))
                act.wait_ge(mixed_ready, at(n))
                nc.scalar.activation(xT[:, :, 1:S + 1], t_ps[:, :].rearrange("p (k t) -> p k t", k=KD), ACT.Copy)\
                    .then_inc(xt_ready, 1)

            copy_x(0)
            with act.Fori(0, B) as i:
                copy_x(i + 1)
                act.wait_ge(k_done, at(i + 1))
                act.wait_ge(k2_ready, at(i))
                nc.scalar.activation(kr[:, :, :], k_ps[:, :].rearrange("p (k t) -> p k t", k=KD), ACT.Relu)\
                    .then_inc(kr_ready, 1)
                act.wait_ge(r_done, at(i + 1))
                act.wait_ge(o_ready, at(i))
                nc.scalar.activation(r[:, :, :], r_ps[:, :].rearrange("p (s d) -> p s d", s=TS), ACT.Sigmoid)\
                    .then_inc(r_ready, 1)

        @block.vector
        def _(dve):
            opened(dve, xn_ready, mixed_ready, o_ready)
            ch = Chain(dve, chain)
            nc.vector.memset(xT[:, :, 0:1], 0.0)
            norm.stats_dve(dve, ch)
            dve.wait_ge(w_in, 16 * NW)
            ch.link(nc.vector.tensor_scalar(mu[:, 1, :, :], mu[:, 0, :, :], -1.0, 1.0, ALU.mult, ALU.add))
            norm.apply_dve(ch, 0, lambda s: xn[:, s:s + 1, :]).then_inc(xn_ready, 1)

            def mix(n):
                dve.wait_ge(xt_ready, at(n + 1))
                for m in range(2):
                    for k in range(KD):
                        last = nc.vector.tensor_scalar(part[:, m, k, :], xT[:, k, 0:S], mu[:, 1, m, k:k + 1], None, ALU.mult)
                ch.link(last)
                dve.wait_ge(r_done, at(n))
                for m in range(2):
                    for k in range(KD):
                        last = nc.vector.scalar_tensor_tensor(mixed[:, m, k, :], xT[:, k, 1:S + 1], mu[:, 0, m, k:k + 1],
                                                              part[:, m, k, :], ALU.mult, ALU.add)
                last.then_inc(mixed_ready, 1)

            def next_x(n):
                dve.wait_ge(xt_done, at(n))
                norm.apply_dve(ch, n, lambda s: xn[:, s:s + 1, :]).then_inc(xn_ready, 1)

            dve.wait_ge(xt_done, at(1))
            norm.apply_dve(ch, 1, lambda s: xn[:, s:s + 1, :]).then_inc(xn_ready, 1)
            mix(0)
            before = ch.n
            per = 2
            with dve.Fori(0, B) as i:
                ch = Chain(dve, chain, before, i, per)
                next_x(i + 2)
                mix(i + 1)
                dve.wait_ge(v_done, at(i + 1))
                dve.wait_ge(r_ready, at(i + 1))
                dve.wait_ge(h_ready, at(i))
                nc.vector.tensor_tensor(o[:, :, :], v_ps[:, :].rearrange("p (s d) -> p s d", s=TS), r[:, :, :], ALU.mult)\
                    .then_inc(o_ready, 1)
                ch.done(before)

        @block.gpsimd
        def _(pool):
            opened(pool, k2_ready, h_ready)
            with pool.Fori(0, B) as i:
                pool.wait_ge(kr_ready, at(i + 1))
                pool.wait_ge(v_done, at(i))
                nc.gpsimd.tensor_tensor(k2[:, :, :], kr[:, :, :], kr[:, :, :], ALU.mult).then_inc(k2_ready, 1)
                pool.wait_ge(o_ready, at(i + 1))
                hs = h[:, ds(TS * i, TS), :]
                nc.gpsimd.tensor_tensor(hs, hs, o[:, :, :], ALU.add).then_inc(h_ready, 1)


def expert_choice(nc, dram, h, ident):
    E = 16
    CAP = int(S * 2.0 / E)
    FF = 512
    KF = FF // P
    EG = P // CAP
    NEG_E = E // EG
    BG = P // CAP
    with Stage(nc, "moe") as st:
        gate = st.sb("gate", [P, KD, E])
        iota = st.sb("iota", [P, 1, CAP])
        xn = st.sb("xn", [P, TS, D])
        xTb = st.sb("xTb", [P, KD, S])
        xT = st.sb("xT", [P, KD, B * S])
        sc = st.sb("sc", [P, TS, B, E])
        smax = st.sb("smax", [P, TS * B])
        ssum = st.sb("ssum", [P, TS * B])
        work = st.sb("work", [P, S])
        top8 = st.sb("top8", [P, 8])
        taken = st.sb("taken", [P, S])
        zeros = st.sb("zeros", [P, S])
        slot = st.sb("slot", [P, S])
        slotT = st.sb("slotT", [P, TS, B + 1, E])
        xn_parts = [st.sb(f"xn{part}", [P, 2, TS, D], F32R) for part in range(2)]
        pick = st.sb("pick", [P, 2, TS, E, CAP], F32R)
        pickw = st.sb("pickw", [P, TS, E, CAP])
        xg = st.sb("xg", [P, KD, E, B, CAP])
        back = st.sb("back", [P, B, NEG_E, S])
        backb = st.sb("backb", [P, NEG_E, S])
        wx = [st.sb(f"wx{n}", [P, 2 * KD * FF + KF * D]) for n in range(2)]
        act_g = st.sb("act_g", [P, KF, S])
        hT = st.sb("hT", [P, KF, S])
        eo = st.sb("eo", [P, 2, B // BG, D])
        eo2 = st.sb("eo2", [P, NEG_E, B, D])
        g_ps = [st.ps(f"g{n}") for n in range(2)]
        u_ps = [st.ps(f"u{n}") for n in range(2)]
        e_ps = st.ps("e", (P, 2, 512))
        t_ps = st.ps("t")
        l_ps = st.ps("l")
        norm = Norm(nc, st, h)

        w_in, chain, xn_ready, xt_done, xt_ready, xall_ready, lg_done, lg_ready = (
            st.sem(n) for n in ("w_in", "chain", "xn_ready", "xt_done", "xt_ready", "xall_ready", "lg_done", "lg_ready"))
        less_max, exp_ready, sc_ready, scT_done, slot_ready, slotT_done = (
            st.sem(n) for n in ("less_max", "exp_ready", "sc_ready", "scT_done", "slot_ready", "slotT_done"))
        xg_xn_ready, pick_ready, pickw_ready, gather_done, gather_act, gather_dve, back_done, back_act, back_dve = (
            st.sem(n) for n in ("xg_xn_ready", "pick_ready", "pickw_ready", "gather_done", "gather_act", "gather_dve",
                                "back_done", "back_act", "back_dve"))
        gu_done, gelu_ready, hT_ready, eo_done, eo_ready = (
            st.sem(n) for n in ("gu_done", "gelu_ready", "hT_ready", "eo_done", "eo_ready"))
        wx_in = [st.sem(f"wx{n}_in") for n in range(2)]
        eo_sent = [st.sem(f"eo_sent{n}") for n in range(2)]
        backb_ready, y_done, h_ready = st.sem("backb_ready"), st.sem("y_done"), st.sem("h_ready")
        block = st.block()
        NW = 2

        def weights(n):
            a = KD * FF
            return (wx[n][:, 0:a].rearrange("p (k f) -> p k f", k=KD), wx[n][:, a:2 * a].rearrange("p (k f) -> p k f", k=KD),
                    wx[n][:, 2 * a:].rearrange("p (k d) -> p k d", k=KF))

        @block.sync
        def _(sp):
            sp.dma_start(gate[:, :, :], dram["moe_gateT"].rearrange("(k p) n -> p k n", p=P)).then_inc(w_in, 16)
            sp.dma_start(iota[:, 0, :], dram["moe_iota"].partition_broadcast(P)).then_inc(w_in, 16)
            for e in range(2):
                sp.dma_start(wx[e][:, :], dram["moe_experts"][e]).then_inc(wx_in[e], 16)
            for s in eo_sent:
                sp.sem_inc(s, 16)
            with sp.Fori(0, NEG_E) as q:
                for e in range(EG):
                    sp.wait_ge(eo_ready, at(EG * q + e + 1))
                    for b in range(BG):
                        sp.dma_start(eo2[CAP * e:CAP * (e + 1), ds(q, 1), b:B:BG, :],
                                     eo[CAP * b:CAP * (b + 1), e % 2, :, :].rearrange("p (a b) d -> p a b d", a=1))\
                            .then_inc(eo_sent[e % 2], 16)
                    sp.dma_start(wx[e % 2][:, :], dram["moe_experts"][ds(EG * q + e + 2, 1)].rearrange("a p n -> (a p) n"))\
                        .then_inc(wx_in[e % 2], 16)

        @block.tensor
        def _(pe):
            opened(pe, xt_done, lg_done, gather_done, back_done, gu_done, eo_done, y_done)
            pe.wait_ge(w_in, 16 * NW)
            with pe.Fori(0, B) as i:
                pe.wait_ge(xn_ready, at(i + 1))
                for k in range(KD):
                    for s in range(TS):
                        last = nc.tensor.transpose(t_ps[:, k * S + s * P:k * S + (s + 1) * P],
                                                   xn[:, s, k * P:(k + 1) * P], ident[:, :])
                last.then_inc(xt_done, 1)
                pe.wait_ge(xt_ready, at(i + 1))
                pe.wait_ge(lg_ready, at(i))
                for s in range(TS):
                    for k in range(KD):
                        last = nc.tensor.matmul(l_ps[:, s * E:(s + 1) * E], xTb[:, k, s * P:(s + 1) * P], gate[:, k, :],
                                                start=(k == 0), stop=(k == KD - 1))
                last.then_inc(lg_done, 1)
            pe.wait_ge(sc_ready, 1)
            for s in range(TS):
                last = nc.tensor.transpose(l_ps[:, s * P:(s + 1) * P], sc[:, s, :, :].rearrange("p b e -> p (b e)"), ident[:, :])
            last.then_inc(scT_done, 1)
            pe.wait_ge(slot_ready, 1)
            for s in range(TS):
                last = nc.tensor.transpose(l_ps[:, s * P:(s + 1) * P], slot[:, s * P:(s + 1) * P], ident[:, :])
            last.then_inc(slotT_done, 1)
            with pe.Fori(0, B // 2) as t:
                for o in range(2):
                    i = 2 * t + o
                    pe.wait_ge(xg_xn_ready, at(i + 1))
                    pe.wait_ge(pick_ready, at(i + 1))
                    pe.wait_ge(gather_act, at(i))
                    pe.wait_ge(gather_dve, at(i))
                    for k in range(KD):
                        for s in range(TS):
                            for part in range(2):
                                last = nc.tensor.matmul(g_ps[k][:, :], xn_parts[part][:, o, s, k * P:(k + 1) * P],
                                                        pick[:, o, s, :, :].rearrange("p e c -> p (e c)"),
                                                        start=(s + part == 0), stop=(s + part == TS))
                    last.then_inc(gather_done, 1)
                    pe.wait_ge(pickw_ready, at(i + 1))
                    pe.wait_ge(back_act, at(i))
                    pe.wait_ge(back_dve, at(i))
                    for q in range(NEG_E):
                        for s in range(TS):
                            last = nc.tensor.transpose(
                                u_ps[q // 2][:, (q % 2) * S + s * P:(q % 2) * S + (s + 1) * P],
                                pickw[:, s, EG * q:EG * (q + 1), :].rearrange("p e c -> p (e c)"), ident[:, :])
                    last.then_inc(back_done, 1)

            def gate_up(w, x, n):
                for m in range(2):
                    pe.wait_ge(gelu_ready, at(2 * n))
                    pe.wait_ge(hT_ready, at(2 * n))
                    for ps, wn in ((g_ps[m], w[0]), (u_ps[m], w[1])):
                        for f in range(2):
                            for k in range(KD):
                                c = (2 * m + f) * P
                                last = nc.tensor.matmul(ps[:, f * S:(f + 1) * S], wn[:, k, c:c + P], x(k),
                                                        start=(k == 0), stop=(k == KD - 1))
                    last.then_inc(gu_done, 1)

            pe.wait_ge(gather_act, at(B))
            pe.wait_ge(gather_dve, at(B))
            pe.wait_ge(back_act, at(B))
            pe.wait_ge(back_dve, at(B))
            with pe.Fori(0, NEG_E) as q:
                for e in range(EG):
                    n = EG * q + e
                    w = weights(e % 2)
                    pe.wait_ge(wx_in[e % 2], 32 * q + 16 * (e // 2) + 16)
                    gate_up(w, lambda k: xg[:, k, ds(n, 1), :, :].rearrange("p a b c -> p (a b c)"), n)
                    pe.wait_ge(eo_ready, at(n))
                    for m in range(2):
                        pe.wait_ge(hT_ready, at(2 * n + m + 1))
                        for g in range(B // BG):
                            for k in range(2 * m, 2 * m + 2):
                                last = nc.tensor.matmul(e_ps[:, g, 0:D], hT[:, k, g * P:(g + 1) * P], w[2][:, k, :],
                                                        start=(k == 0), stop=(k == KF - 1))
                    last.then_inc(eo_done, 1)
            w = weights(0)
            pe.wait_ge(wx_in[0], 16 * (E // 2 + 1))
            with pe.Fori(0, B) as i:
                gate_up(w, lambda k: xT[:, k, ds(S * i, S)], i + E)
                pe.wait_ge(eo_ready, at(E))
                pe.wait_ge(wx_in[1], 16 * (E // 2 + 1))
                for o in range(2):
                    pe.wait_ge(eo_sent[o], 16 * BG * E // 2 + 16)
                pe.wait_ge(backb_ready, at(i + 1))
                pe.wait_ge(h_ready, at(i))
                for s in range(TS):
                    for q in range(NEG_E):
                        nc.tensor.matmul(e_ps[:, s, 0:D], backb[:, q, s * P:(s + 1) * P],
                                         eo2[:, q, ds(i, 1), :].rearrange("p a d -> p (a d)"), start=(q == 0), stop=False)
                pe.wait_ge(hT_ready, at(2 * (i + E) + 2))
                for s in range(TS):
                    for k in range(KF):
                        last = nc.tensor.matmul(e_ps[:, s, 0:D], hT[:, k, s * P:(s + 1) * P], w[2][:, k, :],
                                                start=False, stop=(k == KF - 1))
                last.then_inc(y_done, 1)

        @block.scalar
        def _(act):
            opened(act, xt_ready, gather_act, back_act, gelu_ready, eo_ready)
            norm.sqrt_act(act)
            with act.Fori(0, B) as i:
                act.wait_ge(xt_done, at(i + 1))
                act.wait_ge(xall_ready, at(i))
                act.wait_ge(lg_done, at(i))
                nc.scalar.activation(xTb[:, :, :], t_ps[:, :].rearrange("p (k t) -> p k t", k=KD), ACT.Copy)\
                    .then_inc(xt_ready, 1)
            act.wait_ge(less_max, 1)
            nc.scalar.activation(sc[:, :, :, :], sc[:, :, :, :], ACT.Exp).then_inc(exp_ready, 1)
            with act.Fori(0, B) as i:
                act.wait_ge(gather_done, at(i + 1))
                nc.scalar.activation(xg[:, 0, :, ds(i, 1), :], g_ps[0][:, :].rearrange("p (e a c) -> p e a c", e=E, a=1),
                                     ACT.Copy).then_inc(gather_act, 1)
                act.wait_ge(back_done, at(i + 1))
                nc.scalar.activation(back[:, ds(i, 1), 0:2, :], u_ps[0][:, :].rearrange("p (a q t) -> p a q t", a=1, q=2),
                                     ACT.Copy).then_inc(back_act, 1)

            def gelus(n):
                for m in range(2):
                    act.wait_ge(gu_done, at(2 * n + m + 1))
                    act.wait_ge(hT_ready, at(2 * n))
                    nc.scalar.activation(act_g[:, 2 * m:2 * m + 2, :], g_ps[m][:, :].rearrange("p (f t) -> p f t", f=2),
                                         ACT.Gelu).then_inc(gelu_ready, 1)

            with act.Fori(0, NEG_E) as q:
                for e in range(EG):
                    n = EG * q + e
                    gelus(n)
                    act.wait_ge(eo_done, at(n + 1))
                    act.wait_ge(eo_sent[e % 2], 16 * BG * (2 * q + e // 2) + 16)
                    nc.scalar.activation(eo[:, e % 2, :, :], e_ps[:, :, 0:D], ACT.Copy)\
                        .then_inc(eo_ready, 1)
            with act.Fori(0, B) as i:
                gelus(i + E)

        @block.vector
        def _(dve):
            opened(dve, xn_ready, lg_ready, xg_xn_ready, pick_ready, gather_dve, back_dve, hT_ready, h_ready)
            ch = Chain(dve, chain)
            nc.vector.memset(zeros[:, :], 0.0)
            norm.stats_dve(dve, ch)
            norm.apply_dve(ch, 0, lambda s: xn[:, s:s + 1, :]).then_inc(xn_ready, 1)
            before, per = ch.n, 1
            with dve.Fori(0, B) as i:
                ch = Chain(dve, chain, before, i, per)
                dve.wait_ge(xt_done, at(i + 1))
                norm.apply_dve(ch, i + 1, lambda s: xn[:, s:s + 1, :]).then_inc(xn_ready, 1)
                dve.wait_ge(lg_done, at(i + 1))
                nc.vector.tensor_copy(sc[:, :, ds(i, 1), :], l_ps[:, 0:TS * E].rearrange("p (s a e) -> p s a e", s=TS, a=1))\
                    .then_inc(lg_ready, 1)
                ch.done(before)
            ch = Chain(dve, chain, before + per * B)
            dve.wait_ge(lg_ready, at(B))
            rows = sc[:, :, :, :].rearrange("p s b e -> p (s b) e")
            wide = lambda t: t[:, :].rearrange("p (n a) -> p n a", a=1).broadcast_to([P, TS * B, E])
            ch.link(nc.vector.tensor_reduce(smax[:, :], rows, AX, ALU.max))
            nc.vector.tensor_tensor(rows, rows, wide(smax), ALU.subtract).then_inc(less_max, 1)
            dve.wait_ge(exp_ready, 1)
            ch.link(nc.vector.tensor_reduce(ssum[:, :], rows, AX, ALU.add))
            ch.link(nc.vector.reciprocal(ssum[:, :], ssum[:, :]))
            nc.vector.tensor_tensor(rows, rows, wide(ssum), ALU.mult).then_inc(sc_ready, 1)
            dve.wait_ge(scT_done, 1)
            ch.link(nc.vector.tensor_copy(work[:, :], l_ps[:, 0:S]))
            for _ in range(CAP // 8):
                ch.link(nc.vector.max(out=top8[:, :], in_=work[:, :]))
                ch.link(nc.vector.match_replace(out=work[:, :], in_to_replace=top8[:, :], in_values=work[:, :], imm_value=-1.0))
            ch.link(nc.vector.tensor_scalar(taken[:, :], work[:, :], 0.0, None, ALU.is_lt))
            ch.link(nc.vector.tensor_tensor_scan(slot[:, :], taken[:, :], zeros[:, :], 0.0, ALU.add, ALU.add))
            nc.vector.tensor_tensor(slot[:, :], slot[:, :], taken[:, :], ALU.mult).then_inc(slot_ready, 1)
            dve.wait_ge(slotT_done, 1)
            nc.vector.memset(slotT[:, :, B:B + 1, :], 0.0)
            ch.link(nc.vector.tensor_copy(slotT[:, :, 0:B, :].rearrange("p s b e -> p s (b e)"),
                                          l_ps[:, 0:S].rearrange("p (s n) -> p s n", s=TS)))

            def prepare(ch, n, o):
                if isinstance(n, int):
                    dve.wait_ge(xn_ready, at(B + 1))
                dve.wait_ge(xg_xn_ready, at(n))
                ch.link(norm.apply_dve(ch, n, lambda s: xn[:, s:s + 1, :]))
                ch.link(nc.vector.tensor_copy(xn_parts[0][:, o, :, :], xn[:, :, :]))
                nc.vector.tensor_tensor(xn_parts[1][:, o, :, :], xn[:, :, :], xn_parts[0][:, o, :, :].bitcast(F32), ALU.subtract)\
                    .then_inc(xg_xn_ready, 1)
                if not isinstance(n, int):
                    dve.wait_ge(pickw_ready, at(n - 1))
                for s in range(TS):
                    last = nc.vector.tensor_tensor(
                        pick[:, o, s, :, :], iota[:, :, :].broadcast_to([P, E, CAP]),
                        slotT[:, s, ds(n, 1), :].rearrange("p a e -> p e a").broadcast_to([P, E, CAP]), ALU.is_equal)
                last.then_inc(pick_ready, 1)

            prepare(ch, 0, 0)
            before, per = ch.n, 2 * 3
            with dve.Fori(0, B // 2) as t:
                ch = Chain(dve, chain, before, t, per)
                for o in range(2):
                    i = 2 * t + o
                    prepare(ch, i + 1, 1 - o)
                    dve.wait_ge(gather_done, at(i + 1))
                    nc.vector.tensor_copy(xg[:, 1, :, ds(i, 1), :], g_ps[1][:, :].rearrange("p (e a c) -> p e a c", e=E, a=1))\
                        .then_inc(gather_dve, 1)
                    dve.wait_ge(back_done, at(i + 1))
                    nc.vector.tensor_copy(back[:, ds(i, 1), 2:4, :], u_ps[1][:, :].rearrange("p (a q t) -> p a q t", a=1, q=2))\
                        .then_inc(back_dve, 1)
                ch.done(before)

            def times_half(n, m):
                dve.wait_ge(gelu_ready, at(2 * n + m + 1))
                nc.vector.tensor_tensor(hT[:, 2 * m:2 * m + 2, :], act_g[:, 2 * m:2 * m + 2, :],
                                        u_ps[m][:, :].rearrange("p (f t) -> p f t", f=2), ALU.mult).then_inc(hT_ready, 1)

            with dve.Fori(0, NEG_E) as q:
                for e in range(EG):
                    n = EG * q + e
                    dve.wait_ge(eo_done, at(n))
                    for m in range(2):
                        times_half(n, m)
            with dve.Fori(0, B) as i:
                dve.wait_ge(eo_done, at(E))
                dve.wait_ge(y_done, at(i))
                for m in range(2):
                    times_half(i + E, m)
                dve.wait_ge(y_done, at(i + 1))
                hs = h[:, ds(TS * i, TS), :]
                nc.vector.tensor_tensor(hs, e_ps[:, :, 0:D], hs, ALU.add).then_inc(h_ready, 1)

        @block.gpsimd
        def _(pool):
            opened(pool, xall_ready, pickw_ready, backb_ready)
            with pool.Fori(0, B) as i:
                pool.wait_ge(xt_ready, at(i + 1))
                nc.gpsimd.tensor_copy(xT[:, :, ds(S * i, S)], xTb[:, :, :]).then_inc(xall_ready, 1)
            with pool.Fori(0, B // 2) as t:
                for o in range(2):
                    i = 2 * t + o
                    pool.wait_ge(pick_ready, at(i + 1))
                    pool.wait_ge(back_done, at(i))
                    for s in range(TS):
                        last = nc.gpsimd.tensor_tensor(
                            pickw[:, s, :, :], pick[:, o, s, :, :].bitcast(F32),
                            sc[:, s, ds(i, 1), :].rearrange("p a e -> p e a").broadcast_to([P, E, CAP]), ALU.mult)
                    last.then_inc(pickw_ready, 1)
            with pool.Fori(0, B) as i:
                pool.wait_ge(back_act, at(B))
                pool.wait_ge(back_dve, at(B))
                pool.wait_ge(y_done, at(i))
                nc.gpsimd.tensor_copy(backb[:, :, :], back[:, ds(i, 1), :, :].rearrange("p a q t -> p (a q) t"))\
                    .then_inc(backb_ready, 1)


def attention_experts(nc, dram, h, ident):
    E = 16
    HW = 128
    QKV = 3 * HW
    SCALE = 1.0 / float(np.sqrt(HW))
    NQ = E * TS
    NO = E // 2 * TS
    NY = NQ + NO
    RING = 4
    CUT = [0, 12, 22, NQ]
    OG = 2
    width = [P, S]
    off = [0, P]
    W = P + S
    LOADS = E + E // OG
    RAW = 4
    PARTS = ((1, 0), (0, 1), (0, 0))
    with Stage(nc, "f3") as st:
        sim = st.sb("sim", [P, KD, E])
        sim2 = st.sb("sim2", [P, KD, E])
        gates = st.sb("gates", [P, 1, E])
        index = st.sb("index", [P, 1, E])
        ones = st.sb("ones", [P, P])
        mask = st.sb("mask", [P, TS, S])
        raw = st.sb("raw", [P, RAW, KD * QKV])
        wqkv = [st.sb(f"wqkv{n}", [P, E, KD, QKV], F32R) for n in range(2)]
        wo = [st.sb(f"wo{n}", [P, E, D], F32R) for n in range(2)]
        xT3 = [st.sb(f"xT_{n}", [P, KD, S], F32R) for n in range(2)]
        aoT = [st.sb(f"aoT{n}", [P, S], F32R) for n in range(2)]
        xn = st.sb("xn", [P, TS, D])
        xT = st.sb("xT", [P, KD, S])
        square = st.sb("square", [P, D])
        ssq = st.sb("ssq", [P, TS])
        ssq_all = st.sb("ssq_all", [P, TILES])
        norms = st.sb("norms", [P, E])
        rows = [st.sb(f"rows{n}", [P, TILES]) for n in range(4)]
        lg = st.sb("lg", [P, TILES, E])
        e1 = st.sb("e1", [P, TILES, E])
        e2 = st.sb("e2", [P, TILES, E])
        best = st.sb("best", [P, TILES, E])
        rw = st.sb("rw", [P, TILES + PAD, E])
        rw_q = st.sb("rw_q", [P, TS, E])
        rw_o = st.sb("rw_o", [P, TS, E])
        acc = st.sb("acc", [P, TS, QKV])
        v = st.sb("v", [P, TS, HW])
        qkT = st.sb("qkT", [P, 2, S])
        carry = st.sb("carry", [P, 2])
        z = st.sb("z", [P, W])
        nmax = st.sb("nmax", [P, TS])
        bias = st.sb("bias", [P, TS])
        pr = st.sb("pr", [P, W])
        psum_of = st.sb("psum_of", [P, TS])
        rsum = st.sb("rsum", [P, TS])
        prT = st.sb("prT", [P, TS, S])
        acco = st.sb("acco", [P, TS, D])
        acco2 = st.sb("acco2", [P, TS, D])
        y_ps = [st.ps(f"y{n}") for n in range(RING)]
        t_ps, s_ps, p_ps, a_ps = (st.ps(n) for n in ("t", "s", "p", "a"))
        norm = Norm(nc, st, h)

        w_in, chain = st.sem("w_in"), st.sem("chain")
        raw_in = [st.sem(f"raw{n}_in") for n in range(RAW)]
        w_high, w_low, xt_high, ao_high = (st.sem(n) for n in ("w_high", "w_low", "xt_high", "ao_high"))
        gates_ready, sim2_ready, norms_done, norms_var, norms_std, sim_ready = (
            st.sem(n) for n in ("gates_ready", "sim2_ready", "norms_done", "norms_var", "norms_std", "sim_ready"))
        xg_ready, xgt_done, xgt_ready, lg_done, lg_ready = (
            st.sem(n) for n in ("xg_ready", "xgt_done", "xgt_ready", "lg_done", "lg_ready"))
        ssq_ready, len_ready, less_max, exps_ready = (
            st.sem(n) for n in ("ssq_ready", "len_ready", "less_max", "exps_ready"))
        xn_ready, xt_done, xt_ready = st.sem("xn_ready"), st.sem("xt_done"), st.sem("xt_ready")
        y_done, y_used, acc_ready, v_ready, qkt_done, qkt_ready = (
            st.sem(n) for n in ("y_done", "y_used", "acc_ready", "v_ready", "qkt_done", "qkt_ready"))
        sc_done, z_ready, exp_done, pt_done, pt_ready, ao_done, ao_ready = (
            st.sem(n) for n in ("sc_done", "z_ready", "exp_done", "pt_done", "pt_ready", "ao_done", "ao_ready"))
        h_ready = st.sem("h_ready")
        block = st.block()
        NW = 4

        @block.sync
        def _(sp):
            sp.dma_start(sim[:, :, :], dram["f3_sim"].rearrange("(k p) n -> p k n", p=P)).then_inc(w_in, 16)
            sp.dma_start(gates[:, 0, :], dram["f3_gates"].partition_broadcast(P)).then_inc(w_in, 16)
            sp.dma_start(index[:, 0, :], dram["f3_index"].partition_broadcast(P)).then_inc(w_in, 16)
            sp.dma_start(mask[:, :, :], dram["f3_mask"]).then_inc(w_in, 16)
            for n in range(LOADS):
                if n >= RAW:
                    sp.wait_ge(w_low, at(n - RAW + 1))
                if n < E:
                    to, what = raw[:, n % RAW, :], dram["f3_wqkv"][:, n].rearrange("p k n -> p (k n)")
                else:
                    to, what = raw[:, n % RAW, 0:OG * D], dram["f3_wo"][:, OG * (n - E):OG * (n - E + 1)].rearrange("p e n -> p (e n)")
                sp.dma_start(to, what).then_inc(raw_in[n % RAW], 16)

        def weights_of(n, part):
            if isinstance(n, int) and n >= E:
                return wo[part][:, OG * (n - E):OG * (n - E + 1), :].rearrange("p e n -> p (e n)")
            return wqkv[part][:, ds(n, 1), :, :].rearrange("p e k n -> p (e k n)")

        def unit_qkv(n):
            return n // TS, n % TS

        def unit_out(n):
            return n % TS, n // TS

        @block.tensor
        def _(pe):
            opened(pe, xgt_done, lg_done, xt_done, y_done, qkt_done, sc_done, pt_done, ao_done)
            pe.wait_ge(sim2_ready, 1)
            for k in range(KD):
                last = nc.tensor.matmul(a_ps[:, 0:E], ones[:, :], sim2[:, k, :], start=(k == 0), stop=(k == KD - 1))
            last.then_inc(norms_done, 1)
            pe.wait_ge(sim_ready, 1)

            def transposes(done):
                for k in range(KD):
                    for s in range(TS):
                        last = nc.tensor.transpose(t_ps[:, k * S + s * P:k * S + (s + 1) * P],
                                                   xn[:, s, k * P:(k + 1) * P], ident[:, :])
                last.then_inc(done, 1)

            with pe.Fori(0, B) as i:
                pe.wait_ge(xg_ready, at(i + 1))
                transposes(xgt_done)
                pe.wait_ge(xgt_ready, at(i + 1))
                pe.wait_ge(lg_ready, at(i))
                for s in range(TS):
                    for k in range(KD):
                        last = nc.tensor.matmul(a_ps[:, s * E:(s + 1) * E], xT[:, k, s * P:(s + 1) * P], sim[:, k, :],
                                                start=(k == 0), stop=(k == KD - 1))
                last.then_inc(lg_done, 1)

            def transpose_x(n):
                pe.wait_ge(xn_ready, at(n + 1))
                transposes(xt_done)

            def products_qkv(b, n0, n1, before):
                for n in range(n0, n1):
                    e, s = unit_qkv(n)
                    if before is None:
                        if s == 0:
                            pe.wait_ge(w_low, at(e + 1))
                        if n >= RING:
                            pe.wait_ge(y_used, at(n - RING + 1))
                    else:
                        pe.wait_ge(y_used, at(before + n - RING + 1))
                    for k in range(KD):
                        for m, (px, pw) in enumerate(PARTS):
                            last = nc.tensor.matmul(y_ps[n % RING][:, 0:QKV], xT3[px][:, k, s * P:(s + 1) * P], wqkv[pw][:, e, k, :],
                                                    start=(k + m == 0), stop=(k == KD - 1 and m == 2))
                    last.then_inc(y_done, 1)

            transpose_x(0)
            pe.wait_ge(xt_ready, at(1))
            products_qkv(0, 0, NQ, None)
            transpose_x(1)
            pe.wait_ge(w_low, at(LOADS))

            def turn(i, last_one=False):
                before = NQ + NY * i
                pe.wait_ge(acc_ready, at(i + 1))
                pe.wait_ge(xt_ready, at(i + 2))
                for a in range(2):
                    for s in range(TS):
                        last = nc.tensor.transpose(t_ps[:, a * S + s * P:a * S + (s + 1) * P],
                                                   acc[:, s, a * HW:(a + 1) * HW], ident[:, :])
                last.then_inc(qkt_done, 1)
                if not last_one:
                    products_qkv(i + 1, CUT[0], CUT[1], before)
                pe.wait_ge(qkt_ready, at(i + 1))
                pe.wait_ge(z_ready, at(i))
                for s in range(TS):
                    last = nc.tensor.matmul(s_ps[:, off[s]:off[s] + width[s]], qkT[:, 0, s * P:(s + 1) * P],
                                            qkT[:, 1, 0:width[s]], start=True, stop=True)
                last.then_inc(sc_done, 1)
                if not last_one:
                    products_qkv(i + 1, CUT[1], CUT[2], before)
                pe.wait_ge(exp_done, at(i + 1))
                pe.wait_ge(pt_ready, at(i))
                for s in range(TS):
                    for k in range(width[s] // P):
                        last = nc.tensor.transpose(p_ps[:, k * S + s * P:k * S + (s + 1) * P],
                                                   pr[:, off[s] + k * P:off[s] + (k + 1) * P], ident[:, :])
                last.then_inc(pt_done, 1)
                if not last_one:
                    products_qkv(i + 1, CUT[2], CUT[3], before)
                pe.wait_ge(pt_ready, at(i + 1))
                pe.wait_ge(v_ready, at(i + 1))
                pe.wait_ge(ao_ready, at(i))
                for k in range(TS):
                    last = nc.tensor.matmul(a_ps[:, k * P:S], v[:, k, :], prT[:, k, k * P:S],
                                            start=(k == 0), stop=(k == TS - 1), skip_group_check=True)
                last.then_inc(ao_done, 1)
                if not last_one:
                    transpose_x(i + 2)
                pe.wait_ge(ao_ready, at(i + 1))
                if not last_one:
                    before += NQ
                for n in range(NO):
                    s, e = unit_out(n)
                    pe.wait_ge(y_used, at(before + n - RING + 1))
                    for m, (pa, pw) in enumerate(PARTS):
                        last = nc.tensor.matmul(y_ps[n % RING][:, :], aoT[pa][:, s * P:(s + 1) * P], wo[pw][:, 2 * e:2 * e + 2, :],
                                                start=(m == 0), stop=(m == 2))
                    last.then_inc(y_done, 1)

            with pe.Fori(0, B - 1) as i:
                turn(i)
            turn(B - 1, last_one=True)

        @block.scalar
        def _(act):
            opened(act, w_high, xgt_ready, xt_high, v_ready, qkt_ready, exp_done, pt_ready, ao_high)
            norm.sqrt_act(act)
            act.wait_ge(w_in, 16 * NW)
            nc.scalar.activation(gates[:, :, :], gates[:, :, :], ACT.Sigmoid).then_inc(gates_ready, 1)
            act.wait_ge(norms_var, 1)
            nc.scalar.activation(norms[:, :], norms[:, :], ACT.Sqrt).then_inc(norms_std, 1)
            copy_to = lambda t: nc.scalar.activation(t[:, :, :], t_ps[:, :].rearrange("p (k t) -> p k t", k=KD), ACT.Copy)

            def round_weights(n, slot, turn, width):
                act.wait_ge(raw_in[slot], 16 * turn + 16)
                nc.scalar.activation(weights_of(n, 0), raw[:, slot, 0:width], ACT.Copy).then_inc(w_high, 1)

            with act.Fori(0, B // 2) as t:
                for o in range(2):
                    i = 2 * t + o
                    act.wait_ge(xgt_done, at(i + 1))
                    act.wait_ge(lg_done, at(i))
                    copy_to(xT).then_inc(xgt_ready, 1)
                    for slot in range(2 * o, 2 * o + 2):
                        round_weights(RAW * t + slot, slot, t, KD * QKV)
            act.wait_ge(ssq_ready, 1)
            nc.scalar.activation(ssq_all[:, :], ssq_all[:, :], ACT.Sqrt).then_inc(len_ready, 1)
            act.wait_ge(less_max, 1)
            nc.scalar.activation(e1[:, :, :], e1[:, :, :], ACT.Exp).then_inc(exps_ready, 1)
            act.wait_ge(lg_done, at(B))
            for n in range(2):
                if n == 1:
                    for m in range(E, LOADS):
                        round_weights(m, m % RAW, m // RAW, OG * D)
                    act.wait_ge(y_done, at(NQ))
                act.wait_ge(xt_done, at(n + 1))
                copy_to(xT3[0]).then_inc(xt_high, 1)

            def turn(i, last_one=False):
                act.wait_ge(acc_ready, at(i + 1))
                act.wait_ge(ao_done, at(i))
                nc.scalar.activation(v[:, :, :], acc[:, :, 2 * HW:QKV], ACT.Copy).then_inc(v_ready, 1)
                act.wait_ge(qkt_done, at(i + 1))
                nc.scalar.activation(qkT[:, :, :], t_ps[:, :].rearrange("p (a t) -> p a t", a=2), ACT.Copy)\
                    .then_inc(qkt_ready, 1)
                act.wait_ge(z_ready, at(i + 1))
                for s in range(TS):
                    c = slice(off[s], off[s] + width[s])
                    last = nc.scalar.activation(pr[:, c], z[:, c], ACT.Exp, bias=bias[:, s:s + 1], scale=-SCALE,
                                                accum_out=psum_of[:, s:s + 1])
                last.then_inc(exp_done, 1)
                act.wait_ge(pt_done, at(i + 1))
                nc.scalar.activation(prT[:, 0, :], p_ps[:, 0:S], ACT.Copy)
                nc.scalar.activation(prT[:, 1, P:S], p_ps[:, S + P:2 * S], ACT.Copy).then_inc(pt_ready, 1)
                act.wait_ge(ao_done, at(i + 1))
                act.wait_ge(y_done, at(NQ + NY * i + (0 if last_one else NQ)))
                nc.scalar.activation(aoT[0][:, :], a_ps[:, 0:S], ACT.Copy).then_inc(ao_high, 1)
                if not last_one:
                    act.wait_ge(xt_done, at(i + 3))
                    copy_to(xT3[0]).then_inc(xt_high, 1)

            with act.Fori(0, B - 1) as i:
                turn(i)
            turn(B - 1, last_one=True)

        @block.vector
        def _(dve):
            opened(dve, xt_ready, ao_ready, xg_ready, lg_ready, xn_ready, y_used, acc_ready, z_ready)
            ch = Chain(dve, chain)
            nc.vector.memset(ones[:, :], 1.0)
            nc.vector.memset(rw[:, TILES:TILES + PAD, :], 0.0)
            norm.stats_dve(dve, ch)
            dve.wait_ge(w_in, 16 * NW)
            nc.vector.tensor_tensor(sim2[:, :, :], sim[:, :, :], sim[:, :, :], ALU.mult).then_inc(sim2_ready, 1)
            dve.wait_ge(norms_done, 1)
            nc.vector.tensor_scalar(norms[:, :], a_ps[:, 0:E], 1e-12, None, ALU.add).then_inc(norms_var, 1)
            dve.wait_ge(norms_std, 1)
            ch.link(nc.vector.reciprocal(norms[:, :], norms[:, :]))
            nc.vector.tensor_tensor(sim[:, :, :], sim[:, :, :],
                                    norms[:, :].rearrange("p (a e) -> p a e", a=1).broadcast_to([P, KD, E]), ALU.mult)\
                .then_inc(sim_ready, 1)
            norm.apply_dve(ch, 0, lambda s: xn[:, s:s + 1, :]).then_inc(xg_ready, 1)
            before, per = ch.n, 3
            with dve.Fori(0, B) as i:
                ch = Chain(dve, chain, before, i, per)
                dve.wait_ge(xg_ready, at(i + 1))
                for s in range(TS):
                    last = nc.vector.tensor_tensor_reduce(square[:, :], xn[:, s, :], xn[:, s, :], 1.0, 0.0, ALU.mult, ALU.add,
                                                          ssq[:, s:s + 1])
                    ch.link(last)
                nc.vector.tensor_copy(ssq_all[:, ds(TS * i, TS)], ssq[:, :])
                dve.wait_ge(xgt_done, at(i + 1))
                norm.apply_dve(ch, i + 1, lambda s: xn[:, s:s + 1, :]).then_inc(xg_ready, 1)
                dve.wait_ge(lg_done, at(i + 1))
                nc.vector.tensor_copy(lg[:, ds(TS * i, TS), :], a_ps[:, 0:TS * E].rearrange("p (s e) -> p s e", s=TS))\
                    .then_inc(lg_ready, 1)
                ch.done(before)
            ch = Chain(dve, chain, before + per * B)
            wide = lambda t: t[:, :].rearrange("p (n a) -> p n a", a=1).broadcast_to([P, TILES, E])
            all_ = lambda t: t[:, 0:TILES, :]
            dve.wait_ge(lg_ready, at(B))
            nc.vector.tensor_scalar(ssq_all[:, :], ssq_all[:, :], 1e-12, None, ALU.add).then_inc(ssq_ready, 1)
            dve.wait_ge(len_ready, 1)
            dve.wait_ge(gates_ready, 1)
            ch.link(nc.vector.reciprocal(ssq_all[:, :], ssq_all[:, :]))
            ch.link(nc.vector.tensor_tensor(all_(lg), all_(lg), wide(ssq_all), ALU.mult))
            ch.link(nc.vector.tensor_tensor(all_(lg), all_(lg), gates[:, :, :].broadcast_to([P, TILES, E]), ALU.subtract))
            top, where, none, high = rows
            ch.link(nc.vector.tensor_reduce(top[:, :], all_(lg), AX, ALU.max))
            ch.link(nc.vector.tensor_scalar(high[:, :], top[:, :], 0.0, None, ALU.max))
            ch.link(nc.vector.tensor_scalar(none[:, :], top[:, :], 0.0, None, ALU.is_le))
            ch.link(nc.vector.tensor_copy(all_(e1), all_(lg)))
            for n in range(2):
                if n == 1:
                    ch.link(nc.vector.scalar_tensor_tensor(all_(e1), all_(best), NEG, all_(e1), ALU.mult, ALU.add))
                    ch.link(nc.vector.tensor_reduce(top[:, :], all_(e1), AX, ALU.max))
                ch.link(nc.vector.tensor_tensor(all_(e2), all_(e1), wide(top), ALU.not_equal))
                ch.link(nc.vector.scalar_tensor_tensor(all_(e2), all_(e2), 64.0, index[:, :, :].broadcast_to([P, TILES, E]),
                                                       ALU.mult, ALU.add))
                ch.link(nc.vector.tensor_reduce(where[:, :], all_(e2), AX, ALU.min))
                ch.link(nc.vector.tensor_tensor(all_(e2), index[:, :, :].broadcast_to([P, TILES, E]), wide(where), ALU.is_equal))
                if n == 0:
                    ch.link(nc.vector.tensor_copy(all_(best), all_(e2)))
                else:
                    ch.link(nc.vector.tensor_tensor(all_(best), all_(best), all_(e2), ALU.add))
            ch.link(nc.vector.tensor_tensor(all_(best), all_(best), wide(none), ALU.mult))
            ch.link(nc.vector.scalar_tensor_tensor(all_(best), all_(lg), 0.0, all_(best), ALU.is_gt, ALU.add))
            nc.vector.scalar_tensor_tensor(all_(e1), all_(lg), 0.0, wide(high), ALU.max, ALU.subtract).then_inc(less_max, 1)
            dve.wait_ge(exps_ready, 1)
            ch.link(nc.vector.tensor_tensor(all_(e1), all_(e1), all_(best), ALU.mult))
            ch.link(nc.vector.tensor_reduce(top[:, :], all_(e1), AX, ALU.add))
            ch.link(nc.vector.reciprocal(top[:, :], top[:, :]))
            ch.link(nc.vector.tensor_tensor(all_(rw), all_(e1), wide(top), ALU.mult))

            def accumulate_qkv(ch, n0, n1, before):
                for n in range(n0, n1):
                    e, s = unit_qkv(n)
                    dve.wait_ge(y_done, at(before + n + 1))
                    y = y_ps[n % RING][:, 0:QKV]
                    if e == 0:
                        last = nc.vector.tensor_scalar(acc[:, s, :], y, rw_q[:, s, e:e + 1], None, ALU.mult)
                    else:
                        dve.wait_ge(y_used, at(before + n - TS + 1))
                        last = nc.vector.scalar_tensor_tensor(acc[:, s, :], y, rw_q[:, s, e:e + 1], acc[:, s, :],
                                                              ALU.mult, ALU.add)
                    last.then_inc(y_used, 1)

            dve.wait_ge(xg_ready, at(B + 1))
            norm.apply_dve(ch, 0, lambda s: xn[:, s:s + 1, :]).then_inc(xn_ready, 1)
            ch.link(nc.vector.tensor_copy(rw_q[:, :, :], rw[:, 0:TS, :]))

            def rest_of_x(n):
                dve.wait_ge(xt_high, at(n + 1))
                nc.vector.tensor_tensor(xT3[1][:, :, :], t_ps[:, :].rearrange("p (k t) -> p k t", k=KD),
                                        xT3[0][:, :, :].bitcast(F32), ALU.subtract).then_inc(xt_ready, 1)

            rest_of_x(0)
            norm.apply_dve(ch, 1, lambda s: xn[:, s:s + 1, :]).then_inc(xn_ready, 1)
            accumulate_qkv(ch, 0, NQ, 0)
            rest_of_x(1)
            dve.wait_ge(y_used, at(NQ))
            ch.link(nc.vector.memset(carry[:, 0:1], 0.0))
            nc.vector.memset(carry[:, 1:2], 0.0).then_inc(acc_ready, 1)
            before, per = ch.n, 6

            def turn(ch, i, last_one=False):
                y_before = NQ + NY * i
                ch.link(nc.vector.tensor_copy(rw_o[:, :, :], rw_q[:, :, :]))
                if not last_one:
                    ch.link(nc.vector.tensor_copy(rw_q[:, :, :], rw[:, ds(TS * i + TS, TS), :]))
                dve.wait_ge(v_ready, at(i + 1))
                dve.wait_ge(qkt_done, at(i + 1))
                if not last_one:
                    accumulate_qkv(ch, CUT[0], CUT[1], y_before)
                dve.wait_ge(sc_done, at(i + 1))
                dve.wait_ge(exp_done, at(i))
                nc.vector.memset(carry[:, 0:1], 0.0)
                for s in range(TS):
                    c = slice(off[s], off[s] + width[s])
                    last = nc.vector.tensor_tensor_reduce(z[:, c], s_ps[:, c], mask[:, s, 0:width[s]], -1.0, BIG,
                                                          ALU.add, ALU.min, nmax[:, s:s + 1])
                ch.link(last)
                nc.vector.tensor_scalar(bias[:, :], nmax[:, :], SCALE, None, ALU.mult).then_inc(z_ready, 1)
                if not last_one:
                    accumulate_qkv(ch, CUT[1], CUT[2], y_before)
                if not last_one:
                    dve.wait_ge(xt_done, at(i + 2))
                    norm.apply_dve(ch, i + 2, lambda s: xn[:, s:s + 1, :]).then_inc(xn_ready, 1)
                    accumulate_qkv(ch, CUT[2], CUT[3], y_before)
                    dve.wait_ge(y_used, at(y_before + NQ))
                    nc.vector.memset(carry[:, 1:2], 0.0).then_inc(acc_ready, 1)
                    y_before += NQ
                dve.wait_ge(ao_high, at(i + 1))
                nc.vector.tensor_tensor(aoT[1][:, :], a_ps[:, 0:S], aoT[0][:, :].bitcast(F32), ALU.subtract).then_inc(ao_ready, 1)
                if not last_one:
                    rest_of_x(i + 2)
                ch.link(nc.vector.reciprocal(rsum[:, :], psum_of[:, :]))
                for n in range(NO):
                    s, e = unit_out(n)
                    dve.wait_ge(y_done, at(y_before + n + 1))
                    for a in range(2):
                        y = y_ps[n % RING][:, a * D:(a + 1) * D]
                        g = rw_o[:, s, 2 * e + a:2 * e + a + 1]
                        o = acco[:, s, :] if a == 0 else acco2[:, s, :]
                        if e == 0:
                            last = nc.vector.tensor_scalar(o, y, g, None, ALU.mult)
                        else:
                            dve.wait_ge(y_used, at(y_before + n - TS + 1))
                            last = nc.vector.scalar_tensor_tensor(o, y, g, o, ALU.mult, ALU.add)
                    last.then_inc(y_used, 1)
                dve.wait_ge(y_used, at(y_before + NO))
                ch.link(nc.vector.tensor_tensor(acco[:, :, :], acco[:, :, :], acco2[:, :, :], ALU.add))
                for s in range(TS):
                    hs = h[:, ds(TS * i + s, 1), :]
                    last = nc.vector.scalar_tensor_tensor(hs, acco[:, s:s + 1, :], rsum[:, s:s + 1], hs, ALU.mult, ALU.add)
                last.then_inc(h_ready, 1)
                dve.wait_ge(h_ready, i + 1)

            with dve.Fori(0, B - 1) as i:
                ch = Chain(dve, chain, before, i, per)
                turn(ch, i)
                ch.done(before)
            turn(Chain(dve, chain, before + per * (B - 1)), B - 1, last_one=True)

        @block.gpsimd
        def _(pool):
            opened(pool, w_low)

            def rest_of_weights(n, slot, width):
                pool.wait_ge(w_high, at(n + 1))
                nc.gpsimd.tensor_tensor(weights_of(n, 1), raw[:, slot, 0:width], weights_of(n, 0).bitcast(F32), ALU.subtract)\
                    .then_inc(w_low, 1)

            with pool.Fori(0, E // RAW) as i:
                for slot in range(RAW):
                    rest_of_weights(RAW * i + slot, slot, KD * QKV)
            for n in range(E, LOADS):
                rest_of_weights(n, n % RAW, OG * D)


def store_out(nc, out, h):
    with Stage(nc, "store") as st:
        stored = st.sem("stored")
        block = st.block()

        @block.sync
        def _(sp):
            sp.dma_start(out.rearrange("b (s p) d -> p (b s) d", p=P), h[:, 0:TILES, :]).then_inc(stored, 16)
            sp.wait_ge(stored, 16)


def attention_of(name, scale, **kinds):
    return (lambda nc, dram, h_padded, ident: attention(nc, dram, h_padded, ident, name, scale, **kinds)), True


STAGE_LIST = [
    attention_of("a0", 0.25, causal=True, kind="add"),
    (ternary_mlp, False),
    attention_of("a1", 0.25),
    (channel_mixer, False),
    attention_of("a2", 0.25, causal=True, kind="add", relative=True),
    (expert_choice, False),
    attention_of("a3", 1.0 / 16.0, kind="mult", latent=True),
    (attention_experts, False),
]


def build(nc, dram, out, stages=9):
    with ExitStack() as ctx:
        padded = ctx.enter_context(nc.sbuf_tensor("h", [P, TS + TILES + PAD, D], F32))
        h = padded[:, TS:, :]
        ident = ctx.enter_context(nc.sbuf_tensor("ident_sb", [P, P], F32))
        tok_mixer(nc, dram, h, ident)
        for n, (stage, whole) in enumerate(STAGE_LIST):
            if n + 2 <= stages:
                stage(nc, dram, padded if whole else h, ident)
        store_out(nc, out, h)


STAGES = 9


def kernel(**inputs):
    import numpy as np
    import concourse.bacc as _bacc
    from concourse import mybir as _mybir
    from concourse.bass_utils import run_bass_kernel_spmd as _run

    c = np.ascontiguousarray
    a = {k: np.asarray(v) for k, v in inputs.items()}
    lay = {}
    lay["ident"] = np.eye(128, dtype=np.float32)
    x = a["x"]
    lay["tok_x"] = np.concatenate([x.transpose(0, 1, 3, 2), np.ones((8, 1, 4, 256), np.float32)], axis=1)
    lay["tok_xflat"] = x.transpose(0, 2, 3, 1).reshape(8, 256, 256)
    lay["tok_wqkv"] = np.concatenate(
        [np.concatenate([a[f"L0_tok_W{n}_w"].T, a[f"L0_tok_W{n}_b"][None]], axis=0) for n in "qkv"], axis=1)
    lay["tok_wbT"] = a["L0_tok_w_bias"].T
    mask = np.zeros((256, 256, 4), np.uint8)
    mask[:, :, 0] = a["L0_tok_local_mask"].T.view(np.uint8)
    lay["tok_maskT"] = mask.view(np.int32)[:, :, 0]
    lay["tok_outw"] = a["L0_tok_out_w"]
    lay["tok_vecs"] = np.stack([a["L0_tok_out_b"], a["L0_tok_ln_g"], a["L0_tok_ln_b"]])

    row = np.arange(128)
    lay["parity"] = np.stack([(row // 16) % 2 == 0, (row // 16) % 2 == 1], axis=1).astype(np.float32)
    order = np.concatenate([np.arange(16) + 16 * (8 * (g // 2) + g % 2 + 2 * j) for g in range(4) for j in range(4)])

    def attn(name, wq, wk, wv, wo, bq, bk, bv, bo):
        lay[name + "_wq"], lay[name + "_wk"], lay[name + "_wv"], lay[name + "_wo"] = wq, wk, wv, wo[order]
        lay[name + "_bqk"] = np.stack([bq.reshape(2, 128).T, bk.reshape(2, 128).T], axis=1)
        lay[name + "_bv"], lay[name + "_bo"] = bv, bo

    def tiles(m):
        return m.reshape(2, 128, -1).transpose(1, 0, 2)

    i, j = np.arange(256)[:, None], np.arange(256)[None, :]
    fenwick = np.zeros((256, 256), bool)
    for t in range(256):
        fenwick[t, t] = True
        step = 1
        while t - step >= 0:
            fenwick[t, t - step] = True
            step *= 2
    w, bb = a["L0_attn_W_qkv"], a["L0_attn_b_qkv"]
    attn("a0", w[:, 0:256], w[:, 256:512], w[:, 512:768], a["L0_attn_W_proj"], bb[0:256], bb[256:512], bb[512:768], a["L0_attn_b_proj"])
    lay["a0_matrix"] = tiles(np.where(fenwick, 0.0, NEG).astype(np.float32))

    lay["f0_wfcT"] = a["L0_ffn_W_fc"].T
    lay["f0_wprojT"] = a["L0_ffn_W_proj"].T
    lay["f0_lnwb"] = np.stack([a["L0_ffn_ln_w"].reshape(8, 128).T, a["L0_ffn_ln_b"].reshape(8, 128).T], axis=1)
    attn("a1", *(a["L1_attn_W" + n].T for n in "qkvo"), *(a["L1_attn_b" + n] for n in "qkvo"))
    for n in "rkv":
        lay[f"f1_w{n}T"] = a["L1_ffn_W_" + n].T
    lay["f1_mu"] = np.stack([a["L1_ffn_mu_" + n].reshape(2, 128).T for n in "rk"], axis=1)
    attn("a2", *(a["L2_attn_W" + n] for n in "qkvo"), *(a["L2_attn_b" + n] for n in "qkvo"))
    lay["a2_matrix"] = tiles(np.where(j <= i, 0.0, NEG).astype(np.float32))
    relT = np.zeros((8, 16, 2, 256), np.float32)
    relT[0::2, :, 0], relT[1::2, :, 1] = a["L2_attn_rel_key"][256:512].T, a["L2_attn_rel_key"][256:512].T
    lay["a2_relT"] = relT.reshape(128, 2, 256)
    lay["moe_gateT"] = a["L2_ffn_gate_w"].T
    lay["moe_iota"] = np.arange(1, 33, dtype=np.float32)

    def chunks(w):
        return w.reshape(-1, 128, w.shape[1]).transpose(1, 0, 2).reshape(128, -1)

    def expert(wg, wu, wd):
        return np.concatenate([chunks(wg.T), chunks(wu.T), chunks(wd.T)], axis=1)

    shared = expert(a["L2_ffn_Ws_g"], a["L2_ffn_Ws_u"], a["L2_ffn_Ws_d"])
    lay["moe_experts"] = np.stack([expert(a["L2_ffn_Wg"][e], a["L2_ffn_Wu"][e], a["L2_ffn_Wd"][e]) for e in range(16)]
                                  + [shared, shared])

    z256 = np.zeros(256, np.float32)
    attn("a3", a["L3_attn_W_q"], a["L3_attn_W_k"], a["L3_attn_W_v"], a["L3_attn_W_o"], z256, z256, z256, z256)
    lay["a3_wdown"] = a["L3_attn_W_down_kv"]
    lay["a3_wupk"], lay["a3_wupv"] = a["L3_attn_W_up_k"], a["L3_attn_W_up_v"]
    lay["a3_matrix"] = tiles(np.exp(np.float32(-0.01) * np.abs(i - j).astype(np.float32)))
    lay["f3_sim"], lay["f3_gates"] = a["L3_ffn_sim_matrix"], a["L3_ffn_gates"]
    lay["f3_index"] = np.arange(16, dtype=np.float32)
    lay["f3_mask"] = lay["a2_matrix"]
    lay["f3_wqkv"] = np.concatenate([a[f"L3_ffn_{n}_proj"] for n in "qkv"], axis=2).reshape(16, 2, 128, 384).transpose(2, 0, 1, 3)
    lay["f3_wo"] = a["L3_ffn_o_proj"].transpose(1, 0, 2)

    nc = _bacc.Bacc("TRN2", target_bir_lowering=False, num_devices=1)
    arrays, dram = {}, {}
    for name, v in lay.items():
        v = c(v)
        arrays[f"in_{name}"] = v
        dram[name] = nc.dram_tensor(f"in_{name}", v.shape, _mybir.dt.from_np(v.dtype), kind="ExternalInput").ap()
    out = nc.dram_tensor("out_0_dram", (8, 256, 256), _mybir.dt.float32, kind="ExternalOutput").ap()
    build(nc, dram, out, STAGES)
    r = _run(nc, [arrays], core_ids=[0])
    return r.results[0]["out_0_dram"]
```
